# Optimizing a Trainium2 kernel written in Bass

```python
import numpy as np
import jax
import jax.numpy as jnp

def _softmax(x, axis=-1):
    return jax.nn.softmax(x, axis=axis)

def _gelu(x):
    return jax.nn.gelu(x, approximate=True)

def _silu(x):
    return jax.nn.silu(x)

def _sigmoid(x):
    return jax.nn.sigmoid(x)

def _layernorm(x, axis=-1, eps=1e-05):
    m = jnp.mean(x, axis=axis, keepdims=True)
    v = jnp.var(x, axis=axis, keepdims=True)
    return (x - m) / jnp.sqrt(v + eps)

def _scatter_add(tgt, idx, src, axis=0):
    return tgt.at[idx].add(src)

def _segment_sum(src, seg, n):
    return jax.ops.segment_sum(src, seg, n)
kernel_name = 'mk_xattn_ffn_d2_seqx_r4_c37fca'

def setup_inputs(seed: int=0):
    np.random.seed(seed)
    _w = jnp.asarray

    def _rec_inputs():
        import jax
        import jax.numpy as jnp
        _rk = jax.random.key(seed)
        x = -0.0005146 + 1 * jax.random.normal(jax.random.fold_in(_rk, 1), (32, 112, 256), jnp.float32)
        _lenS = 112 - jax.random.randint(jax.random.fold_in(_rk, 7), (32,), 0, max(1, 112 // 4) + 1, jnp.int32)
        _lenS2 = 375 - jax.random.randint(jax.random.fold_in(_rk, 8), (32,), 0, max(1, 375 // 4) + 1, jnp.int32)
        _ctx_1024P = jax.random.normal(jax.random.fold_in(_rk, 11), (32, 16, 256), jnp.float32)
        _ctx_1024c = jax.random.dirichlet(jax.random.fold_in(_rk, 511), 0.3 * jnp.ones((16,), jnp.float32), (32, 375))
        _ctx_1024t = jnp.einsum('bsk,bkd->bsd', _ctx_1024c, _ctx_1024P)
        _ctx_1024t = _ctx_1024t * jax.lax.rsqrt(jnp.mean(jnp.square(_ctx_1024t)) + 1e-12) * 0.953939
        ctx_1024 = -0.000125008 + 0.999885 * (_ctx_1024t + 0.3 * jax.random.normal(jax.random.fold_in(_rk, 611), (32, 375, 256), jnp.float32))
        _validS = jnp.arange(112)[None, :] < _lenS[:, None]
        _validS2 = jnp.arange(375)[None, :] < _lenS2[:, None]
        _causal = jnp.tril(jnp.ones((112, 112), dtype=bool))
        mask_Bx1xS2_fk0 = jnp.where(jnp.broadcast_to(_validS2[:, None, :], (32, 1, 375)), 0.0, 1.0).astype(jnp.float32)
        return (x, ctx_1024, mask_Bx1xS2_fk0)
    x, ctx_1024, mask_Bx1xS2_fk0 = _rec_inputs()

    def _L0_xattn_setup():
        import jax, jax.numpy as jnp
        import numpy as np
        DIM = 256
        NUM_HEADS = 16
        HEAD_DIM = DIM // NUM_HEADS
        SCALE = HEAD_DIM ** (-0.5)
        key = jax.random.key(seed)
        k1, k2, k3, k4, k5, k6 = jax.random.split(key, 6)
        B, S, L = (4, 2048, 128)
        x = jax.random.normal(k1, (B, S, DIM), dtype=jnp.float32)
        latents = jax.random.normal(k2, (B, L, DIM), dtype=jnp.float32)
        w_q = jax.random.normal(k3, (DIM, DIM), dtype=jnp.float32) * DIM ** (-0.5)
        w_kv = jax.random.normal(k4, (2 * DIM, DIM), dtype=jnp.float32) * DIM ** (-0.5)
        w_out = jax.random.normal(k5, (DIM, DIM), dtype=jnp.float32) * DIM ** (-0.5)
        b_out = jax.random.normal(k6, (DIM,), dtype=jnp.float32) * 0.01
        return {'x': x, 'latents': latents, 'w_q': w_q, 'w_kv': w_kv, 'w_out': w_out, 'b_out': b_out}
    _L0_xattn_all = _L0_xattn_setup()
    _L0_xattn_in = {k: v for k, v in _L0_xattn_all.items() if k in ('w_q', 'w_kv', 'w_out', 'b_out')}
    del _L0_xattn_all

    def _L0_ffn_setup():
        import jax, jax.numpy as jnp
        import numpy as np
        TOP_K = 2
        key = jax.random.key(seed)
        k1, k2, k3 = jax.random.split(key, 3)
        B, S, D, E = (8, 512, 256, 8)
        x = jax.random.normal(k1, (B, S, D), dtype=jnp.float32)
        gate_w = jax.random.normal(k2, (E, D), dtype=jnp.float32) * (1.0 / np.sqrt(D))
        gate_b = jnp.zeros((E,), dtype=jnp.float32)
        expert_w = jax.random.normal(k3, (E, D, D), dtype=jnp.float32) * (1.0 / np.sqrt(D))
        expert_b = jnp.zeros((E, D), dtype=jnp.float32)
        return {'x': x, 'gate_w': gate_w, 'gate_b': gate_b, 'expert_w': expert_w, 'expert_b': expert_b}
    _L0_ffn_all = _L0_ffn_setup()
    _L0_ffn_in = {k: v for k, v in _L0_ffn_all.items() if k in ('gate_w', 'gate_b', 'expert_w', 'expert_b')}
    del _L0_ffn_all

    def _L1_xattn_setup():
        import jax, jax.numpy as jnp
        import numpy as np
        B, S, D = (8, 512, 256)
        NEG = -1000000000.0
        key = jax.random.key(seed)
        kq, kk, kv, km = jax.random.split(key, 4)
        q = jax.random.normal(kq, (B, S, D), dtype=jnp.float32)
        k = jax.random.normal(kk, (B, S, D), dtype=jnp.float32)
        v = jax.random.normal(kv, (B, S, D), dtype=jnp.float32)
        mask = (jax.random.uniform(km, (B, 1, S)) < 0.1).astype(jnp.float32)
        return {'q': q, 'k': k, 'v': v, 'mask': mask}
    _L1_xattn_all = _L1_xattn_setup()
    _L1_xattn_in = {k: v for k, v in _L1_xattn_all.items() if k in ()}
    del _L1_xattn_all

    def _L1_ffn_setup():
        import jax, jax.numpy as jnp
        import numpy as np
        B, S, D, H, E, K = (4, 256, 256, 512, 8, 2)
        key = jax.random.key(seed)
        ks = jax.random.split(key, 5)
        s = 0.02
        return {'x': jax.random.normal(ks[0], (B, S, D), jnp.float32), 'W1': jax.random.normal(ks[1], (E, H, D), jnp.float32) * s, 'b1': jnp.zeros((E, H), jnp.float32), 'W2': jax.random.normal(ks[2], (E, D, H), jnp.float32) * s, 'b2': jnp.zeros((E, D), jnp.float32), 'Wg': jax.random.normal(ks[3], (E, D), jnp.float32) * s, 'bg': jnp.zeros((E,), jnp.float32)}
    _L1_ffn_all = _L1_ffn_setup()
    _L1_ffn_in = {k: v for k, v in _L1_ffn_all.items() if k in ('W1', 'b1', 'W2', 'b2', 'Wg', 'bg')}
    del _L1_ffn_all
    return {'x': x, 'ctx_1024': ctx_1024, 'mask_Bx1xS2_fk0': mask_Bx1xS2_fk0, 'L0_xattn_w_q': _L0_xattn_in['w_q'], 'L0_xattn_w_kv': _L0_xattn_in['w_kv'], 'L0_xattn_w_out': _L0_xattn_in['w_out'], 'L0_xattn_b_out': _L0_xattn_in['b_out'], 'L0_ffn_gate_w': _L0_ffn_in['gate_w'], 'L0_ffn_gate_b': _L0_ffn_in['gate_b'], 'L0_ffn_expert_w': _L0_ffn_in['expert_w'], 'L0_ffn_expert_b': _L0_ffn_in['expert_b'], 'L1_ffn_W1': _L1_ffn_in['W1'], 'L1_ffn_b1': _L1_ffn_in['b1'], 'L1_ffn_W2': _L1_ffn_in['W2'], 'L1_ffn_b2': _L1_ffn_in['b2'], 'L1_ffn_Wg': _L1_ffn_in['Wg'], 'L1_ffn_bg': _L1_ffn_in['bg']}

def reference(x, ctx_1024, mask_Bx1xS2_fk0, L0_xattn_w_q, L0_xattn_w_kv, L0_xattn_w_out, L0_xattn_b_out, L0_ffn_gate_w, L0_ffn_gate_b, L0_ffn_expert_w, L0_ffn_expert_b, L1_ffn_W1, L1_ffn_b1, L1_ffn_W2, L1_ffn_b2, L1_ffn_Wg, L1_ffn_bg):
    import jax
    import jax.numpy as jnp

    def _L0_xattn_ref(x, latents, w_q, w_kv, w_out, b_out):
        import jax, jax.numpy as jnp
        import numpy as np
        DIM = 256
        NUM_HEADS = 16
        HEAD_DIM = DIM // NUM_HEADS
        SCALE = HEAD_DIM ** (-0.5)
        B, L, _ = latents.shape
        S = x.shape[1]
        q = latents @ w_q.T
        kv = x @ w_kv.T
        k, v = jnp.split(kv, 2, axis=-1)
        q = q.reshape(B, L, NUM_HEADS, HEAD_DIM)
        k = k.reshape(B, S, NUM_HEADS, HEAD_DIM)
        v = v.reshape(B, S, NUM_HEADS, HEAD_DIM)
        attn = jnp.einsum('blhd,bshd->bhls', q, k) * SCALE
        attn = jax.nn.softmax(attn, axis=-1)
        out = jnp.einsum('bhls,bshd->blhd', attn, v)
        out = out.reshape(B, L, DIM)
        return out @ w_out.T + b_out

    def _L0_ffn_ref(x, gate_w, gate_b, expert_w, expert_b):
        import jax, jax.numpy as jnp
        import numpy as np
        TOP_K = 2
        gate = jnp.einsum('bsd,ed->bse', x, gate_w) + gate_b
        _, idx = jax.lax.top_k(gate, TOP_K)
        E = gate_w.shape[0]
        flat_idx = idx.reshape(-1)
        counts = jnp.zeros((E,), dtype=x.dtype).at[flat_idx].add(1.0)
        expert_out = jax.nn.relu(jnp.einsum('bsd,ehd->bseh', x, expert_w) + expert_b)
        total = flat_idx.size
        out = jnp.einsum('bseh,e->bsh', expert_out, counts) / total
        return out

    def _L1_xattn_ref(q, k, v, mask):
        import jax, jax.numpy as jnp
        import numpy as np
        B, S, D = (8, 512, 256)
        NEG = -1000000000.0
        scale = jnp.asarray(D ** (-0.5), dtype=q.dtype)
        logits = jnp.einsum('bqd,bkd->bqk', q, k) * scale
        logits = logits + mask * NEG
        attn = jax.nn.softmax(logits, axis=-1)
        return jnp.einsum('bqk,bkd->bqd', attn, v)

    def _L1_ffn_ref(x, W1, b1, W2, b2, Wg, bg):
        import jax, jax.numpy as jnp
        import numpy as np
        B, S, D, H, E, K = (4, 256, 256, 512, 8, 2)
        b, s, d = x.shape
        xt = x.reshape(-1, d)
        gate_logits = xt @ Wg.T + bg
        w, idx = jax.lax.top_k(gate_logits, K)
        w = jax.nn.softmax(w, axis=1)
        h = jax.nn.relu(jnp.einsum('td,ehd->eth', xt, W1) + b1[:, None, :])
        y = jnp.einsum('eth,eoh->eto', h, W2) + b2[:, None, :]
        comb = (jax.nn.one_hot(idx, E, dtype=xt.dtype) * w[..., None]).sum(axis=1)
        out = jnp.einsum('eto,te->to', y, comb)
        return out.reshape(b, s, d)
    x = x + _L0_xattn_ref(ctx_1024, _layernorm(x, axis=-1), L0_xattn_w_q, L0_xattn_w_kv, L0_xattn_w_out, L0_xattn_b_out)
    x = x + _L0_ffn_ref(_layernorm(x, axis=-1), L0_ffn_gate_w, L0_ffn_gate_b, L0_ffn_expert_w, L0_ffn_expert_b)
    x = x + _L1_xattn_ref(_layernorm(x, axis=-1), ctx_1024, ctx_1024, mask_Bx1xS2_fk0)
    x = x + _L1_ffn_ref(_layernorm(x, axis=-1), L1_ffn_W1, L1_ffn_b1, L1_ffn_W2, L1_ffn_b2, L1_ffn_Wg, L1_ffn_bg)
    return x

_drawn_inputs = setup_inputs


def setup_inputs(seed=0):
    import zlib

    import numpy as np

    out = dict(_drawn_inputs(seed))
    spreads = {'L0_ffn_gate_b': (0.0, 0.34),
     'L0_ffn_expert_b': (0.0, 0.357),
     'L1_ffn_b1': (0.0, 0.491),
     'L1_ffn_b2': (0.0, 0.1),
     'L1_ffn_bg': (0.0, 0.1)}
    factors = {'L0_xattn_b_out': 5.35, 'L0_ffn_gate_w': 6.676}
    for name, (base, spread) in spreads.items():
        noise = np.random.default_rng([zlib.crc32(name.encode()), seed]).standard_normal(out[name].shape)
        drawn = base * np.exp(spread * noise) if base else spread * noise
        out[name] = jnp.asarray(drawn.astype(out[name].dtype))
    for name, factor in factors.items():
        out[name] = (out[name] * factor).astype(out[name].dtype)
    return out
```

```python
import numpy as np
import concourse.bass as bass
from concourse import mybir
from contextlib import ExitStack

F32 = mybir.dt.float32
F16 = mybir.dt.float16
U32 = mybir.dt.uint32
ALU = mybir.AluOpType
ACT = mybir.ActivationFunctionType
AX = mybir.AxisListType

B, S, KV, D = 32, 112, 375, 256
H, HD = 16, 16
PAIRS = H // 2
KC = 125
NKC = KV // KC
DC = D // 128
E = 8
EPS = 1e-5
UNROLL = 4
STAGES = 4
ONES_ROW = 96
GB = 4
GT = GB * S
HID = 512
HC = HID // 128


def count(t, u, per, extra):
    return t * (UNROLL * per) + (u * per + extra)


def wait(engine, sem, value):
    if isinstance(value, int) and value <= 0:
        return
    engine.wait_ge(sem, value)


def at_most(value, total):
    return min(value, total) if isinstance(value, int) else value


def slot_loads(t, u, slots):
    return t * (16 * UNROLL // slots) + 16 * (u // slots + 1)


def run_steps(engine, step):
    turns = B // UNROLL
    for u in range(UNROLL):
        step(0, u, tuple(u >= s for s in range(STAGES)), True)
    with engine.Fori(1, turns - 1) as t:
        for u in range(UNROLL):
            step(t, u, (True,) * STAGES, True)
    for u in range(UNROLL):
        step(turns - 1, u, (True,) * STAGES, u < UNROLL - 1)
    for u in range(STAGES - 1):
        step(turns, u, tuple(u < s for s in range(STAGES)), False)


def attention_phase(nc, ctx, dram, keep):
    def sb(name, shape, dt):
        return ctx.enter_context(nc.sbuf_tensor(name, shape, dt))

    def sem(name):
        return ctx.enter_context(nc.semaphore(name))

    x_res, xT_hi, xT_lo, gate_counts = keep["x_res"], keep["xT_hi"], keep["xT_lo"], keep["gate_counts"]
    ident, iota = keep["ident"], keep["iota"]
    psum = keep["psum"]

    wq = sb("wq", [128, DC, D], F32)
    wk = sb("wk", [128, DC, D], F32)
    wv = sb("wv", [128, DC, D], F32)
    wo = sb("wo", [128, DC, D], F32)
    bo = sb("bo", [S, D], F32)
    gate_w = sb("gate_w", [128, DC, E], F32)
    gate_whi = sb("gate_whi", [128, DC, E], F16)
    gate_wlo = sb("gate_wlo", [128, DC, E], F16)
    gate_bias = sb("gate_bias", [S, E], F32)
    parity = sb("parity", [128, 2], F32)
    half = sb("half", [S, 1], F32)
    ctxT = sb("ctxT", [128, 2, DC, KV], F32)
    ln1_stats = sb("ln1_stats", [S, 6], F32)
    ln1_mv = sb("ln1_mv", [S, 2], F32)
    ln1_var = sb("ln1_var", [S, 1], F32)
    ln1_rstd = sb("ln1_rstd", [S, 1], F32)
    xn = sb("xn", [S, D], F32)
    xnT = sb("xnT", [128, DC, S], F32)
    q_hi = sb("q_hi", [128, 2, DC, 2, S], F16)
    q_lo = sb("q_lo", [128, 2, DC, 2, S], F16)
    k_hi = sb("k_hi", [128, 2, DC, KV + 1], F16)
    k_lo = sb("k_lo", [128, 2, DC, KV + 1], F16)
    q_stack = sb("q_stack", [128, UNROLL, PAIRS, 2 * S], F16)
    k_stack = sb("k_stack", [128, UNROLL, PAIRS, KV + 1], F16)
    v_aug = sb("v_aug", [KC, UNROLL, NKC, H, 32], F32)
    smax = sb("smax", [S, 2, H], F32)
    neg_max = sb("neg_max", [H, S], F16)
    probsT = sb("probsT", [KC, 2, NKC, H, S], F32)
    oT = sb("oT", [128, 4, S], F32)
    inv_sum = sb("inv_sum", [S, 4, 4, 1], F32)
    o_nat = sb("o_nat", [S, D], F32)
    onT = sb("onT", [128, DC, S], F32)
    ln2_stats = sb("ln2_stats", [S, 6], F32)
    ln2_mv = sb("ln2_mv", [S, 2], F32)
    ln2_var = sb("ln2_var", [S, 1], F32)
    ln2_rstd = sb("ln2_rstd", [S, 1], F32)
    x1n = sb("x1n", [S, D], F32)
    logits = sb("logits", [S, E], F32)
    top8 = sb("top8", [S, 8], F32)
    top8_at = sb("top8_at", [S, 8], U32)

    names = """const_in weights_in setup_done pool_setup gate_split
        ctx_in0 ctx_in1 x_in0 x_in1 q_in0 q_in1 q_in2 q_in3 k_in0 k_in1 k_in2 k_in3 k_pool0 k_pool1 k_pool2 k_pool3 m_in
        mT_done xnT_done q_done k_done v_done scores_done scoresT_done pv_done oT_back_done onT_done
        out_done x1nT_done gate_done
        negm_ready xnT_ready qhi_ready khi_ready exp_done oT_ready onT_ready x1hi_ready v_ready
        ln1_st ln1_agg xn_ready max_done qlo_ready klo_ready inv_ready o_ready x1_ready ln2_st ln2_agg
        x1n_ready x1lo_ready logits_ready top_ready at_ready count1 count2
        passed ln1_eps ln1_rs xb_ready ln2_eps ln2_rs""".split()
    m = {n: sem("a_" + n) for n in names}
    ctx_in = [m["ctx_in0"], m["ctx_in1"]]
    x_in = [m["x_in0"], m["x_in1"]]
    q_in = [m[f"q_in{i}"] for i in range(4)]
    k_in = [m[f"k_in{i}"] for i in range(4)]
    k_pool_in = [m[f"k_pool{i}"] for i in range(4)]

    bank_a = psum[:, 6, :]
    bank_d = psum[:, 7, :]
    N_CONST, N_W = 3, 7

    def apart(engine):
        engine.sem_inc(m["passed"], 1)

    KEY_ROWS = ((0, k_hi), (1, k_lo), (2, k_hi))
    QUERY_ROWS = ((0, q_hi), (1, q_hi), (2, q_lo))

    def key_rows(engine, u, part, src, j, arrived):
        engine.dma_start(k_stack[32 * part:32 * part + 32, u % 4, j::4, 0:KV],
                         src[32 * j:32 * j + 32, u % 2, :, 0:KV]).then_inc(arrived[u % 4], 16)

    with nc.Block() as block:

        @block.sync
        def _(sp):
            for dst, src in ((ident[:], dram["ident"]), (iota[:], dram["iota"]), (parity[:], dram["parity"])):
                sp.dma_start(dst, src).then_inc(m["const_in"], 16)

            def load(t, u):
                b = t * UNROLL + u
                wait(sp, m["v_done"], count(t, u - 2, 2, 2))
                apart(sp)
                sp.dma_start(x_res[:, bass.ds(b, 1), :].rearrange("p o d -> p (o d)"),
                             dram["x"][bass.ds(b, 1), :, :].rearrange("o s d -> (o s) d")).then_inc(x_in[u % 2], 16)
                sp.dma_start(ctxT[:, u % 2, :, :],
                             dram["ctxT"][bass.ds(b, 1), :, :].rearrange("o (c p) s -> p (o c) s", p=128)).then_inc(ctx_in[u % 2], 16)

            load(0, 0)
            for dst, src in ((wq, "wqT"), (wk, "wkT"), (wv, "wvT"), (wo, "woT"), (gate_w, "gate_wT")):
                sp.dma_start(dst[:], dram[src].rearrange("(c p) n -> p c n", p=128)).then_inc(m["weights_in"], 16)
            sp.dma_start(bo[:], dram["bo"].rearrange("(o n) -> o n", o=1).broadcast_to([S, D])).then_inc(m["weights_in"], 16)
            sp.dma_start(gate_bias[:], dram["gate_b"].rearrange("(o n) -> o n", o=1).broadcast_to([S, E])).then_inc(m["weights_in"], 16)
            sp.wait_ge(m["setup_done"], 4)

            def step(t, u, on, more):
                a, b_, c, d = on
                if more:
                    load(t, u + 1)
                if c:
                    wait(sp, m["negm_ready"], count(t, u - 2, 1, 1))
                    apart(sp)
                    row = q_stack[ONES_ROW:ONES_ROW + 1, (u - 2) % 4, :, :].rearrange("o r (s q) -> o (r s) q", s=2)
                    sp.dma_start(row, neg_max[:, :]).then_inc(m["m_in"], 16)
                if a:
                    wait(sp, m["scoresT_done"], count(t, u - 4, 6, 6))
                    apart(sp)
                    wait(sp, m["qlo_ready"], count(t, u, 2, 2))
                    apart(sp)
                    for part, src in QUERY_ROWS:
                        for j in range(4):
                            sp.dma_start(q_stack[32 * part:32 * part + 32, u % 4, j::4, :],
                                         src[32 * j:32 * j + 32, u % 2, :, :, :].rearrange("p c s q -> p c (s q)")).then_inc(q_in[u % 4], 16)
                    wait(sp, m["klo_ready"], count(t, u, 2, 2))
                    apart(sp)
                    for j in range(4):
                        for part, src in KEY_ROWS[:2]:
                            key_rows(sp, u, part, src, j, k_in)

            run_steps(sp, step)

        @block.gpsimd
        def _(pool):
            nc.gpsimd.memset(v_aug[:], 0.0).then_inc(m["pool_setup"], 1)
            nc.gpsimd.memset(half[:], -0.5).then_inc(m["pool_setup"], 1)
            pool.wait_ge(m["pool_setup"], 2)
            nc.gpsimd.memset(v_aug[:, :, :, :, HD:HD + 1], 1.0).then_inc(m["setup_done"], 1)
            pool.wait_ge(m["weights_in"], 16 * N_W)

            def ln1_rstd_of(t, u):
                wait(pool, m["ln1_agg"], count(t, u, 1, 1))
                apart(pool)
                nc.gpsimd.tensor_scalar(ln1_var[:], ln1_mv[:, 1:2], EPS, None, ALU.add).then_inc(m["ln1_eps"], 1)
                wait(pool, m["ln1_eps"], count(t, u, 1, 1))
                nc.gpsimd.tensor_tensor(ln1_rstd[:], ln1_var[:], half[:], ALU.pow).then_inc(m["ln1_rs"], 1)

            ln1_rstd_of(0, 0)

            def step(t, u, on, more):
                b = t * UNROLL + u
                if on[0]:
                    wait(pool, m["xn_ready"], count(t, u, 1, 1))
                    apart(pool)
                    xb = x_res[:, bass.ds(b, 1), :].rearrange("p o d -> p (o d)")
                    nc.gpsimd.tensor_tensor(xb, xb, bo[:], ALU.add).then_inc(m["xb_ready"], 1)
                    wait(pool, m["scoresT_done"], count(t, u - 4, 6, 6))
                    wait(pool, m["klo_ready"], count(t, u, 2, 2))
                    apart(pool)
                    for j in range(4):
                        key_rows(pool, u, *KEY_ROWS[2], j, k_pool_in)
                if on[3]:
                    wait(pool, m["ln2_agg"], count(t, u - 3, 1, 1))
                    apart(pool)
                    nc.gpsimd.tensor_scalar(ln2_var[:], ln2_mv[:, 1:2], EPS, None, ALU.add).then_inc(m["ln2_eps"], 1)
                    wait(pool, m["ln2_eps"], count(t, u - 3, 1, 1))
                    nc.gpsimd.tensor_tensor(ln2_rstd[:], ln2_var[:], half[:], ALU.pow).then_inc(m["ln2_rs"], 1)
                if more:
                    ln1_rstd_of(t, u + 1)

            run_steps(pool, step)

        @block.tensor
        def _(pe):
            pe.wait_ge(m["const_in"], 16 * N_CONST)
            pe.wait_ge(m["weights_in"], 16 * N_W)
            pe.wait_ge(m["setup_done"], 4)
            pe.wait_ge(m["gate_split"], 2)

            def scores(t, u, h):
                b4, s = (u - 1) % 4, h % 2
                n = h + 16 * (u - 1)
                if h == 0:
                    wait(pe, q_in[b4], slot_loads(t, u - 1, 4) * 12)
                    wait(pe, k_in[b4], slot_loads(t, u - 1, 4) * 8)
                    wait(pe, k_pool_in[b4], slot_loads(t, u - 1, 4) * 4)
                wait(pe, m["max_done"], count(t, u - 1, 16, h - 1))
                nc.tensor.matmul(psum[0:S, 4 + s, 0:KV], q_stack[0:96, b4, h // 2, s * S:(s + 1) * S],
                                 k_stack[0:96, b4, h // 2, 0:KV], start=True, stop=True).then_inc(m["scores_done"], 1)

            def scoresT(t, u, n):
                b4, hg, c = (u - 2) % 4, n // NKC, n % NKC
                if n == 0:
                    wait(pe, m["m_in"], count(t, u - 2, 16, 16))
                wait(pe, m["exp_done"], count(t, u - 2, 6, n - 1))
                for r in range(4):
                    pair = 4 * hg + r
                    last = nc.tensor.matmul(psum[0:KC, 2 * (n % 2) + r // 2, (r % 2) * 2 * S:(r % 2 + 1) * 2 * S],
                                            k_stack[0:ONES_ROW + 1, b4, pair, c * KC:(c + 1) * KC],
                                            q_stack[0:ONES_ROW + 1, b4, pair, :], start=True, stop=True)
                last.then_inc(m["scoresT_done"], 1)

            def step(t, u, on, more):
                a, b_, c, d = on
                b2a, b4d, b2d = u % 2, (u - 3) % 4, (u - 3) % 2
                bd = t * UNROLL + (u - 3)

                def values(g):
                    if g % 2 == 0:
                        wait(pe, m["exp_done"], count(t, u - 3, 6, 3 + 3 * (g // 2)))
                    for cc in range(NKC):
                        for j in range(4):
                            h = 4 * g + j
                            last = nc.tensor.matmul(bank_d[32 * j:32 * j + 32, g * S:(g + 1) * S], v_aug[:, b4d, cc, h, :],
                                                    probsT[:, b2d, cc, h, :], start=(cc == 0), stop=(cc == NKC - 1))
                    if g == 3:
                        last.then_inc(m["pv_done"], 1)

                def keys(mc):
                    if mc == 0:
                        wait(pe, ctx_in[b2a], slot_loads(t, u, 2))
                        wait(pe, m["qlo_ready"], count(t, u, 2, 2))
                    else:
                        wait(pe, m["klo_ready"], count(t, u, 2, 1))
                    for kc in range(DC):
                        last = nc.tensor.matmul(bank_a[:, 0:KV], wk[:, kc, mc * 128:(mc + 1) * 128], ctxT[:, b2a, kc, :],
                                                start=(kc == 0), stop=(kc == DC - 1))
                    last.then_inc(m["k_done"], 1)

                def vals(chunks):
                    if chunks[0] == 0:
                        wait(pe, m["klo_ready"], count(t, u, 2, 2))
                    else:
                        wait(pe, m["v_ready"], count(t, u, 3, 2))
                    for n, cc in enumerate(chunks):
                        for kc in range(DC):
                            last = nc.tensor.matmul(bank_a[0:KC, n * D:(n + 1) * D], ctxT[:, b2a, kc, cc * KC:(cc + 1) * KC], wv[:, kc, :],
                                                    start=(kc == 0), stop=(kc == DC - 1))
                    last.then_inc(m["v_done"], 1)

                def pair_scores(h):
                    if b_:
                        scores(t, u, h)
                        scores(t, u, h + 1)

                def unit_scoresT(n):
                    if c:
                        scoresT(t, u, n)

                if d:
                    wait(pe, m["logits_ready"], count(t, u - 4, 1, 1))
                    values(0)
                if a or c:
                    wait(pe, m["v_ready"], at_most(count(t, u - 1, 3, 3), 3 * B))
                if c:
                    wait(pe, m["max_done"], count(t, u - 2, 16, 16))
                    nc.tensor.transpose(bank_a[0:H, 2 * S:3 * S], smax[:, u % 2, :], ident[0:S, 0:S]).then_inc(m["mT_done"], 1)
                if a:
                    wait(pe, m["xn_ready"], count(t, u, 1, 1))
                    for kc in range(DC):
                        last = nc.tensor.transpose(bank_a[:, kc * S:(kc + 1) * S], xn[:, kc * 128:(kc + 1) * 128], ident[0:S, 0:S])
                    last.then_inc(m["xnT_done"], 1)
                if d:
                    values(1)
                pair_scores(0)
                if a:
                    wait(pe, m["xnT_ready"], count(t, u, 1, 1))
                    if c:
                        wait(pe, m["negm_ready"], count(t, u - 2, 1, 1))
                    for mc in range(DC):
                        for kc in range(DC):
                            last = nc.tensor.matmul(bank_a[:, mc * S:(mc + 1) * S], wq[:, kc, mc * 128:(mc + 1) * 128], xnT[:, kc, :],
                                                    start=(kc == 0), stop=(kc == DC - 1))
                    last.then_inc(m["q_done"], 1)
                if d:
                    values(2)
                    values(3)
                pair_scores(2)
                if a:
                    keys(0)
                if d:
                    wait(pe, m["oT_ready"], count(t, u - 3, 1, 1))
                    for g in range(4):
                        last = nc.tensor.transpose(bank_d[0:S, g * 128:(g + 1) * 128], oT[:, g, :], ident[:, :])
                    last.then_inc(m["oT_back_done"], 1)
                unit_scoresT(0)
                pair_scores(4)
                unit_scoresT(1)
                if a:
                    keys(1)
                if d:
                    wait(pe, m["o_ready"], count(t, u - 3, 1, 1))
                    for kc in range(DC):
                        last = nc.tensor.transpose(bank_d[:, kc * S:(kc + 1) * S], o_nat[:, kc * 128:(kc + 1) * 128], ident[0:S, 0:S])
                    last.then_inc(m["onT_done"], 1)
                pair_scores(6)
                unit_scoresT(2)
                if a:
                    vals((0, 1))
                if d:
                    wait(pe, m["onT_ready"], count(t, u - 3, 1, 1))
                    for kc in range(DC):
                        last = nc.tensor.matmul(bank_d[0:S, 0:D], onT[:, kc, :], wo[:, kc, :], start=(kc == 0), stop=(kc == DC - 1))
                    last.then_inc(m["out_done"], 1)
                pair_scores(8)
                unit_scoresT(3)
                if a:
                    vals((2,))
                pair_scores(10)
                unit_scoresT(4)
                if d:
                    wait(pe, m["x1n_ready"], count(t, u - 3, 1, 1))
                    for kc in range(DC):
                        last = nc.tensor.transpose(bank_d[:, kc * S:(kc + 1) * S], x1n[:, kc * 128:(kc + 1) * 128], ident[0:S, 0:S])
                    last.then_inc(m["x1nT_done"], 1)
                pair_scores(12)
                unit_scoresT(5)
                if d:
                    wait(pe, m["x1lo_ready"], count(t, u - 3, 1, 1))
                    n = 0
                    for left, right in ((xT_hi, gate_whi), (xT_hi, gate_wlo), (xT_lo, gate_whi)):
                        for kc in range(DC):
                            last = nc.tensor.matmul(bank_d[0:S, 0:E], left[:, kc, bass.ds(bd * S, S)], right[:, kc, :],
                                                    start=(n == 0), stop=(n == 3 * DC - 1))
                            n += 1
                    last.then_inc(m["gate_done"], 1)
                pair_scores(14)

            run_steps(pe, step)

        @block.scalar
        def _(act):
            act.wait_ge(m["setup_done"], 4)

            def exps(t, u, n):
                p, hg, c = (u - 2) % 2, n // NKC, n % NKC
                if n == 0:
                    wait(act, m["pv_done"], count(t, u - 4, 1, 1))
                wait(act, m["scoresT_done"], count(t, u - 2, 6, n + 1))
                nc.scalar.activation(probsT[:, p, c, 8 * hg:8 * hg + 8, :].rearrange("p (k h) q -> p k (h q)", k=2),
                                     psum[0:KC, 2 * (n % 2):2 * (n % 2) + 2, 0:4 * S], ACT.Exp,
                                     scale=float(HD) ** -0.5).then_inc(m["exp_done"], 1)

            def step(t, u, on, more):
                a, b_, c, d = on
                bd = t * UNROLL + (u - 3)

                def khi(mc):
                    wait(act, m["k_done"], count(t, u, 2, mc + 1))
                    if mc == 0:
                        wait(act, k_in[(u - 2) % 4], slot_loads(t, u - 2, 4) * 8)
                        wait(act, k_pool_in[(u - 2) % 4], slot_loads(t, u - 2, 4) * 4)
                    nc.scalar.activation(k_hi[:, u % 2, mc, 0:KV], bank_a[:, 0:KV], ACT.Copy).then_inc(m["khi_ready"], 1)

                def vout(chunks):
                    if chunks[0] == 0:
                        wait(act, m["pv_done"], count(t, u - 4, 1, 1))
                    wait(act, m["v_done"], count(t, u, 2, 1 if chunks[0] == 0 else 2))
                    for n, cc in enumerate(chunks):
                        nc.scalar.activation(v_aug[:, u % 4, cc, :, 0:HD], bank_a[0:KC, n * D:(n + 1) * D].rearrange("p (h w) -> p h w", w=HD),
                                             ACT.Copy).then_inc(m["v_ready"], 1)

                if a:
                    wait(act, m["xnT_done"], count(t, u, 1, 1))
                    wait(act, m["q_done"], count(t, u - 1, 1, 1))
                    nc.scalar.activation(xnT[:, :, :].rearrange("p c s -> p (c s)"), bank_a[:, 0:DC * S], ACT.Copy).then_inc(m["xnT_ready"], 1)
                if c:
                    wait(act, m["mT_done"], count(t, u - 2, 1, 1))
                    wait(act, m["m_in"], count(t, u - 3, 16, 16))
                    nc.scalar.activation(neg_max[:, :], bank_a[0:H, 2 * S:3 * S], ACT.Copy, scale=-1.0).then_inc(m["negm_ready"], 1)
                if a:
                    wait(act, m["q_done"], count(t, u, 1, 1))
                    wait(act, q_in[(u - 2) % 4], slot_loads(t, u - 2, 4) * 12)
                    for s in range(2):
                        nc.scalar.activation(q_hi[:, u % 2, :, s, :], bank_a[:, 0:DC * S].rearrange("p (c s) -> p c s", c=DC),
                                             ACT.Copy, scale=parity[:, s:s + 1]).then_inc(m["qhi_ready"], 1)
                if d:
                    wait(act, m["pv_done"], count(t, u - 3, 1, 1))
                    wait(act, m["oT_back_done"], count(t, u - 4, 1, 1))
                    nc.scalar.activation(oT[:, :, :].rearrange("p g s -> p (g s)"), bank_d[:, 0:4 * S], ACT.Copy).then_inc(m["oT_ready"], 1)
                if a:
                    khi(0)
                if c:
                    exps(t, u, 0)
                    exps(t, u, 1)
                if a:
                    khi(1)
                if d:
                    wait(act, m["onT_done"], count(t, u - 3, 1, 1))
                    wait(act, m["out_done"], count(t, u - 4, 1, 1))
                    nc.scalar.activation(onT[:, :, :].rearrange("p c s -> p (c s)"), bank_d[:, 0:DC * S], ACT.Copy).then_inc(m["onT_ready"], 1)
                if c:
                    exps(t, u, 2)
                if a:
                    vout((0, 1))
                if c:
                    exps(t, u, 3)
                if a:
                    vout((2,))
                if c:
                    exps(t, u, 4)
                if d:
                    wait(act, m["x1nT_done"], count(t, u - 3, 1, 1))
                    nc.scalar.activation(xT_hi[:, :, bass.ds(bd * S, S)], bank_d[:, 0:DC * S].rearrange("p (c s) -> p c s", c=DC),
                                         ACT.Copy).then_inc(m["x1hi_ready"], 1)
                if c:
                    exps(t, u, 5)

            run_steps(act, step)

        @block.vector
        def _(dve):
            nc.vector.memset(q_stack[96:128, :, :, :], 0.0).then_inc(m["setup_done"], 1)
            nc.vector.memset(k_stack[96:128, :, :, :], 1.0).then_inc(m["setup_done"], 1)
            nc.vector.memset(gate_counts[:], 0.0).then_inc(m["setup_done"], 1)
            dve.wait_ge(m["weights_in"], 16 * N_W)
            nc.vector.tensor_copy(gate_whi[:], gate_w[:]).then_inc(m["gate_split"], 1)
            dve.wait_ge(m["gate_split"], 1)
            nc.vector.tensor_tensor(gate_wlo[:], gate_w[:], gate_whi[:], ALU.subtract).then_inc(m["gate_split"], 1)
            dve.wait_ge(m["const_in"], 16 * N_CONST)
            dve.wait_ge(m["setup_done"], 4)

            def maxima(t, u, heads):
                for h in heads:
                    if h == 0:
                        wait(dve, m["mT_done"], count(t, u - 3, 1, 1))
                    wait(dve, m["scores_done"], count(t, u - 1, 16, h + 1))
                    nc.vector.reduce_max(smax[:, (u - 1) % 2, h:h + 1], psum[0:S, 4 + h % 2, 0:KV], AX.X).then_inc(m["max_done"], 1)

            def ln1_stats_of(t, u):
                xb = x_res[:, bass.ds(t * UNROLL + u, 1), :].rearrange("p o d -> p (o d)")
                wait(dve, x_in[u % 2], slot_loads(t, u, 2))
                apart(dve)
                nc.vector.bn_stats(ln1_stats[:], xb).then_inc(m["ln1_st"], 1)
                wait(dve, m["ln1_st"], count(t, u, 1, 1))
                apart(dve)
                nc.vector.bn_aggr(ln1_mv[:], ln1_stats[:]).then_inc(m["ln1_agg"], 1)

            def ln1_out(t, u):
                xb = x_res[:, bass.ds(t * UNROLL + u, 1), :].rearrange("p o d -> p (o d)")
                wait(dve, m["ln1_rs"], count(t, u, 1, 1))
                wait(dve, m["xnT_done"], count(t, u - 1, 1, 1))
                nc.vector.tensor_scalar(xn[:], xb, ln1_mv[:, 0:1], ln1_rstd[:], ALU.subtract, ALU.mult).then_inc(m["xn_ready"], 1)

            ln1_stats_of(0, 0)
            ln1_out(0, 0)

            def step(t, u, on, more):
                a, b_, c, d = on
                bd = t * UNROLL + (u - 3)

                def klo(mc):
                    if a:
                        wait(dve, m["khi_ready"], count(t, u, 2, mc + 1))
                        nc.vector.tensor_tensor(k_lo[:, u % 2, mc, 0:KV], bank_a[:, 0:KV], k_hi[:, u % 2, mc, 0:KV],
                                                ALU.subtract).then_inc(m["klo_ready"], 1)

                def pair_max(h):
                    if b_:
                        maxima(t, u, (h, h + 1))

                pair_max(0)
                if a:
                    for s in range(2):
                        wait(dve, m["qhi_ready"], count(t, u, 2, 2))
                        nc.vector.scalar_tensor_tensor(q_lo[:, u % 2, :, s, :], bank_a[:, 0:DC * S].rearrange("p (c s) -> p c s", c=DC),
                                                       parity[:, s:s + 1], q_hi[:, u % 2, :, s, :],
                                                       ALU.mult, ALU.subtract).then_inc(m["qlo_ready"], 1)
                pair_max(2)
                klo(0)
                if d:
                    o4 = bank_d[0:S, :].rearrange("p (g j w) -> p g j w", g=4, j=4)
                    wait(dve, m["oT_back_done"], count(t, u - 3, 1, 1))
                    nc.vector.reciprocal(inv_sum[:], o4[:, :, :, HD:HD + 1]).then_inc(m["inv_ready"], 1)
                    wait(dve, m["inv_ready"], count(t, u - 3, 1, 1))
                    wait(dve, m["onT_done"], count(t, u - 4, 1, 1))
                    nc.vector.tensor_tensor(o_nat[:].rearrange("p (h w) -> p h w", w=HD),
                                            bank_d[0:S, :].rearrange("p (h w) -> p h w", w=32)[:, :, 0:HD],
                                            inv_sum[:].rearrange("p g j o -> p (g j) o").broadcast_to([S, H, HD]),
                                            ALU.mult).then_inc(m["o_ready"], 1)
                pair_max(4)
                klo(1)
                pair_max(6)
                if d:
                    x1 = x_res[:, bass.ds(bd, 1), :].rearrange("p o d -> p (o d)")
                    wait(dve, m["out_done"], count(t, u - 3, 1, 1))
                    wait(dve, m["xb_ready"], count(t, u - 3, 1, 1))
                    nc.vector.tensor_tensor(x1, bank_d[0:S, 0:D], x1, ALU.add).then_inc(m["x1_ready"], 1)
                    wait(dve, m["x1_ready"], count(t, u - 3, 1, 1))
                    apart(dve)
                    nc.vector.bn_stats(ln2_stats[:], x1).then_inc(m["ln2_st"], 1)
                    wait(dve, m["ln2_st"], count(t, u - 3, 1, 1))
                    apart(dve)
                    nc.vector.bn_aggr(ln2_mv[:], ln2_stats[:]).then_inc(m["ln2_agg"], 1)
                pair_max(8)
                pair_max(10)
                if d:
                    wait(dve, m["ln2_rs"], count(t, u - 3, 1, 1))
                    wait(dve, m["x1nT_done"], count(t, u - 4, 1, 1))
                    nc.vector.tensor_scalar(x1n[:], x1, ln2_mv[:, 0:1], ln2_rstd[:], ALU.subtract, ALU.mult).then_inc(m["x1n_ready"], 1)
                if more:
                    ln1_stats_of(t, u + 1)
                if d:
                    wait(dve, m["x1hi_ready"], count(t, u - 3, 1, 1))
                    nc.vector.tensor_tensor(xT_lo[:, :, bass.ds(bd * S, S)], bank_d[:, 0:DC * S].rearrange("p (c s) -> p c s", c=DC),
                                            xT_hi[:, :, bass.ds(bd * S, S)], ALU.subtract).then_inc(m["x1lo_ready"], 1)
                pair_max(12)
                if more:
                    ln1_out(t, u + 1)
                if d:
                    wait(dve, m["gate_done"], count(t, u - 3, 1, 1))
                    wait(dve, m["count2"], count(t, u - 4, 1, 1))
                    nc.vector.tensor_tensor(logits[:], bank_d[0:S, 0:E], gate_bias[:], ALU.add).then_inc(m["logits_ready"], 1)
                    wait(dve, m["logits_ready"], count(t, u - 3, 1, 1))
                    apart(dve)
                    nc.vector.max(top8[:], logits[:]).then_inc(m["top_ready"], 1)
                    wait(dve, m["top_ready"], count(t, u - 3, 1, 1))
                    apart(dve)
                    nc.vector.max_index(top8_at[:], top8[:], logits[:]).then_inc(m["at_ready"], 1)
                    wait(dve, m["at_ready"], count(t, u - 3, 1, 1))
                    nc.vector.scalar_tensor_tensor(gate_counts[:], iota[:], top8_at[:, 0:1], gate_counts[:],
                                                   ALU.is_equal, ALU.add).then_inc(m["count1"], 1)
                    wait(dve, m["count1"], count(t, u - 3, 1, 1))
                    nc.vector.scalar_tensor_tensor(gate_counts[:], iota[:], top8_at[:, 1:2], gate_counts[:],
                                                   ALU.is_equal, ALU.add).then_inc(m["count2"], 1)
                pair_max(14)

            run_steps(dve, step)


def middle_phase(nc, ctx, dram, keep):
    def sb(name, shape, dt):
        return ctx.enter_context(nc.sbuf_tensor(name, shape, dt))

    def sem(name):
        return ctx.enter_context(nc.semaphore(name))

    x_res, xT_hi, xT_lo, gate_counts = keep["x_res"], keep["xT_hi"], keep["xT_lo"], keep["gate_counts"]
    ident, iota, psum, comb = keep["ident"], keep["iota"], keep["psum"], keep["comb"]

    we = sb("we", [128, DC, E, D], F32)
    we_hi = sb("we_hi", [128, DC, E, D], F16)
    we_lo = sb("we_lo", [128, DC, E, D], F16)
    expert_b = sb("expert_b", [128, DC, E], F32)
    share = sb("share", [128, E], F32)
    neg_bias = sb("neg_bias", [128, DC, E], F32)
    bias_sum = sb("bias_sum", [128, DC], F32)
    ones = sb("ones", [S, 128], F32)
    half = sb("half2", [S, 1], F32)
    acc = sb("acc", [128, 2, DC, GT], F32)
    ctxT = sb("ctxT2", [128, 2, DC, KV], F32)
    ctx_rows = sb("ctx_rows", [KC, 2, NKC, D], F32)
    mask = sb("mask", [S, 2, KV], F32)
    mask_add = sb("mask_add", [S, 2, KV], F32)
    ln_stats = sb("ln_stats", [S, 2, 6], F32)
    ln_mv = sb("ln_mv", [S, 2, 2], F32)
    ln_var = sb("ln_var", [S, 2, 1], F32)
    ln_rstd = sb("ln_rstd", [S, 2, 1], F32)
    x2n = sb("x2n", [S, D], F32)
    x2nT = sb("x2nT", [128, DC, S], F32)
    masked = sb("masked", [S, KV], F32)
    row_max = sb("row_max", [S, 1], F32)
    exp_bias = sb("exp_bias", [S, 1], F32)
    probs = sb("probs", [S, KV], F32)
    prob_sum = sb("prob_sum", [S, 2, 1], F32)
    inv_sum = sb("inv_sum2", [S, 1], F32)
    probsT = sb("probsT2", [KC, NKC, S], F32)
    x3n = sb("x3n", [S, D], F32)
    route_w = sb("route_w", [128, DC, E], F32)
    route_whi = sb("route_whi", [128, DC, E], F16)
    route_wlo = sb("route_wlo", [128, DC, E], F16)
    route_bias = sb("route_bias", [S, E], F32)
    logits = sb("logits2", [S, E], F32)
    top8 = sb("top82", [S, 8], F32)
    top8_at = sb("top8_at2", [S, 8], U32)
    gap = sb("gap", [S, 1], F32)
    gap_exp = sb("gap_exp", [S, 1], F32)
    gap_sum = sb("gap_sum", [S, 1], F32)
    first_w = sb("first_w", [S, 1], F32)
    second_w = sb("second_w", [S, 1], F32)
    second = sb("second", [S, E], F32)

    names = """weights_in we_in ready0 share_ps share_rdy nb_rdy bs_rdy we_hi_rdy we_lo_rdy route_split consts
        ctxT_in0 ctxT_in1 rows_in0 rows_in1 mask_in0 mask_in1 passed
        ffn_done accT_done x2nT_done s1_done pT_done o_done x3nT_done route_done
        x2nT_rdy exp_rdy pT_rdy x3hi_rdy gexp_rdy
        acc_rdy x2_rdy st2 ag2 x2n_rdy masked_rdy eb_rdy inv_rdy x3_rdy st3 ag3 x3n_rdy x3lo_rdy
        lg_rdy top_rdy at_rdy gap_rdy gs_rdy fw_rdy sw_rdy c1_rdy c2_rdy c2w_rdy comb_rdy
        eps2 rs2 eps3 rs3 mask_rdy""".split()
    m = {n: sem("m_" + n) for n in names}
    ctxT_in, rows_in, mask_in = ([m[f"{k}{i}"] for i in range(2)] for k in ("ctxT_in", "rows_in", "mask_in"))
    LAG_ATT, LAG_OUT, LAG_ROUTE = 4, 5, 6
    TURN = 2 * GB
    N_W = 5
    NEG = -1e9 * 16.0

    def cnt(t, u, per, extra):
        return t * (TURN * per) + (u * per + extra)

    def loads(t, u):
        return t * (16 * TURN // 2) + 16 * (u // 2 + 1)

    def apart(engine):
        engine.sem_inc(m["passed"], 1)

    def steps(engine, step):
        turns = B // TURN
        for u in range(TURN):
            step(0, u, (True, u >= LAG_ATT, u >= LAG_OUT, u >= LAG_ROUTE))
        with engine.Fori(1, turns) as t:
            for u in range(TURN):
                step(t, u, (True,) * 4)
        for u in range(LAG_ROUTE):
            step(turns, u, (False, u < LAG_ATT, u < LAG_OUT, True))

    with nc.Block() as block:

        @block.sync
        def _(sp):
            for e in range(E):
                sp.dma_start(we[:, :, e, :], dram["weT"].rearrange("(c p) e h -> p c e h", p=128)[:, :, e, :]).then_inc(m["we_in"], 16)
            sp.dma_start(expert_b[:], dram["expert_bT"].rearrange("(c p) e -> p c e", p=128)).then_inc(m["weights_in"], 16)
            sp.dma_start(route_w[:], dram["route_wT"].rearrange("(c p) e -> p c e", p=128)).then_inc(m["weights_in"], 16)
            sp.dma_start(route_bias[:], dram["route_b"].rearrange("(o n) -> o n", o=1).broadcast_to([S, E])).then_inc(m["weights_in"], 16)

            def load(t, u):
                b, p = t * TURN + u, u % 2
                wait(sp, m["s1_done"], cnt(t, u - 2, 1, 1))
                apart(sp)
                sp.dma_start(ctxT[:, p, :, :], dram["ctxT"][bass.ds(b, 1), :, :].rearrange("o (c p) s -> p (o c) s", p=128)).then_inc(ctxT_in[p], 16)
                wait(sp, m["mask_rdy"], cnt(t, u - 2, 1, 1))
                apart(sp)
                sp.dma_start(mask[:, p, :], dram["mask"][bass.ds(b, 1), 0, :].broadcast_to([S, KV])).then_inc(mask_in[p], 16)
                wait(sp, m["o_done"], cnt(t, u - 2, 1, 1))
                apart(sp)
                sp.dma_start(ctx_rows[:, p, :, :], dram["ctx"][bass.ds(b, 1), :, :].rearrange("o (c p) d -> p (o c) d", p=KC)).then_inc(rows_in[p], 16)

            turns = B // TURN
            for u in range(TURN):
                load(0, u)
            with sp.Fori(1, turns) as t:
                for u in range(TURN):
                    load(t, u)

        @block.gpsimd
        def _(pool):
            nc.gpsimd.memset(ones[:], 1.0).then_inc(m["consts"], 1)
            nc.gpsimd.memset(half[:], -0.5).then_inc(m["consts"], 1)
            pool.wait_ge(m["consts"], 2)

            def rstd(agg, eps, rs, n, value):
                wait(pool, m[agg], value)
                apart(pool)
                nc.gpsimd.tensor_scalar(ln_var[:, n, :], ln_mv[:, n, 1:2], EPS, None, ALU.add).then_inc(m[eps], 1)
                wait(pool, m[eps], value)
                nc.gpsimd.tensor_tensor(ln_rstd[:, n, :], ln_var[:, n, :], half[:], ALU.pow).then_inc(m[rs], 1)

            def step(t, u, on):
                f, a, o, r = on
                if a:
                    p = (u - LAG_ATT) % 2
                    wait(pool, mask_in[p], loads(t, u - LAG_ATT))
                    wait(pool, m["masked_rdy"], cnt(t, u - LAG_ATT - 2, 1, 1))
                    apart(pool)
                    nc.gpsimd.tensor_scalar(mask_add[:, p, :], mask[:, p, :], NEG, 0.0, ALU.mult, ALU.add).then_inc(m["mask_rdy"], 1)
                if r:
                    rstd("ag3", "eps3", "rs3", 1, cnt(t, u - LAG_ROUTE, 1, 1))
                if a:
                    rstd("ag2", "eps2", "rs2", 0, cnt(t, u - LAG_ATT, 1, 1))

            steps(pool, step)

        @block.tensor
        def _(pe):
            pe.wait_ge(m["consts"], 2)
            nc.tensor.matmul(psum[:, 0, 0:E], ones[:], gate_counts[:], start=True, stop=True).then_inc(m["share_ps"], 1)
            pe.wait_ge(m["route_split"], 2)
            pe.wait_ge(m["share_rdy"], 1)

            def mixture(t, u, k):
                e, hc = 2 * (u % GB) + k // 2, k % 2
                g0 = t * (2 * GT) + (u // GB) * GT
                if isinstance(t, int) and t == 0 and u < GB:
                    pe.wait_ge(m["we_lo_rdy"], e + 1)
                wait(pe, m["acc_rdy"], cnt(t, u, 4, k - 1))
                n = 0
                for w, x in ((we_hi, xT_hi), (we_hi, xT_lo), (we_lo, xT_hi)):
                    for kc in range(DC):
                        last = nc.tensor.matmul(psum[:, k % 2, 0:GT], w[:, kc, e, hc * 128:(hc + 1) * 128], x[:, kc, bass.ds(g0, GT)],
                                                start=(n == 0), stop=(n == 5))
                        n += 1
                last.then_inc(m["ffn_done"], 1)

            def step(t, u, on):
                f, a, o, r = on
                ua, uo, ur = u - LAG_ATT, u - LAG_OUT, u - LAG_ROUTE

                def mix(k):
                    if f:
                        mixture(t, u, k)

                if a:
                    wait(pe, m["acc_rdy"], cnt(t, (ua // GB) * GB, 4, 4 * GB))
                    wait(pe, m["x2_rdy"], cnt(t, ua - 1, 1, 1))
                    for hc in range(DC):
                        last = nc.tensor.transpose(psum[0:S, 2, hc * 128:(hc + 1) * 128],
                                                   acc[:, (ua // GB) % 2, hc, (ua % GB) * S:(ua % GB + 1) * S], ident[:, :])
                    last.then_inc(m["accT_done"], 1)
                if o:
                    wait(pe, m["exp_rdy"], cnt(t, uo, 1, 1))
                    wait(pe, m["pT_rdy"], cnt(t, uo - 1, 1, 1))
                    for c in range(NKC):
                        last = nc.tensor.transpose(psum[0:KC, 5, c * S:(c + 1) * S], probs[:, c * KC:(c + 1) * KC], ident[0:S, 0:S])
                    last.then_inc(m["pT_done"], 1)
                mix(0)
                if r:
                    wait(pe, m["x3n_rdy"], cnt(t, ur, 1, 1))
                    wait(pe, m["lg_rdy"], cnt(t, ur - 1, 1, 1))
                    for kc in range(DC):
                        last = nc.tensor.transpose(psum[:, 7, kc * S:(kc + 1) * S], x3n[:, kc * 128:(kc + 1) * 128], ident[0:S, 0:S])
                    last.then_inc(m["x3nT_done"], 1)
                if o:
                    wait(pe, rows_in[uo % 2], loads(t, uo))
                    wait(pe, m["pT_rdy"], cnt(t, uo, 1, 1))
                    wait(pe, m["x3_rdy"], cnt(t, uo - 1, 1, 1))
                    for c in range(NKC):
                        last = nc.tensor.matmul(psum[0:S, 6, 0:D], probsT[:, c, :], ctx_rows[:, uo % 2, c, :], start=(c == 0), stop=(c == NKC - 1))
                    last.then_inc(m["o_done"], 1)
                mix(1)
                if a:
                    wait(pe, m["x2n_rdy"], cnt(t, ua, 1, 1))
                    wait(pe, m["x2nT_rdy"], cnt(t, ua - 1, 1, 1))
                    for kc in range(DC):
                        last = nc.tensor.transpose(psum[:, 3, kc * S:(kc + 1) * S], x2n[:, kc * 128:(kc + 1) * 128], ident[0:S, 0:S])
                    last.then_inc(m["x2nT_done"], 1)
                mix(2)
                if r:
                    wait(pe, m["x3lo_rdy"], cnt(t, ur, 1, 1))
                    b0 = (t * TURN + ur) * S
                    n = 0
                    for left, right in ((xT_hi, route_whi), (xT_hi, route_wlo), (xT_lo, route_whi)):
                        for kc in range(DC):
                            last = nc.tensor.matmul(psum[0:S, 7, 0:E], left[:, kc, bass.ds(b0, S)], right[:, kc, :], start=(n == 0), stop=(n == 5))
                            n += 1
                    last.then_inc(m["route_done"], 1)
                if a:
                    wait(pe, ctxT_in[ua % 2], loads(t, ua))
                    wait(pe, m["x2nT_rdy"], cnt(t, ua, 1, 1))
                    wait(pe, m["masked_rdy"], cnt(t, ua - 1, 1, 1))
                    for kc in range(DC):
                        last = nc.tensor.matmul(psum[0:S, 4, 0:KV], x2nT[:, kc, :], ctxT[:, ua % 2, kc, :], start=(kc == 0), stop=(kc == DC - 1))
                    last.then_inc(m["s1_done"], 1)
                mix(3)

            steps(pe, step)

        @block.scalar
        def _(act):
            act.wait_ge(m["share_ps"], 1)
            nc.scalar.activation(share[:], psum[:, 0, 0:E], ACT.Copy, scale=1.0 / (2 * B * S)).then_inc(m["share_rdy"], 1)
            act.wait_ge(m["share_rdy"], 1)
            act.wait_ge(m["we_in"], 16 * E)
            for e in range(E):
                nc.scalar.activation(we_hi[:, :, e, :], we[:, :, e, :], ACT.Copy, scale=share[:, e:e + 1]).then_inc(m["we_hi_rdy"], 1)

            def step(t, u, on):
                f, a, o, r = on
                ua, uo, ur = u - LAG_ATT, u - LAG_OUT, u - LAG_ROUTE
                if o:
                    wait(act, m["eb_rdy"], cnt(t, uo, 1, 1))
                    wait(act, m["pT_done"], cnt(t, uo - 1, 1, 1))
                    nc.scalar.activation(probs[:], masked[:], ACT.Exp, bias=exp_bias[:], scale=float(D) ** -0.5,
                                         accum_out=prob_sum[:, uo % 2, :]).then_inc(m["exp_rdy"], 1)
                    wait(act, m["pT_done"], cnt(t, uo, 1, 1))
                    wait(act, m["o_done"], cnt(t, uo - 1, 1, 1))
                    nc.scalar.activation(probsT[:].rearrange("p c s -> p (c s)"), psum[0:KC, 5, 0:NKC * S], ACT.Copy).then_inc(m["pT_rdy"], 1)
                if r:
                    b0 = (t * TURN + ur) * S
                    wait(act, m["x3nT_done"], cnt(t, ur, 1, 1))
                    nc.scalar.activation(xT_hi[:, :, bass.ds(b0, S)], psum[:, 7, 0:DC * S].rearrange("p (c s) -> p c s", c=DC), ACT.Copy).then_inc(m["x3hi_rdy"], 1)
                if a:
                    wait(act, m["x2nT_done"], cnt(t, ua, 1, 1))
                    wait(act, m["s1_done"], cnt(t, ua - 1, 1, 1))
                    nc.scalar.activation(x2nT[:].rearrange("p c s -> p (c s)"), psum[:, 3, 0:DC * S], ACT.Copy).then_inc(m["x2nT_rdy"], 1)
                if r:
                    wait(act, m["gap_rdy"], cnt(t, ur, 1, 1))
                    nc.scalar.activation(gap_exp[:], gap[:], ACT.Exp).then_inc(m["gexp_rdy"], 1)

            steps(act, step)

        @block.vector
        def _(dve):
            dve.wait_ge(m["weights_in"], 48)
            nc.vector.tensor_copy(route_whi[:], route_w[:]).then_inc(m["route_split"], 1)
            dve.wait_ge(m["route_split"], 1)
            nc.vector.tensor_tensor(route_wlo[:], route_w[:], route_whi[:], ALU.subtract).then_inc(m["route_split"], 1)
            dve.wait_ge(m["share_rdy"], 1)
            nc.vector.scalar_tensor_tensor(neg_bias[:], expert_b[:], -1.0, share[:].rearrange("p (o e) -> p o e", o=1).broadcast_to([128, DC, E]),
                                           ALU.mult, ALU.mult).then_inc(m["nb_rdy"], 1)
            dve.wait_ge(m["nb_rdy"], 1)
            nc.vector.tensor_reduce(bias_sum[:], neg_bias[:], AX.X, ALU.add, negate=True).then_inc(m["bs_rdy"], 1)
            for e in range(E):
                dve.wait_ge(m["we_hi_rdy"], e + 1)
                nc.vector.scalar_tensor_tensor(we_lo[:, :, e, :], we[:, :, e, :], share[:, e:e + 1], we_hi[:, :, e, :],
                                               ALU.mult, ALU.subtract).then_inc(m["we_lo_rdy"], 1)
            dve.wait_ge(m["bs_rdy"], 1)

            def mix(t, u, k):
                e, hc = 2 * (u % GB) + k // 2, k % 2
                out = acc[:, u // GB, hc, :]
                wait(dve, m["ffn_done"], cnt(t, u, 4, k + 1))
                if e == 0:
                    wait(dve, m["accT_done"], cnt(t, u - GB - 1, 1, 1))
                    nc.vector.tensor_scalar(out, psum[:, k % 2, 0:GT], neg_bias[:, hc, 0:1], bias_sum[:, hc:hc + 1],
                                            ALU.max, ALU.add).then_inc(m["acc_rdy"], 1)
                else:
                    wait(dve, m["acc_rdy"], cnt(t, u, 4, k - 1))
                    nc.vector.scalar_tensor_tensor(out, psum[:, k % 2, 0:GT], neg_bias[:, hc, e:e + 1], out,
                                                   ALU.max, ALU.add).then_inc(m["acc_rdy"], 1)

            def step(t, u, on):
                f, a, o, r = on
                ua, uo, ur = u - LAG_ATT, u - LAG_OUT, u - LAG_ROUTE
                xrow = lambda uu: x_res[:, bass.ds(t * TURN + uu, 1), :].rearrange("p o d -> p (o d)")

                def norm_stats(x, n, st, ag, value):
                    apart(dve)
                    nc.vector.bn_stats(ln_stats[:, n, :], x).then_inc(m[st], 1)
                    wait(dve, m[st], value)
                    apart(dve)
                    nc.vector.bn_aggr(ln_mv[:, n, :], ln_stats[:, n, :]).then_inc(m[ag], 1)

                if o:
                    v = cnt(t, uo, 1, 1)
                    wait(dve, m["s1_done"], v)
                    wait(dve, m["mask_rdy"], v)
                    wait(dve, m["exp_rdy"], cnt(t, uo - 1, 1, 1))
                    apart(dve)
                    nc.vector.tensor_tensor_reduce(out=masked[:], in0=psum[0:S, 4, 0:KV], in1=mask_add[:, uo % 2, :], scale=1.0, scalar=-3.0e38,
                                                   op0=ALU.add, op1=ALU.max, accum_out=row_max[:]).then_inc(m["masked_rdy"], 1)
                    wait(dve, m["masked_rdy"], v)
                    nc.vector.tensor_scalar(exp_bias[:], row_max[:], -float(D) ** -0.5, None, ALU.mult).then_inc(m["eb_rdy"], 1)
                if r:
                    v = cnt(t, ur, 1, 1)
                    wait(dve, m["x3_rdy"], v)
                    norm_stats(xrow(ur), 1, "st3", "ag3", v)
                if a:
                    v = cnt(t, ua, 1, 1)
                    wait(dve, m["accT_done"], v)
                    nc.vector.tensor_tensor(xrow(ua), psum[0:S, 2, 0:D], xrow(ua), ALU.add).then_inc(m["x2_rdy"], 1)
                    wait(dve, m["x2_rdy"], v)
                    norm_stats(xrow(ua), 0, "st2", "ag2", v)
                if r:
                    v = cnt(t, ur, 1, 1)
                    wait(dve, m["rs3"], v)
                    wait(dve, m["x3nT_done"], cnt(t, ur - 1, 1, 1))
                    nc.vector.tensor_scalar(x3n[:], xrow(ur), ln_mv[:, 1, 0:1], ln_rstd[:, 1, :], ALU.subtract, ALU.mult).then_inc(m["x3n_rdy"], 1)
                if f:
                    mix(t, u, 0)
                if a:
                    v = cnt(t, ua, 1, 1)
                    wait(dve, m["rs2"], v)
                    wait(dve, m["x2nT_done"], cnt(t, ua - 1, 1, 1))
                    nc.vector.tensor_scalar(x2n[:], xrow(ua), ln_mv[:, 0, 0:1], ln_rstd[:, 0, :], ALU.subtract, ALU.mult).then_inc(m["x2n_rdy"], 1)
                if r:
                    v = cnt(t, ur, 1, 1)
                    b0 = (t * TURN + ur) * S
                    wait(dve, m["x3hi_rdy"], v)
                    nc.vector.tensor_tensor(xT_lo[:, :, bass.ds(b0, S)], psum[:, 7, 0:DC * S].rearrange("p (c s) -> p c s", c=DC),
                                            xT_hi[:, :, bass.ds(b0, S)], ALU.subtract).then_inc(m["x3lo_rdy"], 1)
                if f:
                    mix(t, u, 1)
                if o:
                    v = cnt(t, uo, 1, 1)
                    wait(dve, m["exp_rdy"], v)
                    nc.vector.reciprocal(inv_sum[:], prob_sum[:, uo % 2, :]).then_inc(m["inv_rdy"], 1)
                    wait(dve, m["inv_rdy"], v)
                    wait(dve, m["o_done"], v)
                    nc.vector.scalar_tensor_tensor(xrow(uo), psum[0:S, 6, 0:D], inv_sum[:], xrow(uo), ALU.mult, ALU.add).then_inc(m["x3_rdy"], 1)
                if f:
                    mix(t, u, 2)
                if r:
                    v = cnt(t, ur, 1, 1)
                    wait(dve, m["route_done"], v)
                    nc.vector.tensor_tensor(logits[:], psum[0:S, 7, 0:E], route_bias[:], ALU.add).then_inc(m["lg_rdy"], 1)
                    wait(dve, m["lg_rdy"], v)
                    apart(dve)
                    nc.vector.max(top8[:], logits[:]).then_inc(m["top_rdy"], 1)
                    wait(dve, m["top_rdy"], v)
                    wait(dve, m["gexp_rdy"], cnt(t, ur - 1, 1, 1))
                    nc.vector.tensor_tensor(gap[:], top8[:, 1:2], top8[:, 0:1], ALU.subtract).then_inc(m["gap_rdy"], 1)
                    apart(dve)
                    nc.vector.max_index(top8_at[:], top8[:], logits[:]).then_inc(m["at_rdy"], 1)
                if f:
                    mix(t, u, 3)
                if r:
                    v = cnt(t, ur, 1, 1)
                    wait(dve, m["gexp_rdy"], v)
                    nc.vector.tensor_scalar(gap_sum[:], gap_exp[:], 1.0, None, ALU.add).then_inc(m["gs_rdy"], 1)
                    wait(dve, m["gs_rdy"], v)
                    nc.vector.reciprocal(first_w[:], gap_sum[:]).then_inc(m["fw_rdy"], 1)
                    wait(dve, m["fw_rdy"], v)
                    nc.vector.tensor_tensor(second_w[:], gap_exp[:], first_w[:], ALU.mult).then_inc(m["sw_rdy"], 1)
                    row = comb[:, bass.ds(t * TURN + ur, 1), :].rearrange("p o e -> p (o e)")
                    wait(dve, m["at_rdy"], v)
                    nc.vector.tensor_scalar(row, iota[:], top8_at[:, 0:1], None, ALU.is_equal).then_inc(m["c1_rdy"], 1)
                    nc.vector.tensor_scalar(second[:], iota[:], top8_at[:, 1:2], None, ALU.is_equal).then_inc(m["c2_rdy"], 1)
                    wait(dve, m["sw_rdy"], v)
                    wait(dve, m["c2_rdy"], v)
                    nc.vector.tensor_scalar(second[:], second[:], second_w[:], None, ALU.mult).then_inc(m["c2w_rdy"], 1)
                    wait(dve, m["c2w_rdy"], v)
                    wait(dve, m["c1_rdy"], v)
                    nc.vector.scalar_tensor_tensor(row, row, first_w[:], second[:], ALU.mult, ALU.add).then_inc(m["comb_rdy"], 1)

            steps(dve, step)


def expert_phase(nc, ctx, dram, keep):
    def sb(name, shape, dt):
        return ctx.enter_context(nc.sbuf_tensor(name, shape, dt))

    def sem(name):
        return ctx.enter_context(nc.semaphore(name))

    x_res, xT_hi, xT_lo, comb, psum = (keep[k] for k in ("x_res", "xT_hi", "xT_lo", "comb", "psum"))
    w1_raw = sb("w1_raw", [128, 2, DC, HID], F32)
    w2_raw = sb("w2_raw", [128, 2, HC, D], F32)
    w1_hi = sb("w1_hi", [128, E, DC, HID], F16)
    w1_lo = sb("w1_lo", [128, E, DC, HID], F16)
    w2_hi = sb("w2_hi", [128, E, HC, D], F16)
    w2_lo = sb("w2_lo", [128, E, HC, D], F16)
    b1 = sb("b1", [128, HC, E], F32)
    b2 = sb("b2", [1, E, D], F32)
    b2_hi = sb("b2_hi", [1, E, D], F16)
    b2_lo = sb("b2_lo", [1, E, D], F16)
    ones_row = sb("ones_row", [1, S], F16)
    h = sb("h", [128, 2, HC, GT], F32)
    h_hi = sb("h_hi", [128, 2, HC, GT], F16)
    h_lo = sb("h_lo", [128, 2, HC, GT], F16)
    names = """b_in w1_in0 w1_in1 w2_in0 w2_in1 w1_hi_rdy w1_lo_rdy w2_hi_rdy w2_lo_rdy b2_rdy consts
        up_done h_rdy hi_rdy lo_rdy down_done y_added out_done""".split()
    m = {n: sem("x_" + n) for n in names}
    w1_in, w2_in = [m["w1_in0"], m["w1_in1"]], [m["w2_in0"], m["w2_in1"]]
    GROUPS = B // GB

    def cnt(t, u, per, extra):
        return t * (E * per) + (u * per + extra)

    def steps(engine, step):
        for e in range(E):
            step(0, e, True, e > 0)
        with engine.Fori(1, GROUPS) as t:
            for e in range(E):
                step(t, e, True, True)
        step(GROUPS, 0, False, True)

    with nc.Block() as block:

        @block.sync
        def _(sp):
            sp.dma_start(b1[:], dram["b1T"].rearrange("(c p) e -> p c e", p=128)).then_inc(m["b_in"], 16)
            sp.dma_start(b2[:], dram["b2"].rearrange("(o e) d -> o e d", o=1)).then_inc(m["b_in"], 16)
            for e in range(E):
                p = e % 2
                if e >= 2:
                    sp.wait_ge(m["w1_lo_rdy"], e - 1)
                sp.dma_start(w1_raw[:, p, :, :], dram["w1T"].rearrange("(c p) e h -> p c e h", p=128)[:, :, e, :]).then_inc(w1_in[p], 16)
                if e >= 2:
                    sp.wait_ge(m["w2_lo_rdy"], e - 1)
                sp.dma_start(w2_raw[:, p, :, :], dram["w2T"][e].rearrange("(c p) d -> p c d", p=128)).then_inc(w2_in[p], 16)
            with sp.Fori(0, GROUPS) as t:
                sp.wait_ge(m["y_added"], t * (E * GB) + E * GB)
                sp.sem_inc(m["consts"], 1)
                sp.dma_start(dram["out"].rearrange("b s d -> s b d")[:, bass.ds(t * GB, GB), :], x_res[:, bass.ds(t * GB, GB), :]).then_inc(m["out_done"], 16)
            sp.wait_ge(m["out_done"], 16 * GROUPS)

        @block.gpsimd
        def _(pool):
            for e in range(E):
                pool.wait_ge(w1_in[e % 2], 16 * (e // 2 + 1))
                nc.gpsimd.tensor_copy(w1_hi[:, e, :, :], w1_raw[:, e % 2, :, :]).then_inc(m["w1_hi_rdy"], 1)
                pool.wait_ge(w2_in[e % 2], 16 * (e // 2 + 1))
                nc.gpsimd.tensor_copy(w2_hi[:, e, :, :], w2_raw[:, e % 2, :, :]).then_inc(m["w2_hi_rdy"], 1)

        @block.tensor
        def _(pe):
            pe.wait_ge(m["b2_rdy"], 3)

            def step(t, e, up, down):
                p, q = e % 2, (e - 1) % 2
                ed = (e - 1) % E
                for c in range(HC):
                    if up:
                        if isinstance(t, int) and t == 0 and c == 0:
                            pe.wait_ge(m["w1_lo_rdy"], e + 1)
                        wait(pe, m["h_rdy"], cnt(t, e - 1, HC, c + 1))
                        n = 0
                        for w, x in ((w1_hi, xT_hi), (w1_hi, xT_lo), (w1_lo, xT_hi)):
                            for kc in range(DC):
                                last = nc.tensor.matmul(psum[:, c, 0:GT], w[:, e, kc, c * 128:(c + 1) * 128], x[:, kc, bass.ds(t * GT, GT)],
                                                        start=(n == 0), stop=(n == 5))
                                n += 1
                        last.then_inc(m["up_done"], 1)
                    if down:
                        if c == 0:
                            wait(pe, m["lo_rdy"], cnt(t, e - 1, HC, HC))
                            if isinstance(t, int) and t == 0:
                                pe.wait_ge(m["w2_lo_rdy"], e)
                        wait(pe, m["y_added"], cnt(t, e - 2, GB, c + 1))
                        out = psum[0:S, 4 + c, 0:D]
                        nc.tensor.matmul(out, ones_row[:], b2_hi[:, ed, :], start=True, stop=False)
                        nc.tensor.matmul(out, ones_row[:], b2_lo[:, ed, :], start=False, stop=False)
                        n = 0
                        for hh, w in ((h_hi, w2_hi), (h_hi, w2_lo), (h_lo, w2_hi)):
                            for kc in range(HC):
                                last = nc.tensor.matmul(out, hh[:, q, kc, c * S:(c + 1) * S], w[:, ed, kc, :], start=False, stop=(n == 11))
                                n += 1
                        last.then_inc(m["down_done"], 1)

            steps(pe, step)

        @block.scalar
        def _(act):
            act.wait_ge(m["b_in"], 32)

            def step(t, e, up, down):
                if not up:
                    return
                p = e % 2
                for c in range(HC):
                    wait(act, m["up_done"], cnt(t, e, HC, c + 1))
                    wait(act, m["lo_rdy"], cnt(t, e - 2, HC, c + 1))
                    nc.scalar.activation(h[:, p, c, :], psum[:, c, 0:GT], ACT.Relu, bias=b1[:, c, e:e + 1]).then_inc(m["h_rdy"], 1)
                    wait(act, m["h_rdy"], cnt(t, e, HC, c + 1))
                    wait(act, m["down_done"], cnt(t, e - 2, GB, GB))
                    nc.scalar.activation(h_hi[:, p, c, :], h[:, p, c, :], ACT.Copy).then_inc(m["hi_rdy"], 1)

            steps(act, step)

        @block.vector
        def _(dve):
            nc.vector.memset(ones_row[:], 1.0).then_inc(m["b2_rdy"], 1)
            dve.wait_ge(m["b_in"], 32)
            nc.vector.tensor_copy(b2_hi[:], b2[:]).then_inc(m["b2_rdy"], 1)
            dve.wait_ge(m["b2_rdy"], 2)
            nc.vector.tensor_tensor(b2_lo[:], b2[:], b2_hi[:], ALU.subtract).then_inc(m["b2_rdy"], 1)

            def weights(e):
                dve.wait_ge(m["w1_hi_rdy"], e + 1)
                nc.vector.tensor_tensor(w1_lo[:, e, :, :], w1_raw[:, e % 2, :, :], w1_hi[:, e, :, :], ALU.subtract).then_inc(m["w1_lo_rdy"], 1)
                dve.wait_ge(m["w2_hi_rdy"], e + 1)
                nc.vector.tensor_tensor(w2_lo[:, e, :, :], w2_raw[:, e % 2, :, :], w2_hi[:, e, :, :], ALU.subtract).then_inc(m["w2_lo_rdy"], 1)

            weights(0)

            def step(t, e, up, down):
                p, q = e % 2, (e - 1) % 2
                ed = (e - 1) % E
                g = t - 1 if e == 0 else t
                if isinstance(t, int) and t == 0 and e + 1 < E:
                    weights(e + 1)
                for c in range(HC):
                    if up:
                        wait(dve, m["hi_rdy"], cnt(t, e, HC, c + 1))
                        nc.vector.tensor_tensor(h_lo[:, p, c, :], h[:, p, c, :], h_hi[:, p, c, :], ALU.subtract).then_inc(m["lo_rdy"], 1)
                    if down:
                        b = g * GB + c
                        xb = x_res[:, bass.ds(b, 1), :].rearrange("p o d -> p (o d)")
                        wt = comb[:, bass.ds(b, 1), ed:ed + 1].rearrange("p o e -> p (o e)")
                        wait(dve, m["down_done"], cnt(t, e - 1, GB, c + 1))
                        wait(dve, m["y_added"], cnt(t, e - 2, GB, c + 1))
                        nc.vector.scalar_tensor_tensor(xb, psum[0:S, 4 + c, 0:D], wt, xb, ALU.mult, ALU.add).then_inc(m["y_added"], 1)

            steps(dve, step)


def build(nc, dram):
    with ExitStack() as ctx:
        def sb(name, shape, dt):
            return ctx.enter_context(nc.sbuf_tensor(name, shape, dt))

        keep = {
            "x_res": sb("x_res", [S, B, D], F32),
            "xT_hi": sb("xT_hi", [128, DC, B * S], F16),
            "xT_lo": sb("xT_lo", [128, DC, B * S], F16),
            "gate_counts": sb("gate_counts", [S, E], F32),
            "comb": sb("comb", [S, B, E], F32),
            "ident": sb("ident", [128, 128], F32),
            "iota": sb("iota", [S, E], F32),
            "psum": ctx.enter_context(nc.psum_tensor("psum", [128, 8, 512], F32)),
        }
        for phase in (attention_phase, middle_phase, expert_phase):
            with ExitStack() as scope:
                phase(nc, scope, dram, keep)


def kernel(**inputs):
    import concourse.bacc as bacc
    from concourse.bass_utils import run_bass_kernel_spmd

    a = {name: np.asarray(value) for name, value in inputs.items()}
    w_kv = a["L0_xattn_w_kv"]
    host = {
        "x": a["x"],
        "ctx": a["ctx_1024"],
        "ctxT": a["ctx_1024"].transpose(0, 2, 1),
        "mask": a["mask_Bx1xS2_fk0"],
        "wqT": a["L0_xattn_w_q"].T,
        "wkT": w_kv[:D].T,
        "wvT": w_kv[D:].T,
        "woT": a["L0_xattn_w_out"].T,
        "bo": a["L0_xattn_b_out"],
        "gate_wT": a["L0_ffn_gate_w"].T,
        "gate_b": a["L0_ffn_gate_b"],
        "weT": a["L0_ffn_expert_w"].transpose(2, 0, 1),
        "expert_bT": a["L0_ffn_expert_b"].T,
        "w1T": a["L1_ffn_W1"].transpose(2, 0, 1),
        "b1T": a["L1_ffn_b1"].T,
        "w2T": a["L1_ffn_W2"].transpose(0, 2, 1),
        "b2": a["L1_ffn_b2"],
        "route_wT": a["L1_ffn_Wg"].T,
        "route_b": a["L1_ffn_bg"],
        "ident": np.eye(128, dtype=np.float32),
        "iota": np.broadcast_to(np.arange(E, dtype=np.float32), (S, E)),
        "parity": ((np.arange(128)[:, None] // HD) % 2 == np.arange(2)).astype(np.float32),
    }
    nc = bacc.Bacc("TRN2", target_bir_lowering=False, num_devices=1)
    arrays, dram = {}, {}
    for name, value in host.items():
        arrays[f"in_{name}_dram"] = np.ascontiguousarray(value)
        dram[name] = nc.dram_tensor(f"in_{name}_dram", value.shape, mybir.dt.from_np(value.dtype), kind="ExternalInput").ap()
    dram["out"] = nc.dram_tensor("out_0_dram", (B, S, D), F32, kind="ExternalOutput").ap()
    build(nc, dram)
    result = run_bass_kernel_spmd(nc, [arrays], core_ids=[0])
    return result.results[0]["out_0_dram"]
```

```python
import numpy as np
import concourse.bass as bass
from concourse import mybir
from contextlib import ExitStack

F32 = mybir.dt.float32
F16 = mybir.dt.float16
U32 = mybir.dt.uint32
ALU = mybir.AluOpType
ACT = mybir.ActivationFunctionType
AX = mybir.AxisListType

B, S, KV, D = 32, 112, 375, 256
H, HD = 16, 16
PAIRS = H // 2
KC = 125
NKC = KV // KC
DC = D // 128
E = 8
EPS = 1e-5
UNROLL = 4
LAG_B, LAG_C, LAG_D = 2, 3, 4
ONES_ROW = 96
GB = 4
GT = GB * S
HID = 512
HC = HID // 128
TOKENS = B * S
TILE = 256
NT = (2 * TOKENS + E * (TILE - 1)) // TILE
CAP = TOKENS + 128
DUMMY = E * CAP
DISPATCH_ROWS = DUMMY + 2 * 128
ROW = 272
AT_W, AT_TOKEN = D, D + E
PAD_OUT = TOKENS
OUT_ROWS = TOKENS + 3 * 128
W_COLS = E * (DC * HID + HC * D)
W_PIECE = W_COLS // B



def count(t, u, per, extra):
    return t * (UNROLL * per) + (u * per + extra)


def wait(engine, sem, value):
    if isinstance(value, int) and value <= 0:
        return
    engine.wait_ge(sem, value)


def at_most(value, total):
    return min(value, total) if isinstance(value, int) else value


def slot_loads(t, u, slots):
    return t * (16 * UNROLL // slots) + 16 * (u // slots + 1)


def run_steps(engine, step):
    turns, lags = B // UNROLL, (0, LAG_B, LAG_C, LAG_D)
    for t in range(2):
        for u in range(UNROLL):
            step(t, u, tuple(t * UNROLL + u >= lag for lag in lags), True)
    with engine.Fori(2, turns - 1) as t:
        for u in range(UNROLL):
            step(t, u, (True,) * 4, True)
    for u in range(UNROLL):
        step(turns - 1, u, (True,) * 4, u < UNROLL - 1)
    for u in range(LAG_D):
        step(turns, u, tuple(u < lag for lag in lags), False)


def attention_phase(nc, ctx, dram, keep):
    def sb(name, shape, dt):
        return ctx.enter_context(nc.sbuf_tensor(name, shape, dt))

    def sem(name):
        return ctx.enter_context(nc.semaphore(name))

    x_res, xT_hi, xT_lo, gate_counts = keep["x_res"], keep["xT_hi"], keep["xT_lo"], keep["gate_counts"]
    ident, iota = keep["ident"], keep["iota"]
    psum = keep["psum"]

    wq = sb("wq", [128, DC, D], F32)
    wk = sb("wk", [128, DC, D], F32)
    wv = sb("wv", [128, DC, D], F32)
    wo = sb("wo", [128, DC, D], F32)
    bo = sb("bo", [S, D], F32)
    gate_w = sb("gate_w", [128, DC, E], F32)
    gate_whi = sb("gate_whi", [128, DC, E], F16)
    gate_wlo = sb("gate_wlo", [128, DC, E], F16)
    wk_hi, wk_lo = sb("wk_hi", [128, DC, D], F16), sb("wk_lo", [128, DC, D], F16)
    wv_hi, wv_lo = sb("wv_hi", [128, DC, D], F16), sb("wv_lo", [128, DC, D], F16)
    gate_bias = sb("gate_bias", [S, E], F32)
    parity = sb("parity", [128, 2], F32)
    half = sb("half", [S, 1], F32)
    ctxT = sb("ctxT", [128, 2, DC, KV], F32)
    ctx_hi = sb("ctx_hi", [128, 2, DC, KV], F16)
    ctx_lo = sb("ctx_lo", [128, 2, DC, KV], F16)
    ln1_stats = sb("ln1_stats", [S, 6], F32)
    ln1_mv = sb("ln1_mv", [S, 2], F32)
    ln1_var = sb("ln1_var", [S, 1], F32)
    ln1_rstd = sb("ln1_rstd", [S, 1], F32)
    xn = sb("xn", [S, D], F32)
    xnT = sb("xnT", [128, DC, S], F32)
    q_hi = sb("q_hi", [128, 2, DC, 2, S], F16)
    q_lo = sb("q_lo", [128, 2, DC, 2, S], F16)
    k_hi = sb("k_hi", [128, 2, DC, KV + 1], F16)
    k_lo = sb("k_lo", [128, 2, DC, KV + 1], F16)
    q_stack = sb("q_stack", [128, UNROLL, PAIRS, 2 * S], F16)
    k_stack = sb("k_stack", [128, UNROLL, PAIRS, KV + 1], F16)
    v_aug = sb("v_aug", [KC, UNROLL, NKC, H, 32], F32)
    smax = sb("smax", [S, 2, H], F32)
    neg_max = sb("neg_max", [H, S], F16)
    probsT = sb("probsT", [KC, 2, NKC, H, S], F32)
    oT = sb("oT", [128, 4, S], F32)
    inv_sum = sb("inv_sum", [S, 4, 4, 1], F32)
    o_nat = sb("o_nat", [S, D], F32)
    onT = sb("onT", [128, DC, S], F32)
    ln2_stats = sb("ln2_stats", [S, 6], F32)
    ln2_mv = sb("ln2_mv", [S, 2], F32)
    ln2_var = sb("ln2_var", [S, 1], F32)
    ln2_rstd = sb("ln2_rstd", [S, 1], F32)
    x1n = sb("x1n", [S, D], F32)
    logits = sb("logits", [S, E], F32)
    top8 = sb("top8", [S, 8], F32)
    top8_at = sb("top8_at", [S, 8], U32)

    names = """const_in weights_in setup_done pool_setup weight_split ctxhi_ready ctxlo_ready
        ctx_in0 ctx_in1 x_in0 x_in1 q_in0 q_in1 q_in2 q_in3 k_in0 k_in1 k_in2 k_in3 q_pool0 q_pool1 q_pool2 q_pool3 k_pool0 k_pool1 k_pool2 k_pool3 m_in
        mT_done xnT_done q_done k_done v_done scores_done scoresT_done pv_done oT_back_done onT_done
        out_done x1nT_done gate_done
        negm_ready xnT_ready qhi_ready khi_ready exp_done oT_ready onT_ready x1hi_ready v_ready
        ln1_st ln1_agg xn_ready max_done qlo_ready klo_ready inv_ready o_ready x1_ready ln2_st ln2_agg
        x1n_ready x1lo_ready logits_ready top_ready at_ready count1 count2
        passed ln1_eps ln1_rs xb_ready ln2_eps ln2_rs""".split()
    m = {n: sem("a_" + n) for n in names}
    keep["attention_semaphores"] = list(m.values())
    ctx_in = [m["ctx_in0"], m["ctx_in1"]]
    x_in = [m["x_in0"], m["x_in1"]]
    q_in = [m[f"q_in{i}"] for i in range(4)]
    q_pool_in = [m[f"q_pool{i}"] for i in range(4)]
    k_in = [m[f"k_in{i}"] for i in range(4)]
    k_pool_in = [m[f"k_pool{i}"] for i in range(4)]

    bank_a = psum[:, 6, :]
    bank_d = psum[:, 7, :]
    N_CONST, N_W = 3, 7

    def apart(engine):
        engine.sem_inc(m["passed"], 1)

    KEY_ROWS = ((0, k_hi), (1, k_lo), (2, k_hi))
    QUERY_ROWS = ((0, q_hi), (1, q_hi), (2, q_lo))

    def query_rows(engine, u, part, src, j, arrived):
        engine.dma_start(q_stack[32 * part:32 * part + 32, u % 4, j::4, :],
                         src[32 * j:32 * j + 32, u % 2, :, :, :].rearrange("p c s q -> p c (s q)")).then_inc(arrived[u % 4], 16)

    def key_rows(engine, u, part, src, j, arrived):
        engine.dma_start(k_stack[32 * part:32 * part + 32, u % 4, j::4, 0:KV],
                         src[32 * j:32 * j + 32, u % 2, :, 0:KV]).then_inc(arrived[u % 4], 16)

    with nc.Block() as block:

        @block.sync
        def _(sp):
            for dst, src in ((ident[:], dram["ident"]), (iota[:], dram["iota"]), (parity[:], dram["parity"])):
                sp.dma_start(dst, src).then_inc(m["const_in"], 16)

            def load(t, u):
                b = t * UNROLL + u
                wait(sp, m["ctxlo_ready"], count(t, u - 2, 1, 1))
                apart(sp)
                sp.dma_start(x_res[:, bass.ds(b, 1), :].rearrange("p o d -> p (o d)"),
                             dram["x"][bass.ds(b, 1), :, :].rearrange("o s d -> (o s) d")).then_inc(x_in[u % 2], 16)
                sp.dma_start(ctxT[:, u % 2, :, :],
                             dram["ctxT"][bass.ds(b, 1), :, :].rearrange("o (c p) s -> p (o c) s", p=128)).then_inc(ctx_in[u % 2], 16)

            load(0, 0)
            load(0, 1)
            for dst, src in ((wq, "wqT"), (wk, "wkT"), (wv, "wvT"), (wo, "woT"), (gate_w, "gate_wT")):
                sp.dma_start(dst[:], dram[src].rearrange("(c p) n -> p c n", p=128)).then_inc(m["weights_in"], 16)
            sp.dma_start(bo[:], dram["bo"].rearrange("(o n) -> o n", o=1).broadcast_to([S, D])).then_inc(m["weights_in"], 16)
            sp.dma_start(gate_bias[:], dram["gate_b"].rearrange("(o n) -> o n", o=1).broadcast_to([S, E])).then_inc(m["weights_in"], 16)
            sp.wait_ge(m["setup_done"], 4)

            def step(t, u, on, more):
                a, b_, c, d = on
                if not isinstance(t, int) or t * UNROLL + u + 2 < B:
                    load(t, u + 2)
                if c:
                    wait(sp, m["negm_ready"], count(t, u - LAG_C, 1, 1))
                    apart(sp)
                    row = q_stack[ONES_ROW:ONES_ROW + 1, (u - LAG_C) % 4, :, :].rearrange("o r (s q) -> o (r s) q", s=2)
                    sp.dma_start(row, neg_max[:, :]).then_inc(m["m_in"], 16)
                if a:
                    wait(sp, m["scoresT_done"], count(t, u - 4, 6, 6))
                    apart(sp)
                    wait(sp, m["qhi_ready"], count(t, u, 2, 2))
                    apart(sp)
                    for part, src in QUERY_ROWS[:2]:
                        for j in range(4):
                            query_rows(sp, u, part, src, j, q_in)
                    wait(sp, m["khi_ready"], count(t, u, 2, 2))
                    apart(sp)
                    for j in range(4):
                        key_rows(sp, u, *KEY_ROWS[0], j, k_in)
                    wait(sp, m["klo_ready"], count(t, u, 2, 2))
                    apart(sp)
                    for j in range(4):
                        key_rows(sp, u, *KEY_ROWS[1], j, k_in)

            run_steps(sp, step)

        @block.gpsimd
        def _(pool):
            nc.gpsimd.memset(v_aug[:], 0.0).then_inc(m["pool_setup"], 1)
            nc.gpsimd.memset(half[:], -0.5).then_inc(m["pool_setup"], 1)
            pool.wait_ge(m["pool_setup"], 2)
            nc.gpsimd.memset(v_aug[:, :, :, :, HD:HD + 1], 1.0).then_inc(m["setup_done"], 1)
            pool.wait_ge(m["weights_in"], 16 * N_W)

            def ln1_rstd_of(t, u):
                wait(pool, m["ln1_agg"], count(t, u, 1, 1))
                apart(pool)
                nc.gpsimd.tensor_scalar(ln1_var[:], ln1_mv[:, 1:2], EPS, None, ALU.add).then_inc(m["ln1_eps"], 1)
                wait(pool, m["ln1_eps"], count(t, u, 1, 1))
                nc.gpsimd.tensor_tensor(ln1_rstd[:], ln1_var[:], half[:], ALU.pow).then_inc(m["ln1_rs"], 1)

            def ctx_low(t, u):
                wait(pool, m["ctxhi_ready"], count(t, u, 1, 1))
                wait(pool, m["v_done"], count(t, u - 2, 2, 2))
                nc.gpsimd.tensor_tensor(ctx_lo[:, u % 2, :, :], ctxT[:, u % 2, :, :], ctx_hi[:, u % 2, :, :], ALU.subtract).then_inc(m["ctxlo_ready"], 1)

            ln1_rstd_of(0, 0)
            ctx_low(0, 0)

            def step(t, u, on, more):
                b = t * UNROLL + u
                if on[0]:
                    wait(pool, m["xn_ready"], count(t, u, 1, 1))
                    apart(pool)
                    xb = x_res[:, bass.ds(b, 1), :].rearrange("p o d -> p (o d)")
                    nc.gpsimd.tensor_tensor(xb, xb, bo[:], ALU.add).then_inc(m["xb_ready"], 1)
                if more:
                    ctx_low(t, u + 1)
                if on[0]:
                    wait(pool, m["scoresT_done"], count(t, u - 4, 6, 6))
                    wait(pool, m["qlo_ready"], count(t, u, 2, 2))
                    apart(pool)
                    for j in range(4):
                        query_rows(pool, u, *QUERY_ROWS[2], j, q_pool_in)
                if on[3]:
                    wait(pool, m["ln2_agg"], count(t, u - LAG_D, 1, 1))
                    apart(pool)
                    nc.gpsimd.tensor_scalar(ln2_var[:], ln2_mv[:, 1:2], EPS, None, ALU.add).then_inc(m["ln2_eps"], 1)
                    wait(pool, m["ln2_eps"], count(t, u - LAG_D, 1, 1))
                    nc.gpsimd.tensor_tensor(ln2_rstd[:], ln2_var[:], half[:], ALU.pow).then_inc(m["ln2_rs"], 1)
                if more:
                    ln1_rstd_of(t, u + 1)
                if on[0]:
                    wait(pool, m["khi_ready"], count(t, u, 2, 2))
                    apart(pool)
                    for j in range(4):
                        key_rows(pool, u, *KEY_ROWS[2], j, k_pool_in)

            run_steps(pool, step)

        @block.tensor
        def _(pe):
            pe.wait_ge(m["const_in"], 16 * N_CONST)
            pe.wait_ge(m["weights_in"], 16 * N_W)
            pe.wait_ge(m["setup_done"], 4)
            pe.wait_ge(m["weight_split"], 6)

            def scores(t, u, h):
                b4, s = (u - LAG_B) % 4, h % 2
                n = h + 16 * (u - LAG_B)
                if h == 0:
                    wait(pe, q_in[b4], slot_loads(t, u - LAG_B, 4) * 8)
                    wait(pe, q_pool_in[b4], slot_loads(t, u - LAG_B, 4) * 4)
                    wait(pe, k_in[b4], slot_loads(t, u - LAG_B, 4) * 8)
                    wait(pe, k_pool_in[b4], slot_loads(t, u - LAG_B, 4) * 4)
                wait(pe, m["max_done"], count(t, u - LAG_B, 16, h - 1))
                nc.tensor.matmul(psum[0:S, 4 + s, 0:KV], q_stack[0:96, b4, h // 2, s * S:(s + 1) * S],
                                 k_stack[0:96, b4, h // 2, 0:KV], start=True, stop=True).then_inc(m["scores_done"], 1)

            def scoresT(t, u, n):
                b4, hg, c = (u - LAG_C) % 4, n // NKC, n % NKC
                if n == 0:
                    wait(pe, m["m_in"], count(t, u - LAG_C, 16, 16))
                wait(pe, m["exp_done"], count(t, u - LAG_C, 6, n - 1))
                for r in range(4):
                    pair = 4 * hg + r
                    last = nc.tensor.matmul(psum[0:KC, 2 * (n % 2) + r // 2, (r % 2) * 2 * S:(r % 2 + 1) * 2 * S],
                                            k_stack[0:ONES_ROW + 1, b4, pair, c * KC:(c + 1) * KC],
                                            q_stack[0:ONES_ROW + 1, b4, pair, :], start=True, stop=True)
                last.then_inc(m["scoresT_done"], 1)

            def step(t, u, on, more):
                a, b_, c, d = on
                b2a, b4d, b2d = u % 2, (u - LAG_D) % 4, (u - LAG_D) % 2
                bd = t * UNROLL + (u - LAG_D)

                def values(g):
                    if g % 2 == 0:
                        wait(pe, m["exp_done"], count(t, u - LAG_D, 6, 3 + 3 * (g // 2)))
                    for cc in range(NKC):
                        for j in range(4):
                            h = 4 * g + j
                            last = nc.tensor.matmul(bank_d[32 * j:32 * j + 32, g * S:(g + 1) * S], v_aug[:, b4d, cc, h, :],
                                                    probsT[:, b2d, cc, h, :], start=(cc == 0), stop=(cc == NKC - 1))
                    if g == 3:
                        last.then_inc(m["pv_done"], 1)

                def keys(mc):
                    if mc == 0:
                        wait(pe, m["ctxlo_ready"], count(t, u, 1, 1))
                        wait(pe, m["qlo_ready"], count(t, u, 2, 2))
                    else:
                        wait(pe, m["klo_ready"], count(t, u, 2, 1))
                    n = 0
                    for w, x in ((wk_hi, ctx_hi), (wk_hi, ctx_lo), (wk_lo, ctx_hi)):
                        for kc in range(DC):
                            last = nc.tensor.matmul(bank_a[:, 0:KV], w[:, kc, mc * 128:(mc + 1) * 128], x[:, b2a, kc, :],
                                                    start=(n == 0), stop=(n == 3 * DC - 1))
                            n += 1
                    last.then_inc(m["k_done"], 1)

                def vals(chunks):
                    if chunks[0] == 0:
                        wait(pe, m["klo_ready"], count(t, u, 2, 2))
                    else:
                        wait(pe, m["v_ready"], count(t, u, 3, 2))
                    for n, cc in enumerate(chunks):
                        done = 0
                        for x, w in ((ctx_hi, wv_hi), (ctx_lo, wv_hi), (ctx_hi, wv_lo)):
                            for kc in range(DC):
                                last = nc.tensor.matmul(bank_a[0:KC, n * D:(n + 1) * D], x[:, b2a, kc, cc * KC:(cc + 1) * KC], w[:, kc, :],
                                                        start=(done == 0), stop=(done == 3 * DC - 1))
                                done += 1
                    last.then_inc(m["v_done"], 1)

                def pair_scores(h):
                    if b_:
                        scores(t, u, h)
                        scores(t, u, h + 1)

                def unit_scoresT(n):
                    if c:
                        scoresT(t, u, n)

                if a or c:
                    wait(pe, m["v_ready"], at_most(count(t, u - 1, 3, 3), 3 * B))
                if a:
                    wait(pe, m["xn_ready"], count(t, u, 1, 1))
                    for kc in range(DC):
                        last = nc.tensor.transpose(bank_a[:, kc * S:(kc + 1) * S], xn[:, kc * 128:(kc + 1) * 128], ident[0:S, 0:S])
                    last.then_inc(m["xnT_done"], 1)
                if d:
                    wait(pe, m["logits_ready"], count(t, u - LAG_D - 1, 1, 1))
                    values(0)
                if c:
                    wait(pe, m["max_done"], count(t, u - LAG_C, 16, 16))
                    if a:
                        wait(pe, m["xnT_ready"], count(t, u, 1, 1))
                    nc.tensor.transpose(bank_a[0:H, 2 * S:3 * S], smax[:, (u - LAG_C) % 2, :], ident[0:S, 0:S]).then_inc(m["mT_done"], 1)
                pair_scores(0)
                if d:
                    values(1)
                if a:
                    wait(pe, m["xnT_ready"], count(t, u, 1, 1))
                    if c:
                        wait(pe, m["negm_ready"], count(t, u - LAG_C, 1, 1))
                    for mc in range(DC):
                        for kc in range(DC):
                            last = nc.tensor.matmul(bank_a[:, mc * S:(mc + 1) * S], wq[:, kc, mc * 128:(mc + 1) * 128], xnT[:, kc, :],
                                                    start=(kc == 0), stop=(kc == DC - 1))
                    last.then_inc(m["q_done"], 1)
                pair_scores(2)
                if d:
                    values(2)
                if d:
                    values(3)
                pair_scores(4)
                if a:
                    keys(0)
                if d:
                    wait(pe, m["oT_ready"], count(t, u - LAG_D, 1, 1))
                    for g in range(4):
                        last = nc.tensor.transpose(bank_d[0:S, g * 128:(g + 1) * 128], oT[:, g, :], ident[:, :])
                    last.then_inc(m["oT_back_done"], 1)
                pair_scores(6)
                unit_scoresT(0)
                unit_scoresT(1)
                if a:
                    keys(1)
                if d:
                    wait(pe, m["o_ready"], count(t, u - LAG_D, 1, 1))
                    for kc in range(DC):
                        last = nc.tensor.transpose(bank_d[:, kc * S:(kc + 1) * S], o_nat[:, kc * 128:(kc + 1) * 128], ident[0:S, 0:S])
                    last.then_inc(m["onT_done"], 1)
                pair_scores(8)
                unit_scoresT(2)
                if d:
                    wait(pe, m["onT_ready"], count(t, u - LAG_D, 1, 1))
                    for kc in range(DC):
                        last = nc.tensor.matmul(bank_d[0:S, 0:D], onT[:, kc, :], wo[:, kc, :], start=(kc == 0), stop=(kc == DC - 1))
                    last.then_inc(m["out_done"], 1)
                pair_scores(10)
                if a:
                    vals((0, 1))
                pair_scores(12)
                unit_scoresT(3)
                if d:
                    wait(pe, m["x1n_ready"], count(t, u - LAG_D, 1, 1))
                    for kc in range(DC):
                        last = nc.tensor.transpose(bank_d[:, kc * S:(kc + 1) * S], x1n[:, kc * 128:(kc + 1) * 128], ident[0:S, 0:S])
                    last.then_inc(m["x1nT_done"], 1)
                pair_scores(14)
                unit_scoresT(4)
                if a:
                    vals((2,))
                unit_scoresT(5)
                if d:
                    wait(pe, m["x1lo_ready"], count(t, u - LAG_D, 1, 1))
                    n = 0
                    for left, right in ((xT_hi, gate_whi), (xT_hi, gate_wlo), (xT_lo, gate_whi)):
                        for kc in range(DC):
                            last = nc.tensor.matmul(bank_d[0:S, 0:E], left[:, kc, bass.ds(bd * S, S)], right[:, kc, :],
                                                    start=(n == 0), stop=(n == 3 * DC - 1))
                            n += 1
                    last.then_inc(m["gate_done"], 1)

            run_steps(pe, step)

        @block.scalar
        def _(act):
            act.wait_ge(m["setup_done"], 4)

            def exps(t, u, n):
                p, hg, c = (u - LAG_C) % 2, n // NKC, n % NKC
                if n == 0:
                    wait(act, m["pv_done"], count(t, u - LAG_C - 2, 1, 1))
                wait(act, m["scoresT_done"], count(t, u - LAG_C, 6, n + 1))
                nc.scalar.activation(probsT[:, p, c, 8 * hg:8 * hg + 8, :].rearrange("p (k h) q -> p k (h q)", k=2),
                                     psum[0:KC, 2 * (n % 2):2 * (n % 2) + 2, 0:4 * S], ACT.Exp,
                                     scale=float(HD) ** -0.5).then_inc(m["exp_done"], 1)

            def ctx_high(t, u):
                wait(act, ctx_in[u % 2], slot_loads(t, u, 2))
                wait(act, m["v_done"], count(t, u - 2, 2, 2))
                nc.scalar.activation(ctx_hi[:, u % 2, :, :], ctxT[:, u % 2, :, :], ACT.Copy).then_inc(m["ctxhi_ready"], 1)

            ctx_high(0, 0)

            def step(t, u, on, more):
                a, b_, c, d = on
                bd = t * UNROLL + (u - LAG_D)

                def khi(mc):
                    wait(act, m["k_done"], count(t, u, 2, mc + 1))
                    if mc == 0:
                        wait(act, k_in[(u - 2) % 4], slot_loads(t, u - 2, 4) * 8)
                        wait(act, k_pool_in[(u - 2) % 4], slot_loads(t, u - 2, 4) * 4)
                    nc.scalar.activation(k_hi[:, u % 2, mc, 0:KV], bank_a[:, 0:KV], ACT.Copy).then_inc(m["khi_ready"], 1)

                def vout(chunks):
                    if chunks[0] == 0:
                        wait(act, m["pv_done"], count(t, u - 4, 1, 1))
                    wait(act, m["v_done"], count(t, u, 2, 1 if chunks[0] == 0 else 2))
                    for n, cc in enumerate(chunks):
                        nc.scalar.activation(v_aug[:, u % 4, cc, :, 0:HD], bank_a[0:KC, n * D:(n + 1) * D].rearrange("p (h w) -> p h w", w=HD),
                                             ACT.Copy).then_inc(m["v_ready"], 1)

                if a:
                    wait(act, m["xnT_done"], count(t, u, 1, 1))
                    wait(act, m["q_done"], count(t, u - 1, 1, 1))
                    nc.scalar.activation(xnT[:, :, :].rearrange("p c s -> p (c s)"), bank_a[:, 0:DC * S], ACT.Copy).then_inc(m["xnT_ready"], 1)
                if c:
                    wait(act, m["mT_done"], count(t, u - LAG_C, 1, 1))
                    wait(act, m["m_in"], count(t, u - LAG_C - 1, 16, 16))
                    nc.scalar.activation(neg_max[:, :], bank_a[0:H, 2 * S:3 * S], ACT.Copy, scale=-1.0).then_inc(m["negm_ready"], 1)
                if more:
                    ctx_high(t, u + 1)
                if a:
                    wait(act, m["q_done"], count(t, u, 1, 1))
                    wait(act, q_in[(u - 2) % 4], slot_loads(t, u - 2, 4) * 8)
                    for s in range(2):
                        nc.scalar.activation(q_hi[:, u % 2, :, s, :], bank_a[:, 0:DC * S].rearrange("p (c s) -> p c s", c=DC),
                                             ACT.Copy, scale=parity[:, s:s + 1]).then_inc(m["qhi_ready"], 1)
                if d:
                    wait(act, m["pv_done"], count(t, u - LAG_D, 1, 1))
                    wait(act, m["oT_back_done"], count(t, u - LAG_D - 1, 1, 1))
                    nc.scalar.activation(oT[:, :, :].rearrange("p g s -> p (g s)"), bank_d[:, 0:4 * S], ACT.Copy).then_inc(m["oT_ready"], 1)
                if a:
                    khi(0)
                if c:
                    exps(t, u, 0)
                    exps(t, u, 1)
                if d:
                    wait(act, m["onT_done"], count(t, u - LAG_D, 1, 1))
                    wait(act, m["out_done"], count(t, u - LAG_D - 1, 1, 1))
                    nc.scalar.activation(onT[:, :, :].rearrange("p c s -> p (c s)"), bank_d[:, 0:DC * S], ACT.Copy).then_inc(m["onT_ready"], 1)
                if a:
                    khi(1)
                if c:
                    exps(t, u, 2)
                if a:
                    vout((0, 1))
                if c:
                    exps(t, u, 3)
                if c:
                    exps(t, u, 4)
                if a:
                    vout((2,))
                if c:
                    exps(t, u, 5)

            run_steps(act, step)

        @block.vector
        def _(dve):
            nc.vector.memset(q_stack[96:128, :, :, :], 0.0).then_inc(m["setup_done"], 1)
            nc.vector.memset(k_stack[96:128, :, :, :], 1.0).then_inc(m["setup_done"], 1)
            nc.vector.memset(gate_counts[:], 0.0).then_inc(m["setup_done"], 1)
            dve.wait_ge(m["weights_in"], 16 * N_W)
            nc.vector.tensor_copy(gate_whi[:], gate_w[:]).then_inc(m["weight_split"], 1)
            dve.wait_ge(m["weight_split"], 1)
            nc.vector.tensor_tensor(gate_wlo[:], gate_w[:], gate_whi[:], ALU.subtract).then_inc(m["weight_split"], 1)
            nc.vector.tensor_copy(wk_hi[:], wk[:]).then_inc(m["weight_split"], 1)
            nc.vector.tensor_copy(wv_hi[:], wv[:]).then_inc(m["weight_split"], 1)
            dve.wait_ge(m["weight_split"], 4)
            nc.vector.tensor_tensor(wk_lo[:], wk[:], wk_hi[:], ALU.subtract).then_inc(m["weight_split"], 1)
            nc.vector.tensor_tensor(wv_lo[:], wv[:], wv_hi[:], ALU.subtract).then_inc(m["weight_split"], 1)
            dve.wait_ge(m["const_in"], 16 * N_CONST)
            dve.wait_ge(m["setup_done"], 4)

            def maxima(t, u, heads):
                for h in heads:
                    if h == 0:
                        wait(dve, m["mT_done"], count(t, u - LAG_B - 2, 1, 1))
                    wait(dve, m["scores_done"], count(t, u - LAG_B, 16, h + 1))
                    nc.vector.reduce_max(smax[:, (u - LAG_B) % 2, h:h + 1], psum[0:S, 4 + h % 2, 0:KV], AX.X).then_inc(m["max_done"], 1)

            def ln1_stats_of(t, u):
                xb = x_res[:, bass.ds(t * UNROLL + u, 1), :].rearrange("p o d -> p (o d)")
                wait(dve, x_in[u % 2], slot_loads(t, u, 2))
                apart(dve)
                nc.vector.bn_stats(ln1_stats[:], xb).then_inc(m["ln1_st"], 1)
                wait(dve, m["ln1_st"], count(t, u, 1, 1))
                apart(dve)
                nc.vector.bn_aggr(ln1_mv[:], ln1_stats[:]).then_inc(m["ln1_agg"], 1)

            def ln1_out(t, u):
                xb = x_res[:, bass.ds(t * UNROLL + u, 1), :].rearrange("p o d -> p (o d)")
                wait(dve, m["ln1_rs"], count(t, u, 1, 1))
                wait(dve, m["xnT_done"], count(t, u - 1, 1, 1))
                nc.vector.tensor_scalar(xn[:], xb, ln1_mv[:, 0:1], ln1_rstd[:], ALU.subtract, ALU.mult).then_inc(m["xn_ready"], 1)

            ln1_stats_of(0, 0)
            ln1_out(0, 0)

            def step(t, u, on, more):
                a, b_, c, d = on
                bd = t * UNROLL + (u - LAG_D)

                def klo(mc):
                    if a:
                        wait(dve, m["khi_ready"], count(t, u, 2, mc + 1))
                        nc.vector.tensor_tensor(k_lo[:, u % 2, mc, 0:KV], bank_a[:, 0:KV], k_hi[:, u % 2, mc, 0:KV],
                                                ALU.subtract).then_inc(m["klo_ready"], 1)

                def one_max(h):
                    if b_:
                        maxima(t, u, (h,))

                def pair_max(h):
                    one_max(h)
                    one_max(h + 1)

                pair_max(0)
                pair_max(2)
                if a:
                    for s in range(2):
                        wait(dve, m["qhi_ready"], count(t, u, 2, 2))
                        if s == 0:
                            wait(dve, q_pool_in[(u - 2) % 4], slot_loads(t, u - 2, 4) * 4)
                        nc.vector.scalar_tensor_tensor(q_lo[:, u % 2, :, s, :], bank_a[:, 0:DC * S].rearrange("p (c s) -> p c s", c=DC),
                                                       parity[:, s:s + 1], q_hi[:, u % 2, :, s, :],
                                                       ALU.mult, ALU.subtract).then_inc(m["qlo_ready"], 1)
                pair_max(4)
                klo(0)
                if d:
                    o4 = bank_d[0:S, :].rearrange("p (g j w) -> p g j w", g=4, j=4)
                    wait(dve, m["oT_back_done"], count(t, u - LAG_D, 1, 1))
                    nc.vector.reciprocal(inv_sum[:], o4[:, :, :, HD:HD + 1]).then_inc(m["inv_ready"], 1)
                    wait(dve, m["inv_ready"], count(t, u - LAG_D, 1, 1))
                    wait(dve, m["onT_done"], count(t, u - LAG_D - 1, 1, 1))
                    nc.vector.tensor_tensor(o_nat[:].rearrange("p (h w) -> p h w", w=HD),
                                            bank_d[0:S, :].rearrange("p (h w) -> p h w", w=32)[:, :, 0:HD],
                                            inv_sum[:].rearrange("p g j o -> p (g j) o").broadcast_to([S, H, HD]),
                                            ALU.mult).then_inc(m["o_ready"], 1)
                pair_max(6)
                pair_max(8)
                klo(1)
                if d:
                    x1 = x_res[:, bass.ds(bd, 1), :].rearrange("p o d -> p (o d)")
                    wait(dve, m["out_done"], count(t, u - LAG_D, 1, 1))
                    wait(dve, m["xb_ready"], count(t, u - LAG_D, 1, 1))
                    nc.vector.tensor_tensor(x1, bank_d[0:S, 0:D], x1, ALU.add).then_inc(m["x1_ready"], 1)
                if d:
                    wait(dve, m["x1_ready"], count(t, u - LAG_D, 1, 1))
                    apart(dve)
                    nc.vector.bn_stats(ln2_stats[:], x1).then_inc(m["ln2_st"], 1)
                one_max(10)
                if d:
                    wait(dve, m["ln2_st"], count(t, u - LAG_D, 1, 1))
                    apart(dve)
                    nc.vector.bn_aggr(ln2_mv[:], ln2_stats[:]).then_inc(m["ln2_agg"], 1)
                one_max(11)
                if more:
                    ln1_stats_of(t, u + 1)
                if d:
                    wait(dve, m["ln2_rs"], count(t, u - LAG_D, 1, 1))
                    wait(dve, m["x1nT_done"], count(t, u - LAG_D - 1, 1, 1))
                    nc.vector.tensor_scalar(x1n[:], x1, ln2_mv[:, 0:1], ln2_rstd[:], ALU.subtract, ALU.mult).then_inc(m["x1n_ready"], 1)
                one_max(12)
                one_max(13)
                if d:
                    wait(dve, m["x1nT_done"], count(t, u - LAG_D, 1, 1))
                    nc.vector.tensor_copy(xT_hi[:, :, bass.ds(bd * S, S)], bank_d[:, 0:DC * S].rearrange("p (c s) -> p c s", c=DC)).then_inc(m["x1hi_ready"], 1)
                    wait(dve, m["x1hi_ready"], count(t, u - LAG_D, 1, 1))
                    nc.vector.tensor_tensor(xT_lo[:, :, bass.ds(bd * S, S)], bank_d[:, 0:DC * S].rearrange("p (c s) -> p c s", c=DC),
                                            xT_hi[:, :, bass.ds(bd * S, S)], ALU.subtract).then_inc(m["x1lo_ready"], 1)
                if more:
                    ln1_out(t, u + 1)
                pair_max(14)
                if d:
                    wait(dve, m["gate_done"], count(t, u - LAG_D, 1, 1))
                    wait(dve, m["count2"], count(t, u - LAG_D - 1, 1, 1))
                    nc.vector.tensor_tensor(logits[:], bank_d[0:S, 0:E], gate_bias[:], ALU.add).then_inc(m["logits_ready"], 1)
                if d:
                    wait(dve, m["logits_ready"], count(t, u - LAG_D, 1, 1))
                    apart(dve)
                    nc.vector.max(top8[:], logits[:]).then_inc(m["top_ready"], 1)
                    wait(dve, m["top_ready"], count(t, u - LAG_D, 1, 1))
                    apart(dve)
                    nc.vector.max_index(top8_at[:], top8[:], logits[:]).then_inc(m["at_ready"], 1)
                    wait(dve, m["at_ready"], count(t, u - LAG_D, 1, 1))
                    nc.vector.scalar_tensor_tensor(gate_counts[:], iota[:], top8_at[:, 0:1], gate_counts[:],
                                                   ALU.is_equal, ALU.add).then_inc(m["count1"], 1)
                    wait(dve, m["count1"], count(t, u - LAG_D, 1, 1))
                    nc.vector.scalar_tensor_tensor(gate_counts[:], iota[:], top8_at[:, 1:2], gate_counts[:],
                                                   ALU.is_equal, ALU.add).then_inc(m["count2"], 1)

            run_steps(dve, step)


def middle_phase(nc, ctx, dram, keep):
    def sb(name, shape, dt):
        return ctx.enter_context(nc.sbuf_tensor(name, shape, dt))

    def sem(name):
        return ctx.enter_context(nc.semaphore(name))

    x_res, xT_hi, xT_lo, gate_counts = keep["x_res"], keep["xT_hi"], keep["xT_lo"], keep["gate_counts"]
    ident, iota, psum, cum = keep["ident"], keep["iota"], keep["psum"], keep["cum"]

    we = sb("we", [128, DC, E, D], F32)
    we_hi = sb("we_hi", [128, DC, E, D], F16)
    we_lo = sb("we_lo", [128, DC, E, D], F16)
    expert_b = sb("expert_b", [128, DC, E], F32)
    share = sb("share", [128, E], F32)
    neg_bias = sb("neg_bias", [128, DC, E], F32)
    bias_sum = sb("bias_sum", [128, DC], F32)
    ones = sb("ones", [S, 128], F32)
    half = sb("half2", [S, 1], F32)
    acc = sb("acc", [128, 2, DC, GT], F32)
    ctxT = sb("ctxT2", [128, 2, DC, KV], F32)
    ctx_rows = sb("ctx_rows", [KC, 2, NKC, D], F32)
    mask = sb("mask", [S, 2, KV], F32)
    mask_add = sb("mask_add", [S, 2, KV], F32)
    ln_stats = sb("ln_stats", [S, 2, 6], F32)
    ln_mv = sb("ln_mv", [S, 2, 2], F32)
    ln_var = sb("ln_var", [S, 2, 1], F32)
    ln_rstd = sb("ln_rstd", [S, 2, 1], F32)
    x2n = sb("x2n", [S, D], F32)
    x2nT = sb("x2nT", [128, DC, S], F32)
    masked = sb("masked", [S, KV], F32)
    row_max = sb("row_max", [S, 1], F32)
    exp_bias = sb("exp_bias", [S, 1], F32)
    probs = sb("probs", [S, KV], F32)
    prob_sum = sb("prob_sum", [S, 2, 1], F32)
    inv_sum = sb("inv_sum2", [S, 1], F32)
    probsT = sb("probsT2", [KC, NKC, S], F32)
    rows = sb("rows", [S, 2, ROW], F32)
    place = sb("place", [S, 1], F32)
    slot_base = sb("slot_base", [S, E], F32)
    before = sb("before", [S, S], F32)
    first = sb("first", [S, E], F32)
    chosen = sb("chosen", [S, E], F32)
    second_row = sb("second_row", [S, E], F32)
    slot_of = sb("slot_of", [S, E], F32)
    picked = sb("picked", [S, 2, E], F32)
    slots = sb("slots", [S, 2], F32)
    slots_at = sb("slots_at", [S, 2, 2], U32)
    w_raw = sb("w_raw", [128, 2, W_PIECE], F32)
    w_hi, w_lo = keep["w_hi"], keep["w_lo"]
    pads = sb("pads", [128, 3, ROW], F32)
    route_w = sb("route_w", [128, DC, E], F32)
    route_whi = sb("route_whi", [128, DC, E], F16)
    route_wlo = sb("route_wlo", [128, DC, E], F16)
    route_bias = sb("route_bias", [S, E], F32)
    logits = sb("logits2", [S, E], F32)
    top8 = sb("top82", [S, 8], F32)
    top8_at = sb("top8_at2", [S, 8], U32)
    gap = sb("gap", [S, 1], F32)
    gap_exp = sb("gap_exp", [S, 1], F32)
    gap_sum = sb("gap_sum", [S, 1], F32)
    first_w = sb("first_w", [S, 1], F32)
    second_w = sb("second_w", [S, 1], F32)
    second = sb("second", [S, E], F32)

    names = """weights_in we_in ready0 share_ps share_rdy nb_rdy bs_rdy we_hi_rdy we_lo_rdy route_split consts
        ctxT_in0 ctxT_in1 rows_in0 rows_in1 mask_in0 mask_in1 passed
        ffn_done accT_done x2nT_done s1_done pT_done o_done x3nT_done route_done
        x2nT_rdy exp_rdy pT_rdy x3hi_rdy gexp_rdy
        acc_rdy x2_rdy st2 ag2 x2n_rdy masked_rdy eb_rdy inv_rdy x3_rdy st3 ag3 x3n_rdy x3lo_rdy
        lg_rdy top_rdy at_rdy gap_rdy gs_rdy fw_rdy sw_rdy c1_rdy c2_rdy c2w_rdy comb_rdy chosen_rdy rank_done pos_rdy pick_rdy slots_rdy
        cum_rdy token_rdy scattered0 scattered1 x3_out pads_in pads_out w_in0 w_in1 w_hi_rdy w_lo_rdy rows_set
        eps2 rs2 eps3 rs3 mask_rdy""".split()
    m = {n: sem("m_" + n) for n in names}
    ctxT_in, rows_in, mask_in = ([m[f"{k}{i}"] for i in range(2)] for k in ("ctxT_in", "rows_in", "mask_in"))
    scattered = [m["scattered0"], m["scattered1"]]
    LAG_ATT, LAG_OUT, LAG_ROUTE, LAG_SEND = 4, 5, 6, 7
    TURN = 2 * GB
    N_W = 6
    NEG = -1e9 * 16.0

    def cnt(t, u, per, extra):
        return t * (TURN * per) + (u * per + extra)

    def loads(t, u):
        return t * (16 * TURN // 2) + 16 * (u // 2 + 1)

    def apart(engine):
        engine.sem_inc(m["passed"], 1)

    def steps(engine, step):
        turns = B // TURN
        for u in range(TURN):
            step(0, u, (True, u >= LAG_ATT, u >= LAG_OUT, u >= LAG_ROUTE, u >= LAG_SEND))
        with engine.Fori(1, turns) as t:
            for u in range(TURN):
                step(t, u, (True,) * 5)
        for u in range(LAG_SEND):
            step(turns, u, (False, u < LAG_ATT, u < LAG_OUT, u < LAG_ROUTE, True))

    with nc.Block() as block:

        @block.sync
        def _(sp):
            for used in keep["attention_semaphores"]:
                sp.sem_clear(used)
            for e in range(E):
                sp.dma_start(we[:, :, e, :], dram["weT"].rearrange("(c p) e h -> p c e h", p=128)[:, :, e, :]).then_inc(m["we_in"], 16)
            sp.dma_start(expert_b[:], dram["expert_bT"].rearrange("(c p) e -> p c e", p=128)).then_inc(m["weights_in"], 16)
            sp.dma_start(route_w[:], dram["route_wT"].rearrange("(c p) e -> p c e", p=128)).then_inc(m["weights_in"], 16)
            sp.dma_start(route_bias[:], dram["route_b"].rearrange("(o n) -> o n", o=1).broadcast_to([S, E])).then_inc(m["weights_in"], 16)

            sp.dma_start(before[:], dram["before"]).then_inc(m["weights_in"], 16)
            sp.dma_start(slot_base[:], dram["slot_base"]).then_inc(m["weights_in"], 16)
            sp.dma_start(place[:], dram["place"]).then_inc(m["weights_in"], 16)
            sp.dma_start(pads[:], dram["pads"].rearrange("k p r -> p k r")).then_inc(m["pads_in"], 16)
            sp.wait_ge(m["pads_in"], 16)
            for n in range(2):
                sp.dma_start(dram["dispatch"][DUMMY + n * 128:DUMMY + (n + 1) * 128, :], pads[:, n, :]).then_inc(m["pads_out"], 16)
            for n in range(3):
                sp.dma_start(dram["out"][PAD_OUT + n * 128:PAD_OUT + (n + 1) * 128, :], pads[:, n, 0:D]).then_inc(m["pads_out"], 16)

            def store(t, u):
                b = t * TURN + u
                wait(sp, m["x3_rdy"], cnt(t, u, 1, 1))
                apart(sp)
                sp.dma_start(dram["out"][bass.ds(b * S, S), :], x_res[:, bass.ds(b, 1), :].rearrange("p o d -> p (o d)")).then_inc(m["x3_out"], 16)

            def load(t, u):
                b, p = t * TURN + u, u % 2
                wait(sp, m["w_lo_rdy"], cnt(t, u - 2, 1, 1))
                apart(sp)
                sp.dma_start(w_raw[:, p, :], dram["w12"][:, bass.ds(b * W_PIECE, W_PIECE)]).then_inc(m[f"w_in{p}"], 16)
                wait(sp, m["s1_done"], cnt(t, u - 2, 1, 1))
                apart(sp)
                sp.dma_start(ctxT[:, p, :, :], dram["ctxT"][bass.ds(b, 1), :, :].rearrange("o (c p) s -> p (o c) s", p=128)).then_inc(ctxT_in[p], 16)
                wait(sp, m["mask_rdy"], cnt(t, u - 2, 1, 1))
                apart(sp)
                sp.dma_start(mask[:, p, :], dram["mask"][bass.ds(b, 1), 0, :].broadcast_to([S, KV])).then_inc(mask_in[p], 16)
                wait(sp, m["o_done"], cnt(t, u - 2, 1, 1))
                apart(sp)
                sp.dma_start(ctx_rows[:, p, :, :], dram["ctx"][bass.ds(b, 1), :, :].rearrange("o (c p) d -> p (o c) d", p=KC)).then_inc(rows_in[p], 16)

            turns = B // TURN
            for u in range(TURN):
                load(0, u)
                if u >= 3:
                    store(0, u - 3)
            with sp.Fori(1, turns) as t:
                for u in range(TURN):
                    load(t, u)
                    store(t, u - 3)
            for u in range(3):
                store(turns, u - 3)
            sp.wait_ge(m["x3_out"], 16 * B)
            sp.wait_ge(m["pads_out"], 16 * 5)

        @block.gpsimd
        def _(pool):
            nc.gpsimd.memset(ones[:], 1.0).then_inc(m["consts"], 1)
            nc.gpsimd.memset(half[:], -0.5).then_inc(m["consts"], 1)
            nc.gpsimd.memset(rows[:], 0.0).then_inc(m["rows_set"], 1)
            pool.wait_ge(m["consts"], 2)
            pool.wait_ge(m["weights_in"], 16 * N_W)
            pool.wait_ge(m["rows_set"], 1)
            for n in range(2):
                nc.gpsimd.tensor_scalar(rows[:, n, AT_TOKEN:AT_TOKEN + 1], place[:], float((n - 2) * S), None, ALU.add).then_inc(m["rows_set"], 1)
            pool.wait_ge(m["rows_set"], 3)

            def rstd(agg, eps, rs, n, value):
                wait(pool, m[agg], value)
                apart(pool)
                nc.gpsimd.tensor_scalar(ln_var[:, n, :], ln_mv[:, n, 1:2], EPS, None, ALU.add).then_inc(m[eps], 1)
                wait(pool, m[eps], value)
                nc.gpsimd.tensor_tensor(ln_rstd[:, n, :], ln_var[:, n, :], half[:], ALU.pow).then_inc(m[rs], 1)

            def step(t, u, on):
                f, a, o, r, k = on
                if a:
                    rstd("ag2", "eps2", "rs2", 0, cnt(t, u - LAG_ATT, 1, 1))
                if r:
                    rstd("ag3", "eps3", "rs3", 1, cnt(t, u - LAG_ROUTE, 1, 1))
                if a:
                    p = (u - LAG_ATT) % 2
                    wait(pool, mask_in[p], loads(t, u - LAG_ATT))
                    wait(pool, m["masked_rdy"], cnt(t, u - LAG_ATT - 2, 1, 1))
                    apart(pool)
                    nc.gpsimd.tensor_scalar(mask_add[:, p, :], mask[:, p, :], NEG, 0.0, ALU.mult, ALU.add).then_inc(m["mask_rdy"], 1)
                if a:
                    ua = u - LAG_ATT
                    at = (t * TURN + ua) * W_PIECE
                    wait(pool, m["w_hi_rdy"], cnt(t, ua, 1, 1))
                    apart(pool)
                    nc.gpsimd.tensor_tensor(w_lo[:, bass.ds(at, W_PIECE)], w_raw[:, ua % 2, :], w_hi[:, bass.ds(at, W_PIECE)],
                                            ALU.subtract).then_inc(m["w_lo_rdy"], 1)
                if r:
                    ur = u - LAG_ROUTE
                    wait(pool, scattered[ur % 2], loads(t, ur - 2) * 2)
                    apart(pool)
                    nc.gpsimd.tensor_scalar(rows[:, ur % 2, AT_TOKEN:AT_TOKEN + 1], rows[:, ur % 2, AT_TOKEN:AT_TOKEN + 1],
                                            float(2 * S), None, ALU.add).then_inc(m["token_rdy"], 1)
                if k:
                    uk = u - LAG_SEND
                    wait(pool, m["slots_rdy"], cnt(t, uk, 1, 1))
                    wait(pool, m["comb_rdy"], cnt(t, uk, 1, 1))
                    wait(pool, m["token_rdy"], cnt(t, uk, 1, 1))
                    apart(pool)
                    for n in range(2):
                        nc.gpsimd.indirect_dma_start(dram["dispatch"], bass.IndirectOffsetOnAxis(slots_at[:, uk % 2, n:n + 1], 0),
                                                     rows[:, uk % 2, :], None).then_inc(scattered[uk % 2], 16)

            steps(pool, step)
            for n in range(2):
                pool.wait_ge(scattered[n], 16 * B)

        @block.tensor
        def _(pe):
            pe.wait_ge(m["consts"], 3)
            nc.tensor.matmul(psum[:, 0, 0:E], ones[:], gate_counts[:], start=True, stop=True).then_inc(m["share_ps"], 1)
            pe.wait_ge(m["route_split"], 2)
            pe.wait_ge(m["share_rdy"], 1)

            def mixture(t, u, k):
                e, hc = 2 * (u % GB) + k // 2, k % 2
                g0 = t * (2 * GT) + (u // GB) * GT
                if isinstance(t, int) and t == 0 and u < GB:
                    pe.wait_ge(m["we_lo_rdy"], e + 1)
                wait(pe, m["acc_rdy"], cnt(t, u, 4, k - 1))
                n = 0
                for w, x in ((we_hi, xT_hi), (we_hi, xT_lo), (we_lo, xT_hi)):
                    for kc in range(DC):
                        last = nc.tensor.matmul(psum[:, k % 2, 0:GT], w[:, kc, e, hc * 128:(hc + 1) * 128], x[:, kc, bass.ds(g0, GT)],
                                                start=(n == 0), stop=(n == 5))
                        n += 1
                last.then_inc(m["ffn_done"], 1)

            def step(t, u, on):
                f, a, o, r, k = on
                ua, uo, ur, uk = u - LAG_ATT, u - LAG_OUT, u - LAG_ROUTE, u - LAG_SEND

                def mix(n):
                    if f:
                        mixture(t, u, n)

                if a:
                    wait(pe, m["acc_rdy"], cnt(t, (ua // GB) * GB, 4, 4 * GB))
                    wait(pe, m["x2nT_rdy"], cnt(t, ua - 1, 1, 1))
                    for hc in range(DC):
                        last = nc.tensor.transpose(psum[0:S, 2, hc * 128:(hc + 1) * 128],
                                                   acc[:, (ua // GB) % 2, hc, (ua % GB) * S:(ua % GB + 1) * S], ident[:, :])
                    last.then_inc(m["accT_done"], 1)
                mix(0)
                mix(1)
                if o:
                    wait(pe, m["exp_rdy"], cnt(t, uo, 1, 1))
                    wait(pe, m["pT_rdy"], cnt(t, uo - 1, 1, 1))
                    for c in range(NKC):
                        last = nc.tensor.transpose(psum[0:KC, 5, c * S:(c + 1) * S], probs[:, c * KC:(c + 1) * KC], ident[0:S, 0:S])
                    last.then_inc(m["pT_done"], 1)
                mix(2)
                if a:
                    wait(pe, m["x2n_rdy"], cnt(t, ua, 1, 1))
                    for kc in range(DC):
                        last = nc.tensor.transpose(psum[:, 2, D + kc * S:D + (kc + 1) * S], x2n[:, kc * 128:(kc + 1) * 128], ident[0:S, 0:S])
                    last.then_inc(m["x2nT_done"], 1)
                if o:
                    wait(pe, rows_in[uo % 2], loads(t, uo))
                    wait(pe, m["pT_rdy"], cnt(t, uo, 1, 1))
                    wait(pe, m["x3_rdy"], cnt(t, uo - 1, 1, 1))
                    for c in range(NKC):
                        last = nc.tensor.matmul(psum[0:S, 6, 0:D], probsT[:, c, :], ctx_rows[:, uo % 2, c, :], start=(c == 0), stop=(c == NKC - 1))
                    last.then_inc(m["o_done"], 1)
                mix(3)
                if r:
                    wait(pe, m["x3n_rdy"], cnt(t, ur, 1, 1))
                    wait(pe, m["lg_rdy"], cnt(t, ur - 1, 1, 1))
                    for kc in range(DC):
                        last = nc.tensor.transpose(psum[:, 7, kc * S:(kc + 1) * S], rows[:, ur % 2, kc * 128:(kc + 1) * 128], ident[0:S, 0:S])
                    last.then_inc(m["x3nT_done"], 1)
                if k:
                    wait(pe, m["chosen_rdy"], cnt(t, uk, 1, 1))
                    wait(pe, m["cum_rdy"], cnt(t, uk - 1, 1, 1))
                    nc.tensor.matmul(psum[0:S, 3, 0:E], before[:], chosen[:], start=True, stop=False)
                    nc.tensor.matmul(psum[0:S, 3, 0:E], ones[:, 0:S], cum[:], start=False, stop=True).then_inc(m["rank_done"], 1)
                if a:
                    wait(pe, ctxT_in[ua % 2], loads(t, ua))
                    wait(pe, m["x2nT_rdy"], cnt(t, ua, 1, 1))
                    wait(pe, m["masked_rdy"], cnt(t, ua - 1, 1, 1))
                    for kc in range(DC):
                        last = nc.tensor.matmul(psum[0:S, 4, 0:KV], x2nT[:, kc, :], ctxT[:, ua % 2, kc, :], start=(kc == 0), stop=(kc == DC - 1))
                    last.then_inc(m["s1_done"], 1)
                if r:
                    wait(pe, m["x3lo_rdy"], cnt(t, ur, 1, 1))
                    b0 = (t * TURN + ur) * S
                    n = 0
                    for left, right in ((xT_hi, route_whi), (xT_hi, route_wlo), (xT_lo, route_whi)):
                        for kc in range(DC):
                            last = nc.tensor.matmul(psum[0:S, 7, DC * S:DC * S + E], left[:, kc, bass.ds(b0, S)], right[:, kc, :], start=(n == 0), stop=(n == 5))
                            n += 1
                    last.then_inc(m["route_done"], 1)

            steps(pe, step)

        @block.scalar
        def _(act):
            act.wait_ge(m["share_ps"], 1)
            nc.scalar.activation(share[:], psum[:, 0, 0:E], ACT.Copy, scale=1.0 / (2 * B * S)).then_inc(m["share_rdy"], 1)
            act.wait_ge(m["share_rdy"], 1)
            act.wait_ge(m["we_in"], 16 * E)
            for e in range(E):
                nc.scalar.activation(we_hi[:, :, e, :], we[:, :, e, :], ACT.Copy, scale=share[:, e:e + 1]).then_inc(m["we_hi_rdy"], 1)

            def step(t, u, on):
                f, a, o, r, k = on
                ua, uo, ur, uk = u - LAG_ATT, u - LAG_OUT, u - LAG_ROUTE, u - LAG_SEND
                if o:
                    wait(act, m["eb_rdy"], cnt(t, uo, 1, 1))
                    wait(act, m["pT_done"], cnt(t, uo - 1, 1, 1))
                    nc.scalar.activation(probs[:], masked[:], ACT.Exp, bias=exp_bias[:], scale=float(D) ** -0.5,
                                         accum_out=prob_sum[:, uo % 2, :]).then_inc(m["exp_rdy"], 1)
                if o:
                    wait(act, m["pT_done"], cnt(t, uo, 1, 1))
                    wait(act, m["o_done"], cnt(t, uo - 1, 1, 1))
                    nc.scalar.activation(probsT[:].rearrange("p c s -> p (c s)"), psum[0:KC, 5, 0:NKC * S], ACT.Copy).then_inc(m["pT_rdy"], 1)
                if a:
                    wait(act, m["x2nT_done"], cnt(t, ua, 1, 1))
                    wait(act, m["s1_done"], cnt(t, ua - 1, 1, 1))
                    nc.scalar.activation(x2nT[:].rearrange("p c s -> p (c s)"), psum[:, 2, D:D + DC * S], ACT.Copy).then_inc(m["x2nT_rdy"], 1)
                if k:
                    wait(act, m["gap_rdy"], cnt(t, uk, 1, 1))
                    nc.scalar.activation(gap_exp[:], gap[:], ACT.Exp).then_inc(m["gexp_rdy"], 1)
                if a:
                    wait(act, m[f"w_in{ua % 2}"], loads(t, ua))
                    apart(act)
                    nc.scalar.activation(w_hi[:, bass.ds((t * TURN + ua) * W_PIECE, W_PIECE)], w_raw[:, ua % 2, :], ACT.Copy).then_inc(m["w_hi_rdy"], 1)
                if r:
                    b0 = (t * TURN + ur) * S
                    wait(act, m["x3nT_done"], cnt(t, ur, 1, 1))
                    nc.scalar.activation(xT_hi[:, :, bass.ds(b0, S)], psum[:, 7, 0:DC * S].rearrange("p (c s) -> p c s", c=DC), ACT.Copy).then_inc(m["x3hi_rdy"], 1)

            steps(act, step)

        @block.vector
        def _(dve):
            dve.wait_ge(m["weights_in"], 16 * N_W)
            nc.vector.memset(cum[:], 0.0).then_inc(m["consts"], 1)
            nc.vector.tensor_copy(route_whi[:], route_w[:]).then_inc(m["route_split"], 1)
            dve.wait_ge(m["route_split"], 1)
            nc.vector.tensor_tensor(route_wlo[:], route_w[:], route_whi[:], ALU.subtract).then_inc(m["route_split"], 1)
            dve.wait_ge(m["share_rdy"], 1)
            nc.vector.scalar_tensor_tensor(neg_bias[:], expert_b[:], -1.0, share[:].rearrange("p (o e) -> p o e", o=1).broadcast_to([128, DC, E]),
                                           ALU.mult, ALU.mult).then_inc(m["nb_rdy"], 1)
            dve.wait_ge(m["nb_rdy"], 1)
            nc.vector.tensor_reduce(bias_sum[:], neg_bias[:], AX.X, ALU.add, negate=True).then_inc(m["bs_rdy"], 1)
            for e in range(E):
                dve.wait_ge(m["we_hi_rdy"], e + 1)
                nc.vector.scalar_tensor_tensor(we_lo[:, :, e, :], we[:, :, e, :], share[:, e:e + 1], we_hi[:, :, e, :],
                                               ALU.mult, ALU.subtract).then_inc(m["we_lo_rdy"], 1)
            dve.wait_ge(m["bs_rdy"], 1)

            def mix(t, u, k):
                e, hc = 2 * (u % GB) + k // 2, k % 2
                out = acc[:, u // GB, hc, :]
                wait(dve, m["ffn_done"], cnt(t, u, 4, k + 1))
                if e == 0:
                    wait(dve, m["accT_done"], cnt(t, u - GB - 1, 1, 1))
                    nc.vector.tensor_scalar(out, psum[:, k % 2, 0:GT], neg_bias[:, hc, 0:1], bias_sum[:, hc:hc + 1],
                                            ALU.max, ALU.add).then_inc(m["acc_rdy"], 1)
                else:
                    wait(dve, m["acc_rdy"], cnt(t, u, 4, k - 1))
                    nc.vector.scalar_tensor_tensor(out, psum[:, k % 2, 0:GT], neg_bias[:, hc, e:e + 1], out,
                                                   ALU.max, ALU.add).then_inc(m["acc_rdy"], 1)

            def step(t, u, on):
                f, a, o, r, k = on
                ua, uo, ur, uk = u - LAG_ATT, u - LAG_OUT, u - LAG_ROUTE, u - LAG_SEND
                xrow = lambda uu: x_res[:, bass.ds(t * TURN + uu, 1), :].rearrange("p o d -> p (o d)")

                def norm_stats(x, n, st, ag, value):
                    apart(dve)
                    nc.vector.bn_stats(ln_stats[:, n, :], x).then_inc(m[st], 1)
                    wait(dve, m[st], value)
                    apart(dve)
                    nc.vector.bn_aggr(ln_mv[:, n, :], ln_stats[:, n, :]).then_inc(m[ag], 1)

                if o:
                    v = cnt(t, uo, 1, 1)
                    wait(dve, m["s1_done"], v)
                    wait(dve, m["mask_rdy"], v)
                    wait(dve, m["exp_rdy"], cnt(t, uo - 1, 1, 1))
                    apart(dve)
                    nc.vector.tensor_tensor_reduce(out=masked[:], in0=psum[0:S, 4, 0:KV], in1=mask_add[:, uo % 2, :], scale=1.0, scalar=-3.0e38,
                                                   op0=ALU.add, op1=ALU.max, accum_out=row_max[:]).then_inc(m["masked_rdy"], 1)
                    wait(dve, m["masked_rdy"], v)
                    nc.vector.tensor_scalar(exp_bias[:], row_max[:], -float(D) ** -0.5, None, ALU.mult).then_inc(m["eb_rdy"], 1)
                if a:
                    v = cnt(t, ua, 1, 1)
                    wait(dve, m["accT_done"], v)
                    nc.vector.tensor_tensor(xrow(ua), psum[0:S, 2, 0:D], xrow(ua), ALU.add).then_inc(m["x2_rdy"], 1)
                    wait(dve, m["x2_rdy"], v)
                    norm_stats(xrow(ua), 0, "st2", "ag2", v)
                if f:
                    mix(t, u, 0)
                if r:
                    v = cnt(t, ur, 1, 1)
                    wait(dve, m["x3_rdy"], v)
                    norm_stats(xrow(ur), 1, "st3", "ag3", v)
                if a:
                    v = cnt(t, ua, 1, 1)
                    wait(dve, m["rs2"], v)
                    wait(dve, m["x2nT_done"], cnt(t, ua - 1, 1, 1))
                    nc.vector.tensor_scalar(x2n[:], xrow(ua), ln_mv[:, 0, 0:1], ln_rstd[:, 0, :], ALU.subtract, ALU.mult).then_inc(m["x2n_rdy"], 1)
                if k:
                    v = cnt(t, uk, 1, 1)
                    wait(dve, m["route_done"], v)
                    nc.vector.tensor_tensor(logits[:], psum[0:S, 7, DC * S:DC * S + E], route_bias[:], ALU.add).then_inc(m["lg_rdy"], 1)
                    wait(dve, m["lg_rdy"], v)
                    apart(dve)
                    nc.vector.max(top8[:], logits[:]).then_inc(m["top_rdy"], 1)
                    wait(dve, m["top_rdy"], v)
                    wait(dve, m["gexp_rdy"], cnt(t, uk - 1, 1, 1))
                    nc.vector.tensor_tensor(gap[:], top8[:, 1:2], top8[:, 0:1], ALU.subtract).then_inc(m["gap_rdy"], 1)
                    apart(dve)
                    nc.vector.max_index(top8_at[:], top8[:], logits[:]).then_inc(m["at_rdy"], 1)
                if f:
                    mix(t, u, 1)
                if k:
                    v = cnt(t, uk, 1, 1)
                    wait(dve, m["at_rdy"], v)
                    nc.vector.tensor_scalar(first[:], iota[:], top8_at[:, 0:1], None, ALU.is_equal).then_inc(m["c1_rdy"], 1)
                    nc.vector.tensor_scalar(second[:], iota[:], top8_at[:, 1:2], None, ALU.is_equal).then_inc(m["c2_rdy"], 1)
                    wait(dve, m["c2_rdy"], v)
                    nc.vector.tensor_tensor(chosen[:], first[:], second[:], ALU.add).then_inc(m["chosen_rdy"], 1)
                if r:
                    v = cnt(t, ur, 1, 1)
                    wait(dve, m["rs3"], v)
                    wait(dve, m["x3nT_done"], cnt(t, ur - 1, 1, 1))
                    wait(dve, scattered[ur % 2], loads(t, ur - 2) * 2)
                    nc.vector.tensor_scalar(rows[:, ur % 2, 0:D], xrow(ur), ln_mv[:, 1, 0:1], ln_rstd[:, 1, :], ALU.subtract, ALU.mult).then_inc(m["x3n_rdy"], 1)
                if f:
                    mix(t, u, 2)
                if k:
                    v = cnt(t, uk, 1, 1)
                    wait(dve, m["gexp_rdy"], v)
                    nc.vector.tensor_scalar(gap_sum[:], gap_exp[:], 1.0, None, ALU.add).then_inc(m["gs_rdy"], 1)
                if o:
                    v = cnt(t, uo, 1, 1)
                    wait(dve, m["exp_rdy"], v)
                    nc.vector.reciprocal(inv_sum[:], prob_sum[:, uo % 2, :]).then_inc(m["inv_rdy"], 1)
                if k:
                    wait(dve, m["gs_rdy"], cnt(t, uk, 1, 1))
                    nc.vector.reciprocal(first_w[:], gap_sum[:]).then_inc(m["fw_rdy"], 1)
                if o:
                    v = cnt(t, uo, 1, 1)
                    wait(dve, m["inv_rdy"], v)
                    wait(dve, m["o_done"], v)
                    nc.vector.scalar_tensor_tensor(xrow(uo), psum[0:S, 6, 0:D], inv_sum[:], xrow(uo), ALU.mult, ALU.add).then_inc(m["x3_rdy"], 1)
                if k:
                    wait(dve, m["fw_rdy"], cnt(t, uk, 1, 1))
                    nc.vector.tensor_tensor(second_w[:], gap_exp[:], first_w[:], ALU.mult).then_inc(m["sw_rdy"], 1)
                if f:
                    mix(t, u, 3)
                if k:
                    wait(dve, m["sw_rdy"], cnt(t, uk, 1, 1))
                    nc.vector.tensor_scalar(second_row[:], second[:], second_w[:], None, ALU.mult).then_inc(m["c2w_rdy"], 1)
                if r:
                    v = cnt(t, ur, 1, 1)
                    b0 = (t * TURN + ur) * S
                    wait(dve, m["x3hi_rdy"], v)
                    nc.vector.tensor_tensor(xT_lo[:, :, bass.ds(b0, S)], psum[:, 7, 0:DC * S].rearrange("p (c s) -> p c s", c=DC),
                                            xT_hi[:, :, bass.ds(b0, S)], ALU.subtract).then_inc(m["x3lo_rdy"], 1)
                if k:
                    v = cnt(t, uk, 1, 1)
                    wait(dve, m["c2w_rdy"], v)
                    nc.vector.scalar_tensor_tensor(rows[:, uk % 2, AT_W:AT_W + E], first[:], first_w[:], second_row[:],
                                                   ALU.mult, ALU.add).then_inc(m["comb_rdy"], 1)
                    wait(dve, m["rank_done"], v)
                    nc.vector.tensor_tensor(slot_of[:], psum[0:S, 3, 0:E], slot_base[:], ALU.add).then_inc(m["pos_rdy"], 1)
                    nc.vector.tensor_tensor(cum[:], cum[:], chosen[:], ALU.add).then_inc(m["cum_rdy"], 1)
                    wait(dve, m["pos_rdy"], v)
                    nc.vector.tensor_tensor(picked[:, 0, :], slot_of[:], first[:], ALU.mult).then_inc(m["pick_rdy"], 1)
                    nc.vector.tensor_tensor(picked[:, 1, :], slot_of[:], second[:], ALU.mult).then_inc(m["pick_rdy"], 1)
                    wait(dve, m["pick_rdy"], cnt(t, uk, 3, 2))
                    nc.vector.tensor_reduce(slots[:], picked[:], AX.X, ALU.add).then_inc(m["pick_rdy"], 1)
                    wait(dve, m["pick_rdy"], cnt(t, uk, 3, 3))
                    nc.vector.tensor_copy(slots_at[:, uk % 2, :], slots[:]).then_inc(m["slots_rdy"], 1)

            steps(dve, step)


def expert_phase(nc, ctx, dram, keep):
    def sb(name, shape, dt):
        return ctx.enter_context(nc.sbuf_tensor(name, shape, dt))

    def sem(name):
        return ctx.enter_context(nc.semaphore(name))

    ident, psum, cum = keep["ident"], keep["psum"], keep["cum"]
    w1_cols = E * DC * HID
    w1_hi, w1_lo = (w[:, 0:w1_cols].rearrange("p (e c h) -> p e c h", e=E, c=DC) for w in (keep["w_hi"], keep["w_lo"]))
    w2_hi, w2_lo = (w[:, w1_cols:W_COLS].rearrange("p (e c d) -> p e c d", e=E, c=HC) for w in (keep["w_hi"], keep["w_lo"]))
    TILES_MAX = TOKENS // TILE
    HALF = TILE // 128

    b1 = sb("b1", [128, HC, E], F32)
    b2 = sb("b2", [128, E, D], F32)
    ones = sb("ones_e", [S, 128], F32)
    counts = sb("counts", [128, E], F32)
    pad_place = sb("pad_place", [128, E], F32)
    pad_at = sb("pad_at", [128, E], U32)
    pad_rows = sb("pad_rows", [128, ROW], F32)
    edges = sb("edges", [1, E, TILES_MAX], F32)
    over = sb("over", [1, E, TILES_MAX], F32)
    tiles_of = sb("tiles_of", [1, E], F32)
    upto = sb("upto", [1, E, E], F32)
    upto_tiles = sb("upto_tiles", [1, E, E], F32)
    ends = sb("ends", [1, E], F32)
    tile_no = sb("tile_no", [1, NT], F32)
    expert_no = sb("expert_no", [1, E], F32)
    passed_by = sb("passed_by", [1, NT, E], F32)
    part = sb("part", [1, 2, NT, E], F32)
    expert = sb("expert", [1, NT], F32)
    start = sb("start", [1, NT], F32)
    within = sb("within", [1, NT], F32)
    members = sb("members", [1, NT], F32)
    has = sb("has", [1, 2, NT], F32)
    row_of = sb("row_of", [1, 2, NT], F32)
    table = sb("table", [1, 3, NT], U32)
    rows = sb("rows_e", [128, 2, HALF, ROW], F32)
    meta = sb("meta", [128, 2, HALF, E + 1], F32)
    weight = sb("weight", [128, 2, HALF], F32)
    token_at = sb("token_at", [128, 2, HALF], U32)
    x_hi = sb("x_hi", [128, 2, DC, TILE], F16)
    x_lo = sb("x_lo", [128, 2, DC, TILE], F16)
    h = sb("h", [128, HC, TILE], F32)
    h_hi = sb("h_hi", [128, 2, HC, TILE], F16)
    h_lo = sb("h_lo", [128, 2, HC, TILE], F16)
    y_sum = sb("y_sum", [128, HALF, D], F32)
    y = sb("y", [128, 2, HALF, D], F32)

    names = """const_in ones_set counted counts_rdy pad_at_rdy pads_sent table table_done passed
        rows_in0 rows_in1 xT_done xhi_rdy xlo_rdy up_done h_rdy hhi_rdy hlo_rdy down_done y_sum_rdy y_rdy meta_rdy weight_rdy token_rdy
        added""".split()
    m = {n: sem("x_" + n) for n in names}
    rows_in = [m["rows_in0"], m["rows_in1"]]
    N_CONST = 8

    def cnt(t, u, per, extra):
        return t * (2 * per) + (u * per + extra)

    def apart(engine):
        engine.sem_inc(m["passed"], 1)

    def look_up(engine, what, t, u, most):
        return engine.value_load(table[0:1, what, bass.ds(t * 2 + u, 1)], min_val=0, max_val=most)

    def steps(engine, step):
        for t in range(2):
            for u in range(2):
                step(t, u, True, t + u > 0)
        with engine.Fori(2, NT // 2) as t:
            for u in range(2):
                step(t, u, True, True)
        for n in range(NT // 2 * 2, NT + 1):
            step(n // 2, n % 2, n < NT, True)

    with nc.Block() as block:

        @block.sync
        def _(sp):
            sp.dma_start(b1[:], dram["b1T"].rearrange("(c p) e -> p c e", p=128)).then_inc(m["const_in"], 16)
            sp.dma_start(b2[:], dram["b2"].rearrange("(o e) d -> o e d", o=1).broadcast_to([128, E, D])).then_inc(m["const_in"], 16)
            sp.dma_start(pad_place[:], dram["pad_place"]).then_inc(m["const_in"], 16)
            sp.dma_start(pad_rows[:], dram["pads"][2]).then_inc(m["const_in"], 16)
            sp.dma_start(edges[:], dram["edges"]).then_inc(m["const_in"], 16)
            sp.dma_start(upto[:], dram["upto"]).then_inc(m["const_in"], 16)
            sp.dma_start(tile_no[:], dram["tile_no"]).then_inc(m["const_in"], 16)
            sp.dma_start(expert_no[:], dram["iota"][0:1, :]).then_inc(m["const_in"], 16)
            sp.wait_ge(m["table_done"], 1)
            sp.wait_ge(m["pads_sent"], 16 * E)

            def step(t, u, up, down):
                if not up:
                    return
                row = [look_up(sp, 1 + n, t, u, DISPATCH_ROWS - 128) for n in range(HALF)]
                wait(sp, m["xT_done"], cnt(t, u - 2, 1, 1))
                apart(sp)
                wait(sp, m["meta_rdy"], cnt(t, u - 2, 1, 1))
                apart(sp)
                for n in range(HALF):
                    sp.dma_start(rows[:, u, n, :], dram["dispatch"][bass.ds(row[n], 128), :]).then_inc(rows_in[u], 16)

            steps(sp, step)

        @block.gpsimd
        def _(pool):
            nc.gpsimd.memset(ones[:], 1.0).then_inc(m["ones_set"], 1)
            pool.wait_ge(m["const_in"], 16 * N_CONST)
            pool.wait_ge(m["pad_at_rdy"], 1)
            for e in range(E):
                nc.gpsimd.indirect_dma_start(dram["dispatch"], bass.IndirectOffsetOnAxis(pad_at[:, e:e + 1], 0),
                                             pad_rows[:], None).then_inc(m["pads_sent"], 16)

            def step(t, u, up, down):
                if not down:
                    return
                p = (u - 1) % 2
                wait(pool, m["y_rdy"], cnt(t, u - 1, HALF, HALF))
                wait(pool, m["added"], cnt(t, u - 2, 16 * HALF, 16 * HALF))
                apart(pool)
                for n in range(HALF):
                    nc.gpsimd.indirect_dma_start(dram["out"], bass.IndirectOffsetOnAxis(token_at[:, p, n:n + 1], 0), y[:, p, n, :], None,
                                                 compute_op=ALU.add).then_inc(m["added"], 16)

            steps(pool, step)
            pool.wait_ge(m["added"], 16 * HALF * NT)

        @block.tensor
        def _(pe):
            pe.wait_ge(m["ones_set"], 1)
            nc.tensor.matmul(psum[:, 0, 0:E], ones[:], cum[:], start=True, stop=True).then_inc(m["counted"], 1)
            pe.wait_ge(m["counts_rdy"], 1)
            pe.wait_ge(m["table_done"], 1)

            def turn_rows(t, u):
                p = u % 2
                wait(pe, rows_in[p], t * (16 * HALF) + 16 * HALF * (u // 2 + 1))
                wait(pe, m["xlo_rdy"], cnt(t, u - 1, 1, 1))
                for kc in range(DC):
                    for n in range(HALF):
                        last = nc.tensor.transpose(psum[:, 0, kc * TILE + n * 128:kc * TILE + (n + 1) * 128],
                                                   rows[:, p, n, kc * 128:(kc + 1) * 128], ident[:, :])
                last.then_inc(m["xT_done"], 1)

            turn_rows(0, 0)

            def step(t, u, up, down):
                p, q = u % 2, (u - 1) % 2
                more = up and not (isinstance(t, int) and 2 * t + u == NT - 1)
                if up:
                    e = look_up(pe, 0, t, u, E - 1)
                    wait(pe, m["xlo_rdy"], cnt(t, u, 1, 1))
                    for c in range(HC):
                        if c % 2 == 0:
                            wait(pe, m["h_rdy"], cnt(t, u - 1, HC, c + 2))
                            apart(pe)
                        n = 0
                        for w, x in ((w1_hi, x_hi), (w1_hi, x_lo), (w1_lo, x_hi)):
                            for kc in range(DC):
                                last = nc.tensor.matmul(psum[:, 1 + c // 2, (c % 2) * TILE:(c % 2 + 1) * TILE],
                                                        w[:, bass.ds(e, 1), kc, c * 128:(c + 1) * 128].rearrange("p o h -> p (o h)"),
                                                        x[:, p, kc, :], start=(n == 0), stop=(n == 5))
                                n += 1
                        if c % 2 == 1:
                            last.then_inc(m["up_done"], 1)
                if more:
                    turn_rows(t, u + 1)
                if down:
                    e = look_up(pe, 0, t, u - 1, E - 1)
                    wait(pe, m["hlo_rdy"], cnt(t, u - 1, 2, 2))
                    for s in range(HALF):
                        wait(pe, m["y_sum_rdy"], cnt(t, u - 2, HALF, s + 1))
                        n = 0
                        for hh, w in ((h_hi, w2_hi), (h_hi, w2_lo), (h_lo, w2_hi)):
                            for kc in range(HC):
                                last = nc.tensor.matmul(psum[:, 3 + s, 0:D], hh[:, q, kc, s * 128:(s + 1) * 128],
                                                        w[:, bass.ds(e, 1), kc, :].rearrange("p o d -> p (o d)"), start=(n == 0), stop=(n == 11))
                                n += 1
                        last.then_inc(m["down_done"], 1)

            steps(pe, step)

        @block.scalar
        def _(act):
            act.wait_ge(m["const_in"], 16 * N_CONST)
            act.wait_ge(m["table_done"], 1)

            def high_x(t, u):
                p = u % 2
                wait(act, m["xT_done"], cnt(t, u, 1, 1))
                wait(act, m["up_done"], cnt(t, u - 2, 2, 2))
                nc.scalar.activation(x_hi[:, p, :, :].rearrange("p c s -> p (c s)"), psum[:, 0, 0:DC * TILE], ACT.Copy).then_inc(m["xhi_rdy"], 1)

            high_x(0, 0)

            def step(t, u, up, down):
                if not up:
                    return
                p = u % 2
                more = not (isinstance(t, int) and 2 * t + u == NT - 1)
                e = look_up(act, 0, t, u, E - 1)
                for c in range(HC):
                    if c % 2 == 0:
                        wait(act, m["up_done"], cnt(t, u, 2, c // 2 + 1))
                        wait(act, m["hlo_rdy"], cnt(t, u - 1, 2, c // 2 + 1))
                        apart(act)
                    nc.scalar.activation(h[:, c, :], psum[:, 1 + c // 2, (c % 2) * TILE:(c % 2 + 1) * TILE], ACT.Relu,
                                         bias=b1[:, c, bass.ds(e, 1)]).then_inc(m["h_rdy"], 1)
                if more:
                    high_x(t, u + 1)
                wait(act, m["down_done"], cnt(t, u - 2, HALF, HALF))
                for k in range(2):
                    wait(act, m["h_rdy"], cnt(t, u, HC, 2 * k + 2))
                    nc.scalar.activation(h_hi[:, p, 2 * k:2 * k + 2, :], h[:, 2 * k:2 * k + 2, :], ACT.Copy).then_inc(m["hhi_rdy"], 1)

            steps(act, step)

        @block.vector
        def _(dve):
            dve.wait_ge(m["const_in"], 16 * N_CONST)
            dve.wait_ge(m["counted"], 1)
            nc.vector.tensor_copy(counts[:], psum[:, 0, 0:E]).then_inc(m["counts_rdy"], 1)
            dve.wait_ge(m["counts_rdy"], 1)
            nc.vector.tensor_tensor(pad_at[:], counts[:], pad_place[:], ALU.add).then_inc(m["pad_at_rdy"], 1)

            one = counts[0:1, :]
            across = lambda a, n: a.rearrange("o (n e) -> o n e", n=1).broadcast_to([1, n, E])
            nc.vector.tensor_tensor(over[:], one.rearrange("o (e n) -> o e n", n=1).broadcast_to([1, E, TILES_MAX]), edges[:], ALU.is_gt).then_inc(m["table"], 1)
            dve.wait_ge(m["table"], 1)
            nc.vector.tensor_reduce(tiles_of[:], over[:], AX.X, ALU.add).then_inc(m["table"], 1)
            dve.wait_ge(m["table"], 2)
            nc.vector.tensor_tensor(upto_tiles[:], upto[:], across(tiles_of[:], E), ALU.mult).then_inc(m["table"], 1)
            dve.wait_ge(m["table"], 3)
            nc.vector.tensor_reduce(ends[:], upto_tiles[:], AX.X, ALU.add).then_inc(m["table"], 1)
            along = lambda a: a.rearrange("o (n e) -> o n e", e=1).broadcast_to([1, NT, E])
            dve.wait_ge(m["table"], 4)
            nc.vector.tensor_tensor(passed_by[:], across(ends[:], NT), along(tile_no[:]), ALU.is_le).then_inc(m["table"], 1)
            dve.wait_ge(m["table"], 5)
            nc.vector.tensor_reduce(expert[:], passed_by[:], AX.X, ALU.add).then_inc(m["table"], 1)
            nc.vector.tensor_tensor(part[:, 0, :, :], passed_by[:], across(tiles_of[:], NT), ALU.mult).then_inc(m["table"], 1)
            dve.wait_ge(m["table"], 7)
            nc.vector.tensor_reduce(start[:], part[:, 0, :, :], AX.X, ALU.add).then_inc(m["table"], 1)
            nc.vector.tensor_tensor(part[:, 1, :, :], along(expert[:]), across(expert_no[:], NT), ALU.is_equal).then_inc(m["table"], 1)
            dve.wait_ge(m["table"], 9)
            nc.vector.tensor_tensor(within[:], tile_no[:], start[:], ALU.subtract).then_inc(m["table"], 1)
            nc.vector.tensor_tensor(passed_by[:], part[:, 1, :, :], across(one, NT), ALU.mult).then_inc(m["table"], 1)
            dve.wait_ge(m["table"], 11)
            nc.vector.tensor_scalar(within[:], within[:], float(TILE), None, ALU.mult).then_inc(m["table"], 1)
            nc.vector.tensor_reduce(members[:], passed_by[:], AX.X, ALU.add).then_inc(m["table"], 1)
            dve.wait_ge(m["table"], 13)
            nc.vector.tensor_tensor(has[:, 0, :], members[:], within[:], ALU.is_gt).then_inc(m["table"], 1)
            nc.vector.scalar_tensor_tensor(has[:, 1, :], members[:], -128.0, within[:], ALU.add, ALU.is_gt).then_inc(m["table"], 1)
            nc.vector.scalar_tensor_tensor(row_of[:, 0, :], expert[:], float(CAP), within[:], ALU.mult, ALU.add).then_inc(m["table"], 1)
            dve.wait_ge(m["table"], 16)
            nc.vector.tensor_scalar(row_of[:, 0, :], row_of[:, 0, :], float(-DUMMY), None, ALU.add).then_inc(m["table"], 1)
            dve.wait_ge(m["table"], 17)
            for n in range(HALF):
                nc.vector.tensor_tensor(has[:, n, :], has[:, n, :], row_of[:, 0, :], ALU.mult).then_inc(m["table"], 1)
            dve.wait_ge(m["table"], 19)
            for n in range(HALF):
                nc.vector.tensor_scalar(row_of[:, n, :], has[:, n, :], float(DUMMY + n * 128), None, ALU.add).then_inc(m["table"], 1)
            nc.vector.tensor_scalar(expert[:], expert[:], float(E - 1), None, ALU.min).then_inc(m["table"], 1)
            dve.wait_ge(m["table"], 22)
            nc.vector.tensor_copy(table[:, 0, :], expert[:]).then_inc(m["table"], 1)
            nc.vector.tensor_copy(table[:, 1:3, :], row_of[:]).then_inc(m["table"], 1)
            dve.wait_ge(m["table"], 24)
            dve.sem_inc(m["table_done"], 1)

            def low_x(t, u):
                p = u % 2
                wait(dve, m["xhi_rdy"], cnt(t, u, 1, 1))
                nc.vector.tensor_tensor(x_lo[:, p, :, :].rearrange("p c s -> p (c s)"), psum[:, 0, 0:DC * TILE],
                                        x_hi[:, p, :, :].rearrange("p c s -> p (c s)"), ALU.subtract).then_inc(m["xlo_rdy"], 1)

            low_x(0, 0)

            def step(t, u, up, down):
                p, q = u % 2, (u - 1) % 2
                more = up and not (isinstance(t, int) and 2 * t + u == NT - 1)
                if up:
                    wait(dve, rows_in[p], t * (16 * HALF) + 16 * HALF)
                    nc.vector.tensor_copy(meta[:, p, :, :], rows[:, p, :, AT_W:AT_TOKEN + 1]).then_inc(m["meta_rdy"], 1)
                if more:
                    low_x(t, u + 1)
                if up:
                    for k in range(2):
                        wait(dve, m["hhi_rdy"], cnt(t, u, 2, k + 1))
                        nc.vector.tensor_tensor(h_lo[:, p, 2 * k:2 * k + 2, :], h[:, 2 * k:2 * k + 2, :], h_hi[:, p, 2 * k:2 * k + 2, :],
                                                ALU.subtract).then_inc(m["hlo_rdy"], 1)
                if down:
                    e = look_up(dve, 0, t, u - 1, E - 1)
                    for n in range(HALF):
                        wait(dve, m["down_done"], cnt(t, u - 1, HALF, n + 1))
                        nc.vector.tensor_tensor(y_sum[:, n, :], psum[:, 3 + n, 0:D], b2[:, bass.ds(e, 1), :].rearrange("p o d -> p (o d)"),
                                                ALU.add).then_inc(m["y_sum_rdy"], 1)
                        wait(dve, m["y_sum_rdy"], cnt(t, u - 1, HALF, n + 1))
                        wait(dve, m["weight_rdy"], cnt(t, u - 1, 1, 1))
                        wait(dve, m["added"], cnt(t, u - 3, 16 * HALF, 16 * HALF))
                        nc.vector.tensor_scalar(y[:, q, n, :], y_sum[:, n, :], weight[:, q, n:n + 1], None, ALU.mult).then_inc(m["y_rdy"], 1)
                if up:
                    e = look_up(dve, 0, t, u, E - 1)
                    wait(dve, m["meta_rdy"], cnt(t, u, 1, 1))
                    nc.vector.tensor_copy(weight[:, p, :].rearrange("p (n o) -> p n o", o=1), meta[:, p, :, bass.ds(e, 1)]).then_inc(m["weight_rdy"], 1)
                    wait(dve, m["added"], cnt(t, u - 2, 16 * HALF, 16 * HALF))
                    nc.vector.tensor_copy(token_at[:, p, :].rearrange("p (n o) -> p n o", o=1), meta[:, p, :, E:E + 1]).then_inc(m["token_rdy"], 1)

            steps(dve, step)


def build(nc, dram):
    with ExitStack() as ctx:
        def sb(name, shape, dt):
            return ctx.enter_context(nc.sbuf_tensor(name, shape, dt))

        keep = {
            "x_res": sb("x_res", [S, B, D], F32),
            "xT_hi": sb("xT_hi", [128, DC, B * S], F16),
            "xT_lo": sb("xT_lo", [128, DC, B * S], F16),
            "gate_counts": sb("gate_counts", [S, E], F32),
            "cum": sb("cum", [S, E], F32),
            "ident": sb("ident", [128, 128], F32),
            "iota": sb("iota", [S, E], F32),
            "psum": ctx.enter_context(nc.psum_tensor("psum", [128, 8, 512], F32)),
        }
        with ExitStack() as scope:
            attention_phase(nc, scope, dram, keep)
        keep["w_hi"] = sb("w_hi", [128, W_COLS], F16)
        keep["w_lo"] = sb("w_lo", [128, W_COLS], F16)
        for phase in (middle_phase, expert_phase):
            with ExitStack() as scope:
                phase(nc, scope, dram, keep)


def kernel(**inputs):
    import concourse.bacc as bacc
    from concourse.bass_utils import run_bass_kernel_spmd

    a = {name: np.asarray(value) for name, value in inputs.items()}
    w_kv = a["L0_xattn_w_kv"]
    w1 = a["L1_ffn_W1"].reshape(E, HID, DC, 128).transpose(3, 0, 2, 1)
    w2 = a["L1_ffn_W2"].reshape(E, D, HC, 128).transpose(3, 0, 2, 1)
    pads = np.zeros((3, 128, ROW), np.float32)
    pads[:, :, AT_TOKEN] = PAD_OUT + np.arange(3 * 128).reshape(3, 128)
    host = {
        "x": a["x"],
        "ctx": a["ctx_1024"],
        "ctxT": a["ctx_1024"].transpose(0, 2, 1),
        "mask": a["mask_Bx1xS2_fk0"],
        "wqT": a["L0_xattn_w_q"].T,
        "wkT": w_kv[:D].T,
        "wvT": w_kv[D:].T,
        "woT": a["L0_xattn_w_out"].T,
        "bo": a["L0_xattn_b_out"],
        "gate_wT": a["L0_ffn_gate_w"].T,
        "gate_b": a["L0_ffn_gate_b"],
        "weT": a["L0_ffn_expert_w"].transpose(2, 0, 1),
        "expert_bT": a["L0_ffn_expert_b"].T,
        "w12": np.concatenate([w1.reshape(128, -1), w2.reshape(128, -1)], axis=1),
        "b1T": a["L1_ffn_b1"].T,
        "b2": a["L1_ffn_b2"],
        "route_wT": a["L1_ffn_Wg"].T,
        "route_b": a["L1_ffn_bg"],
        "ident": np.eye(128, dtype=np.float32),
        "iota": np.broadcast_to(np.arange(E, dtype=np.float32), (S, E)),
        "parity": ((np.arange(128)[:, None] // HD) % 2 == np.arange(2)).astype(np.float32),
        "before": np.triu(np.ones((S, S), np.float32), 1),
        "slot_base": np.broadcast_to(np.arange(E, dtype=np.float32) * CAP, (S, E)),
        "place": np.arange(S, dtype=np.float32)[:, None],
        "pads": pads,
        "pad_place": (np.arange(128)[:, None] + np.arange(E) * CAP).astype(np.float32),
        "edges": np.broadcast_to(np.arange(TOKENS // TILE, dtype=np.float32) * TILE, (1, E, TOKENS // TILE)),
        "upto": np.tril(np.ones((E, E), np.float32))[None],
        "tile_no": np.arange(NT, dtype=np.float32)[None],
    }
    nc = bacc.Bacc("TRN2", target_bir_lowering=False, num_devices=1)
    arrays, dram = {}, {}
    for name, value in host.items():
        arrays[f"in_{name}_dram"] = np.ascontiguousarray(value)
        dram[name] = nc.dram_tensor(f"in_{name}_dram", value.shape, mybir.dt.from_np(value.dtype), kind="ExternalInput").ap()
    dram["out"] = nc.dram_tensor("out_0_dram", (OUT_ROWS, D), F32, kind="ExternalOutput").ap()
    dram["dispatch"] = nc.dram_tensor("dispatch_dram", (DISPATCH_ROWS, ROW), F32, kind="Internal").ap()
    build(nc, dram)
    result = run_bass_kernel_spmd(nc, [arrays], core_ids=[0])
    return result.results[0]["out_0_dram"][:TOKENS].reshape(B, S, D)
```

```python
import numpy as np
import concourse.bass as bass
from concourse import mybir
from contextlib import ExitStack

F32 = mybir.dt.float32
F16 = mybir.dt.float16
U32 = mybir.dt.uint32
ALU = mybir.AluOpType
ACT = mybir.ActivationFunctionType
AX = mybir.AxisListType

B, S, KV, D = 32, 112, 375, 256
H, HD = 16, 16
PAIRS = H // 2
KC = 125
NKC = KV // KC
DC = D // 128
E = 8
EPS = 1e-5
UNROLL = 4
LAG_B, LAG_C, LAG_D = 2, 3, 4
ONES_ROW = 96
GB = 4
GT = GB * S
HID = 512
HC = HID // 128
TOKENS = B * S
TILE = 256
NT = (2 * TOKENS + E * (TILE - 1)) // TILE
LAST_TILES = NT - -(-(2 * TOKENS - E * (TILE - 1)) // TILE)
CAP = TOKENS + 128
DUMMY = E * CAP
DISPATCH_ROWS = DUMMY + 2 * 128
ROW = 272
AT_W, AT_TOKEN = D, D + E
PAD_OUT = TOKENS
OUT_ROWS = TOKENS + 3 * 128
W_COLS = E * (DC * HID + HC * D)
W_PIECE = W_COLS // B



def count(t, u, per, extra):
    return t * (UNROLL * per) + (u * per + extra)


def wait(engine, sem, value):
    if isinstance(value, int) and value <= 0:
        return
    engine.wait_ge(sem, value)


def at_most(value, total):
    return min(value, total) if isinstance(value, int) else value


def slot_loads(t, u, slots):
    return t * (16 * UNROLL // slots) + 16 * (u // slots + 1)


def run_steps(engine, step):
    turns, lags = B // UNROLL, (0, LAG_B, LAG_C, LAG_D)
    for t in range(2):
        for u in range(UNROLL):
            step(t, u, tuple(t * UNROLL + u >= lag for lag in lags), True)
    with engine.Fori(2, turns - 1) as t:
        for u in range(UNROLL):
            step(t, u, (True,) * 4, True)
    for u in range(UNROLL):
        step(turns - 1, u, (True,) * 4, u < UNROLL - 1)
    for u in range(LAG_D):
        step(turns, u, tuple(u < lag for lag in lags), False)


def attention_phase(nc, ctx, dram, keep):
    def sb(name, shape, dt):
        return ctx.enter_context(nc.sbuf_tensor(name, shape, dt))

    def sem(name):
        return ctx.enter_context(nc.semaphore(name))

    x_res, xT_hi, xT_lo, gate_counts = keep["x_res"], keep["xT_hi"], keep["xT_lo"], keep["gate_counts"]
    ident, iota = keep["ident"], keep["iota"]
    psum = keep["psum"]

    wq = sb("wq", [128, DC, D], F32)
    wk = sb("wk", [128, DC, D], F32)
    wv = sb("wv", [128, DC, D], F32)
    wo = sb("wo", [128, DC, D], F32)
    bo = sb("bo", [S, D], F32)
    gate_w = sb("gate_w", [128, DC, E], F32)
    gate_whi = sb("gate_whi", [128, DC, E], F16)
    gate_wlo = sb("gate_wlo", [128, DC, E], F16)
    wk_hi, wk_lo = sb("wk_hi", [128, DC, D], F16), sb("wk_lo", [128, DC, D], F16)
    wv_hi, wv_lo = sb("wv_hi", [128, DC, D], F16), sb("wv_lo", [128, DC, D], F16)
    gate_bias = sb("gate_bias", [S, E], F32)
    parity = sb("parity", [128, 2], F32)
    half = sb("half", [S, 1], F32)
    ctxT = sb("ctxT", [128, 2, DC, KV], F32)
    ctx_hi = sb("ctx_hi", [128, 2, DC, KV], F16)
    ctx_lo = sb("ctx_lo", [128, 2, DC, KV], F16)
    ln1_stats = sb("ln1_stats", [S, 6], F32)
    ln1_mv = sb("ln1_mv", [S, 2], F32)
    ln1_var = sb("ln1_var", [S, 1], F32)
    ln1_rstd = sb("ln1_rstd", [S, 1], F32)
    xn = sb("xn", [S, D], F32)
    xnT = sb("xnT", [128, DC, S], F32)
    q_hi = sb("q_hi", [128, 2, DC, 2, S], F16)
    q_lo = sb("q_lo", [128, 2, DC, 2, S], F16)
    k_hi = sb("k_hi", [128, 2, DC, KV + 1], F16)
    k_lo = sb("k_lo", [128, 2, DC, KV + 1], F16)
    q_stack = sb("q_stack", [128, UNROLL, PAIRS, 2 * S], F16)
    k_stack = sb("k_stack", [128, UNROLL, PAIRS, KV + 1], F16)
    v_aug = sb("v_aug", [KC, UNROLL, NKC, H, 32], F32)
    smax = sb("smax", [S, 2, H], F32)
    neg_max = sb("neg_max", [H, S], F16)
    probsT = sb("probsT", [KC, 2, NKC, H, S], F32)
    oT = sb("oT", [128, 4, S], F32)
    inv_sum = sb("inv_sum", [S, 4, 4, 1], F32)
    o_nat = sb("o_nat", [S, D], F32)
    onT = sb("onT", [128, DC, S], F32)
    ln2_stats = sb("ln2_stats", [S, 6], F32)
    ln2_mv = sb("ln2_mv", [S, 2], F32)
    ln2_var = sb("ln2_var", [S, 1], F32)
    ln2_rstd = sb("ln2_rstd", [S, 1], F32)
    x1n = sb("x1n", [S, D], F32)
    logits = sb("logits", [S, E], F32)
    top8 = sb("top8", [S, 8], F32)
    top8_at = sb("top8_at", [S, 8], U32)

    names = """const_in wq_in wkv_in late_in half_set counts_set stack_set values_set weight_split gate_split ctxhi_ready ctxlo_ready
        ctx_in0 ctx_in1 x_in0 x_in1 q_in0 q_in1 q_in2 q_in3 k_in0 k_in1 k_in2 k_in3 q_pool0 q_pool1 q_pool2 q_pool3 k_pool0 k_pool1 k_pool2 k_pool3 m_in
        mT_done xnT_done q_done k_done v_done scores_done scoresT_done pv_done oT_back_done onT_done
        out_done x1nT_done gate_done
        negm_ready xnT_ready qhi_ready khi_ready exp_done oT_ready onT_ready x1hi_ready v_ready
        ln1_st ln1_agg xn_ready max_done qlo_ready klo_ready inv_ready o_ready x1_ready ln2_st ln2_agg
        x1n_ready x1lo_ready logits_ready choice_ready
        passed ln1_eps ln1_rs xb_ready ln2_eps ln2_rs""".split()
    m = {n: sem("a_" + n) for n in names}
    keep["attention_semaphores"] = list(m.values())
    ctx_in = [m["ctx_in0"], m["ctx_in1"]]
    x_in = [m["x_in0"], m["x_in1"]]
    q_in = [m[f"q_in{i}"] for i in range(4)]
    q_pool_in = [m[f"q_pool{i}"] for i in range(4)]
    k_in = [m[f"k_in{i}"] for i in range(4)]
    k_pool_in = [m[f"k_pool{i}"] for i in range(4)]

    bank_a = psum[:, 6, :]
    bank_d = psum[:, 7, :]
    N_CONST, N_LATE = 2, 5

    def apart(engine):
        engine.sem_inc(m["passed"], 1)

    KEY_ROWS = ((0, k_hi), (1, k_lo), (2, k_hi))
    QUERY_ROWS = ((0, q_hi), (1, q_hi), (2, q_lo))

    def query_rows(engine, u, part, src, j, arrived):
        engine.dma_start(q_stack[32 * part:32 * part + 32, u % 4, j::4, :],
                         src[32 * j:32 * j + 32, u % 2, :, :, :].rearrange("p c s q -> p c (s q)")).then_inc(arrived[u % 4], 16)

    def key_rows(engine, u, part, src, j, arrived):
        engine.dma_start(k_stack[32 * part:32 * part + 32, u % 4, j::4, 0:KV],
                         src[32 * j:32 * j + 32, u % 2, :, 0:KV]).then_inc(arrived[u % 4], 16)

    with nc.Block() as block:

        @block.sync
        def _(sp):
            def load(t, u):
                b = t * UNROLL + u
                wait(sp, m["ctxlo_ready"], count(t, u - 2, 1, 1))
                apart(sp)
                sp.dma_start(x_res[:, bass.ds(b, 1), :].rearrange("p o d -> p (o d)"),
                             dram["x"][bass.ds(b, 1), :, :].rearrange("o s d -> (o s) d")).then_inc(x_in[u % 2], 16)
                sp.dma_start(ctxT[:, u % 2, :, :],
                             dram["ctxT"][bass.ds(b, 1), :, :].rearrange("o (c p) s -> p (o c) s", p=128)).then_inc(ctx_in[u % 2], 16)

            def weight(dst, src, arrived):
                sp.dma_start(dst[:], dram[src].rearrange("(c p) n -> p c n", p=128)).then_inc(arrived, 16)

            load(0, 0)
            sp.dma_start(ident[:], dram["ident"]).then_inc(m["const_in"], 16)
            weight(wq, "wqT", m["wq_in"])
            sp.dma_start(parity[:], dram["parity"]).then_inc(m["const_in"], 16)
            weight(wk, "wkT", m["wkv_in"])
            weight(wv, "wvT", m["wkv_in"])
            load(0, 1)
            sp.dma_start(bo[:], dram["bo"].rearrange("(o n) -> o n", o=1).broadcast_to([S, D])).then_inc(m["late_in"], 16)
            weight(wo, "woT", m["late_in"])
            weight(gate_w, "gate_wT", m["late_in"])
            sp.dma_start(gate_bias[:], dram["gate_b"].rearrange("(o n) -> o n", o=1).broadcast_to([S, E])).then_inc(m["late_in"], 16)
            sp.dma_start(iota[:], dram["iota"]).then_inc(m["late_in"], 16)

            def step(t, u, on, more):
                a, b_, c, d = on
                if not isinstance(t, int) or t * UNROLL + u + 2 < B:
                    load(t, u + 2)
                if c:
                    wait(sp, m["negm_ready"], count(t, u - LAG_C, 1, 1))
                    apart(sp)
                    row = q_stack[ONES_ROW:ONES_ROW + 1, (u - LAG_C) % 4, :, :].rearrange("o r (s q) -> o (r s) q", s=2)
                    sp.dma_start(row, neg_max[:, :]).then_inc(m["m_in"], 16)
                if a:
                    wait(sp, m["scoresT_done"], count(t, u - 4, 6, 6))
                    apart(sp)
                    wait(sp, m["qhi_ready"], count(t, u, 2, 2))
                    apart(sp)
                    for part, src in QUERY_ROWS[:2]:
                        for j in range(4):
                            query_rows(sp, u, part, src, j, q_in)
                    wait(sp, m["khi_ready"], count(t, u, 2, 2))
                    apart(sp)
                    for j in range(4):
                        key_rows(sp, u, *KEY_ROWS[0], j, k_in)
                    wait(sp, m["klo_ready"], count(t, u, 2, 2))
                    apart(sp)
                    for j in range(4):
                        key_rows(sp, u, *KEY_ROWS[1], j, k_in)

            run_steps(sp, step)

        @block.gpsimd
        def _(pool):
            nc.gpsimd.memset(half[:], -0.5).then_inc(m["half_set"], 1)
            pool.wait_ge(m["half_set"], 1)

            def ln1_rstd_of(t, u):
                wait(pool, m["ln1_agg"], count(t, u, 1, 1))
                apart(pool)
                nc.gpsimd.tensor_scalar(ln1_var[:], ln1_mv[:, 1:2], EPS, None, ALU.add).then_inc(m["ln1_eps"], 1)
                wait(pool, m["ln1_eps"], count(t, u, 1, 1))
                nc.gpsimd.tensor_tensor(ln1_rstd[:], ln1_var[:], half[:], ALU.pow).then_inc(m["ln1_rs"], 1)

            def ctx_low(t, u):
                wait(pool, m["ctxhi_ready"], count(t, u, 1, 1))
                wait(pool, m["v_done"], count(t, u - 2, 2, 2))
                nc.gpsimd.tensor_tensor(ctx_lo[:, u % 2, :, :], ctxT[:, u % 2, :, :], ctx_hi[:, u % 2, :, :], ALU.subtract).then_inc(m["ctxlo_ready"], 1)

            ln1_rstd_of(0, 0)
            ctx_low(0, 0)

            def step(t, u, on, more):
                b = t * UNROLL + u
                if isinstance(t, int) and t == 0:
                    nc.gpsimd.memset(v_aug[:, u, :, :, HD:HD + 1], 1.0).then_inc(m["values_set"], 1)
                    nc.gpsimd.memset(v_aug[:, u, :, :, HD + 1:], 0.0).then_inc(m["values_set"], 1)
                    if u == 0:
                        pool.wait_ge(m["late_in"], 16 * N_LATE)
                if on[0]:
                    wait(pool, m["xn_ready"], count(t, u, 1, 1))
                    apart(pool)
                    xb = x_res[:, bass.ds(b, 1), :].rearrange("p o d -> p (o d)")
                    nc.gpsimd.tensor_tensor(xb, xb, bo[:], ALU.add).then_inc(m["xb_ready"], 1)
                if more:
                    ctx_low(t, u + 1)
                if on[0]:
                    wait(pool, m["scoresT_done"], count(t, u - 4, 6, 6))
                    wait(pool, m["qlo_ready"], count(t, u, 2, 2))
                    apart(pool)
                    for j in range(4):
                        query_rows(pool, u, *QUERY_ROWS[2], j, q_pool_in)
                if on[3]:
                    wait(pool, m["ln2_agg"], count(t, u - LAG_D, 1, 1))
                    apart(pool)
                    nc.gpsimd.tensor_scalar(ln2_var[:], ln2_mv[:, 1:2], EPS, None, ALU.add).then_inc(m["ln2_eps"], 1)
                    wait(pool, m["ln2_eps"], count(t, u - LAG_D, 1, 1))
                    nc.gpsimd.tensor_tensor(ln2_rstd[:], ln2_var[:], half[:], ALU.pow).then_inc(m["ln2_rs"], 1)
                if more:
                    ln1_rstd_of(t, u + 1)
                if on[0]:
                    wait(pool, m["khi_ready"], count(t, u, 2, 2))
                    apart(pool)
                    for j in range(4):
                        key_rows(pool, u, *KEY_ROWS[2], j, k_pool_in)

            run_steps(pool, step)

        @block.tensor
        def _(pe):
            pe.wait_ge(m["const_in"], 16 * N_CONST)
            pe.wait_ge(m["wq_in"], 16)

            def scores(t, u, h):
                b4, s = (u - LAG_B) % 4, h % 2
                n = h + 16 * (u - LAG_B)
                if h == 0:
                    wait(pe, q_in[b4], slot_loads(t, u - LAG_B, 4) * 8)
                    wait(pe, q_pool_in[b4], slot_loads(t, u - LAG_B, 4) * 4)
                    wait(pe, k_in[b4], slot_loads(t, u - LAG_B, 4) * 8)
                    wait(pe, k_pool_in[b4], slot_loads(t, u - LAG_B, 4) * 4)
                wait(pe, m["max_done"], count(t, u - LAG_B, 16, h - 1))
                nc.tensor.matmul(psum[0:S, 4 + s, 0:KV], q_stack[0:96, b4, h // 2, s * S:(s + 1) * S],
                                 k_stack[0:96, b4, h // 2, 0:KV], start=True, stop=True).then_inc(m["scores_done"], 1)

            def scoresT(t, u, n):
                b4, hg, c = (u - LAG_C) % 4, n // NKC, n % NKC
                if n == 0:
                    if isinstance(t, int) and t * UNROLL + u == LAG_C:
                        pe.wait_ge(m["stack_set"], UNROLL)
                    wait(pe, m["m_in"], count(t, u - LAG_C, 16, 16))
                wait(pe, m["exp_done"], count(t, u - LAG_C, 6, n - 1))
                for r in range(4):
                    pair = 4 * hg + r
                    last = nc.tensor.matmul(psum[0:KC, 2 * (n % 2) + r // 2, (r % 2) * 2 * S:(r % 2 + 1) * 2 * S],
                                            k_stack[0:ONES_ROW + 1, b4, pair, c * KC:(c + 1) * KC],
                                            q_stack[0:ONES_ROW + 1, b4, pair, :], start=True, stop=True)
                last.then_inc(m["scoresT_done"], 1)

            def step(t, u, on, more):
                a, b_, c, d = on
                b2a, b4d, b2d = u % 2, (u - LAG_D) % 4, (u - LAG_D) % 2
                bd = t * UNROLL + (u - LAG_D)

                def values(g):
                    if g == 0 and isinstance(t, int) and t * UNROLL + u == LAG_D:
                        pe.wait_ge(m["values_set"], 2 * UNROLL)
                        pe.wait_ge(m["late_in"], 16 * N_LATE)
                        pe.wait_ge(m["gate_split"], 2)
                    if g % 2 == 0:
                        wait(pe, m["exp_done"], count(t, u - LAG_D, 6, 3 + 3 * (g // 2)))
                    for cc in range(NKC):
                        for j in range(4):
                            h = 4 * g + j
                            last = nc.tensor.matmul(bank_d[32 * j:32 * j + 32, g * S:(g + 1) * S], v_aug[:, b4d, cc, h, :],
                                                    probsT[:, b2d, cc, h, :], start=(cc == 0), stop=(cc == NKC - 1))
                    if g == 3:
                        last.then_inc(m["pv_done"], 1)

                def keys(mc):
                    if mc == 0:
                        if isinstance(t, int) and t + u == 0:
                            pe.wait_ge(m["weight_split"], 4)
                        wait(pe, m["ctxlo_ready"], count(t, u, 1, 1))
                        wait(pe, m["qlo_ready"], count(t, u, 2, 2))
                    else:
                        wait(pe, m["klo_ready"], count(t, u, 2, 1))
                    n = 0
                    for w, x in ((wk_hi, ctx_hi), (wk_hi, ctx_lo), (wk_lo, ctx_hi)):
                        for kc in range(DC):
                            last = nc.tensor.matmul(bank_a[:, 0:KV], w[:, kc, mc * 128:(mc + 1) * 128], x[:, b2a, kc, :],
                                                    start=(n == 0), stop=(n == 3 * DC - 1))
                            n += 1
                    last.then_inc(m["k_done"], 1)

                def vals(chunks):
                    if chunks[0] == 0:
                        wait(pe, m["klo_ready"], count(t, u, 2, 2))
                    else:
                        wait(pe, m["v_ready"], count(t, u, 3, 2))
                    for n, cc in enumerate(chunks):
                        done = 0
                        for x, w in ((ctx_hi, wv_hi), (ctx_lo, wv_hi), (ctx_hi, wv_lo)):
                            for kc in range(DC):
                                last = nc.tensor.matmul(bank_a[0:KC, n * D:(n + 1) * D], x[:, b2a, kc, cc * KC:(cc + 1) * KC], w[:, kc, :],
                                                        start=(done == 0), stop=(done == 3 * DC - 1))
                                done += 1
                    last.then_inc(m["v_done"], 1)

                def pair_scores(h):
                    if b_:
                        scores(t, u, h)
                        scores(t, u, h + 1)

                def unit_scoresT(n):
                    if c:
                        scoresT(t, u, n)

                if a or c:
                    wait(pe, m["v_ready"], at_most(count(t, u - 1, 3, 3), 3 * B))
                if a:
                    wait(pe, m["xn_ready"], count(t, u, 1, 1))
                    for kc in range(DC):
                        last = nc.tensor.transpose(bank_a[:, kc * S:(kc + 1) * S], xn[:, kc * 128:(kc + 1) * 128], ident[0:S, 0:S])
                    last.then_inc(m["xnT_done"], 1)
                if d:
                    wait(pe, m["logits_ready"], count(t, u - LAG_D - 1, 1, 1))
                    values(0)
                if c:
                    wait(pe, m["max_done"], count(t, u - LAG_C, 16, 16))
                    if a:
                        wait(pe, m["xnT_ready"], count(t, u, 1, 1))
                    nc.tensor.transpose(bank_a[0:H, 2 * S:3 * S], smax[:, (u - LAG_C) % 2, :], ident[0:S, 0:S]).then_inc(m["mT_done"], 1)
                pair_scores(0)
                if d:
                    values(1)
                if a:
                    wait(pe, m["xnT_ready"], count(t, u, 1, 1))
                    if c:
                        wait(pe, m["negm_ready"], count(t, u - LAG_C, 1, 1))
                    for mc in range(DC):
                        for kc in range(DC):
                            last = nc.tensor.matmul(bank_a[:, mc * S:(mc + 1) * S], wq[:, kc, mc * 128:(mc + 1) * 128], xnT[:, kc, :],
                                                    start=(kc == 0), stop=(kc == DC - 1))
                    last.then_inc(m["q_done"], 1)
                pair_scores(2)
                if d:
                    values(2)
                if d:
                    values(3)
                pair_scores(4)
                if a:
                    keys(0)
                if d:
                    wait(pe, m["oT_ready"], count(t, u - LAG_D, 1, 1))
                    for g in range(4):
                        last = nc.tensor.transpose(bank_d[0:S, g * 128:(g + 1) * 128], oT[:, g, :], ident[:, :])
                    last.then_inc(m["oT_back_done"], 1)
                pair_scores(6)
                unit_scoresT(0)
                unit_scoresT(1)
                if a:
                    keys(1)
                if d:
                    wait(pe, m["o_ready"], count(t, u - LAG_D, 1, 1))
                    for kc in range(DC):
                        last = nc.tensor.transpose(bank_d[:, kc * S:(kc + 1) * S], o_nat[:, kc * 128:(kc + 1) * 128], ident[0:S, 0:S])
                    last.then_inc(m["onT_done"], 1)
                pair_scores(8)
                unit_scoresT(2)
                if d:
                    wait(pe, m["onT_ready"], count(t, u - LAG_D, 1, 1))
                    for kc in range(DC):
                        last = nc.tensor.matmul(bank_d[0:S, 0:D], onT[:, kc, :], wo[:, kc, :], start=(kc == 0), stop=(kc == DC - 1))
                    last.then_inc(m["out_done"], 1)
                pair_scores(10)
                if a:
                    vals((0, 1))
                pair_scores(12)
                unit_scoresT(3)
                if d:
                    wait(pe, m["x1n_ready"], count(t, u - LAG_D, 1, 1))
                    for kc in range(DC):
                        last = nc.tensor.transpose(bank_d[:, kc * S:(kc + 1) * S], x1n[:, kc * 128:(kc + 1) * 128], ident[0:S, 0:S])
                    last.then_inc(m["x1nT_done"], 1)
                pair_scores(14)
                unit_scoresT(4)
                if a:
                    vals((2,))
                unit_scoresT(5)
                if d:
                    wait(pe, m["x1lo_ready"], count(t, u - LAG_D, 1, 1))
                    n = 0
                    for left, right in ((xT_hi, gate_whi), (xT_hi, gate_wlo), (xT_lo, gate_whi)):
                        for kc in range(DC):
                            last = nc.tensor.matmul(bank_d[0:S, 0:E], left[:, kc, bass.ds(bd * S, S)], right[:, kc, :],
                                                    start=(n == 0), stop=(n == 3 * DC - 1))
                            n += 1
                    last.then_inc(m["gate_done"], 1)

            run_steps(pe, step)

        @block.scalar
        def _(act):
            act.wait_ge(m["const_in"], 16 * N_CONST)

            def exps(t, u, n):
                p, hg, c = (u - LAG_C) % 2, n // NKC, n % NKC
                if n == 0:
                    wait(act, m["pv_done"], count(t, u - LAG_C - 2, 1, 1))
                wait(act, m["scoresT_done"], count(t, u - LAG_C, 6, n + 1))
                nc.scalar.activation(probsT[:, p, c, 8 * hg:8 * hg + 8, :].rearrange("p (k h) q -> p k (h q)", k=2),
                                     psum[0:KC, 2 * (n % 2):2 * (n % 2) + 2, 0:4 * S], ACT.Exp,
                                     scale=float(HD) ** -0.5).then_inc(m["exp_done"], 1)

            def ctx_high(t, u):
                wait(act, ctx_in[u % 2], slot_loads(t, u, 2))
                wait(act, m["v_done"], count(t, u - 2, 2, 2))
                nc.scalar.activation(ctx_hi[:, u % 2, :, :], ctxT[:, u % 2, :, :], ACT.Copy).then_inc(m["ctxhi_ready"], 1)

            ctx_high(0, 0)

            def step(t, u, on, more):
                a, b_, c, d = on
                bd = t * UNROLL + (u - LAG_D)

                def khi(mc):
                    wait(act, m["k_done"], count(t, u, 2, mc + 1))
                    if mc == 0:
                        wait(act, k_in[(u - 2) % 4], slot_loads(t, u - 2, 4) * 8)
                        wait(act, k_pool_in[(u - 2) % 4], slot_loads(t, u - 2, 4) * 4)
                    nc.scalar.activation(k_hi[:, u % 2, mc, 0:KV], bank_a[:, 0:KV], ACT.Copy).then_inc(m["khi_ready"], 1)

                def vout(chunks):
                    if chunks[0] == 0:
                        wait(act, m["pv_done"], count(t, u - 4, 1, 1))
                    wait(act, m["v_done"], count(t, u, 2, 1 if chunks[0] == 0 else 2))
                    for n, cc in enumerate(chunks):
                        nc.scalar.activation(v_aug[:, u % 4, cc, :, 0:HD], bank_a[0:KC, n * D:(n + 1) * D].rearrange("p (h w) -> p h w", w=HD),
                                             ACT.Copy).then_inc(m["v_ready"], 1)

                if a:
                    wait(act, m["xnT_done"], count(t, u, 1, 1))
                    wait(act, m["q_done"], count(t, u - 1, 1, 1))
                    nc.scalar.activation(xnT[:, :, :].rearrange("p c s -> p (c s)"), bank_a[:, 0:DC * S], ACT.Copy).then_inc(m["xnT_ready"], 1)
                if c:
                    wait(act, m["mT_done"], count(t, u - LAG_C, 1, 1))
                    wait(act, m["m_in"], count(t, u - LAG_C - 1, 16, 16))
                    nc.scalar.activation(neg_max[:, :], bank_a[0:H, 2 * S:3 * S], ACT.Copy, scale=-1.0).then_inc(m["negm_ready"], 1)
                if more:
                    ctx_high(t, u + 1)
                if a:
                    wait(act, m["q_done"], count(t, u, 1, 1))
                    wait(act, q_in[(u - 2) % 4], slot_loads(t, u - 2, 4) * 8)
                    for s in range(2):
                        nc.scalar.activation(q_hi[:, u % 2, :, s, :], bank_a[:, 0:DC * S].rearrange("p (c s) -> p c s", c=DC),
                                             ACT.Copy, scale=parity[:, s:s + 1]).then_inc(m["qhi_ready"], 1)
                if d:
                    wait(act, m["pv_done"], count(t, u - LAG_D, 1, 1))
                    wait(act, m["oT_back_done"], count(t, u - LAG_D - 1, 1, 1))
                    nc.scalar.activation(oT[:, :, :].rearrange("p g s -> p (g s)"), bank_d[:, 0:4 * S], ACT.Copy).then_inc(m["oT_ready"], 1)
                if a:
                    khi(0)
                if c:
                    exps(t, u, 0)
                    exps(t, u, 1)
                if d:
                    wait(act, m["onT_done"], count(t, u - LAG_D, 1, 1))
                    wait(act, m["out_done"], count(t, u - LAG_D - 1, 1, 1))
                    nc.scalar.activation(onT[:, :, :].rearrange("p c s -> p (c s)"), bank_d[:, 0:DC * S], ACT.Copy).then_inc(m["onT_ready"], 1)
                if a:
                    khi(1)
                if c:
                    exps(t, u, 2)
                if a:
                    vout((0, 1))
                if c:
                    exps(t, u, 3)
                if c:
                    exps(t, u, 4)
                if a:
                    vout((2,))
                if c:
                    exps(t, u, 5)

            run_steps(act, step)

        @block.vector
        def _(dve):
            nc.vector.memset(gate_counts[:], 0.0).then_inc(m["counts_set"], 1)

            def maxima(t, u, heads):
                for h in heads:
                    if h == 0:
                        wait(dve, m["mT_done"], count(t, u - LAG_B - 2, 1, 1))
                    wait(dve, m["scores_done"], count(t, u - LAG_B, 16, h + 1))
                    nc.vector.reduce_max(smax[:, (u - LAG_B) % 2, h:h + 1], psum[0:S, 4 + h % 2, 0:KV], AX.X).then_inc(m["max_done"], 1)

            def ln1_stats_of(t, u):
                xb = x_res[:, bass.ds(t * UNROLL + u, 1), :].rearrange("p o d -> p (o d)")
                wait(dve, x_in[u % 2], slot_loads(t, u, 2))
                apart(dve)
                nc.vector.bn_stats(ln1_stats[:], xb).then_inc(m["ln1_st"], 1)
                wait(dve, m["ln1_st"], count(t, u, 1, 1))
                apart(dve)
                nc.vector.bn_aggr(ln1_mv[:], ln1_stats[:]).then_inc(m["ln1_agg"], 1)

            def ln1_out(t, u):
                xb = x_res[:, bass.ds(t * UNROLL + u, 1), :].rearrange("p o d -> p (o d)")
                wait(dve, m["ln1_rs"], count(t, u, 1, 1))
                wait(dve, m["xnT_done"], count(t, u - 1, 1, 1))
                nc.vector.tensor_scalar(xn[:], xb, ln1_mv[:, 0:1], ln1_rstd[:], ALU.subtract, ALU.mult).then_inc(m["xn_ready"], 1)

            ln1_stats_of(0, 0)
            ln1_out(0, 0)
            dve.wait_ge(m["wkv_in"], 32)
            nc.vector.tensor_copy(wk_hi[:], wk[:]).then_inc(m["weight_split"], 1)
            nc.vector.tensor_copy(wv_hi[:], wv[:]).then_inc(m["weight_split"], 1)
            dve.wait_ge(m["weight_split"], 2)
            nc.vector.tensor_tensor(wk_lo[:], wk[:], wk_hi[:], ALU.subtract).then_inc(m["weight_split"], 1)
            nc.vector.tensor_tensor(wv_lo[:], wv[:], wv_hi[:], ALU.subtract).then_inc(m["weight_split"], 1)
            dve.wait_ge(m["const_in"], 16 * N_CONST)

            def step(t, u, on, more):
                a, b_, c, d = on
                if isinstance(t, int) and t == 0:
                    nc.vector.memset(k_stack[ONES_ROW:ONES_ROW + 1, u, :, :], 1.0).then_inc(m["stack_set"], 1)
                    if u == 1:
                        dve.wait_ge(m["late_in"], 16 * N_LATE)
                        dve.wait_ge(m["counts_set"], 1)
                        nc.vector.tensor_copy(gate_whi[:], gate_w[:]).then_inc(m["gate_split"], 1)
                        dve.wait_ge(m["gate_split"], 1)
                        nc.vector.tensor_tensor(gate_wlo[:], gate_w[:], gate_whi[:], ALU.subtract).then_inc(m["gate_split"], 1)
                bd = t * UNROLL + (u - LAG_D)

                def klo(mc):
                    if a:
                        wait(dve, m["khi_ready"], count(t, u, 2, mc + 1))
                        nc.vector.tensor_tensor(k_lo[:, u % 2, mc, 0:KV], bank_a[:, 0:KV], k_hi[:, u % 2, mc, 0:KV],
                                                ALU.subtract).then_inc(m["klo_ready"], 1)

                def one_max(h):
                    if b_:
                        maxima(t, u, (h,))

                def pair_max(h):
                    one_max(h)
                    one_max(h + 1)

                pair_max(0)
                pair_max(2)
                if a:
                    for s in range(2):
                        wait(dve, m["qhi_ready"], count(t, u, 2, 2))
                        if s == 0:
                            wait(dve, q_pool_in[(u - 2) % 4], slot_loads(t, u - 2, 4) * 4)
                        nc.vector.scalar_tensor_tensor(q_lo[:, u % 2, :, s, :], bank_a[:, 0:DC * S].rearrange("p (c s) -> p c s", c=DC),
                                                       parity[:, s:s + 1], q_hi[:, u % 2, :, s, :],
                                                       ALU.mult, ALU.subtract).then_inc(m["qlo_ready"], 1)
                pair_max(4)
                klo(0)
                if d:
                    o4 = bank_d[0:S, :].rearrange("p (g j w) -> p g j w", g=4, j=4)
                    wait(dve, m["oT_back_done"], count(t, u - LAG_D, 1, 1))
                    nc.vector.reciprocal(inv_sum[:], o4[:, :, :, HD:HD + 1]).then_inc(m["inv_ready"], 1)
                    wait(dve, m["inv_ready"], count(t, u - LAG_D, 1, 1))
                    wait(dve, m["onT_done"], count(t, u - LAG_D - 1, 1, 1))
                    nc.vector.tensor_tensor(o_nat[:].rearrange("p (h w) -> p h w", w=HD),
                                            bank_d[0:S, :].rearrange("p (h w) -> p h w", w=32)[:, :, 0:HD],
                                            inv_sum[:].rearrange("p g j o -> p (g j) o").broadcast_to([S, H, HD]),
                                            ALU.mult).then_inc(m["o_ready"], 1)
                pair_max(6)
                pair_max(8)
                klo(1)
                if d:
                    x1 = x_res[:, bass.ds(bd, 1), :].rearrange("p o d -> p (o d)")
                    wait(dve, m["out_done"], count(t, u - LAG_D, 1, 1))
                    wait(dve, m["xb_ready"], count(t, u - LAG_D, 1, 1))
                    nc.vector.tensor_tensor(x1, bank_d[0:S, 0:D], x1, ALU.add).then_inc(m["x1_ready"], 1)
                if d:
                    wait(dve, m["x1_ready"], count(t, u - LAG_D, 1, 1))
                    apart(dve)
                    nc.vector.bn_stats(ln2_stats[:], x1).then_inc(m["ln2_st"], 1)
                one_max(10)
                if d:
                    wait(dve, m["ln2_st"], count(t, u - LAG_D, 1, 1))
                    apart(dve)
                    nc.vector.bn_aggr(ln2_mv[:], ln2_stats[:]).then_inc(m["ln2_agg"], 1)
                one_max(11)
                if more:
                    ln1_stats_of(t, u + 1)
                if d:
                    wait(dve, m["ln2_rs"], count(t, u - LAG_D, 1, 1))
                    wait(dve, m["x1nT_done"], count(t, u - LAG_D - 1, 1, 1))
                    nc.vector.tensor_scalar(x1n[:], x1, ln2_mv[:, 0:1], ln2_rstd[:], ALU.subtract, ALU.mult).then_inc(m["x1n_ready"], 1)
                one_max(12)
                one_max(13)
                if d:
                    wait(dve, m["x1nT_done"], count(t, u - LAG_D, 1, 1))
                    nc.vector.tensor_copy(xT_hi[:, :, bass.ds(bd * S, S)], bank_d[:, 0:DC * S].rearrange("p (c s) -> p c s", c=DC)).then_inc(m["x1hi_ready"], 1)
                    wait(dve, m["x1hi_ready"], count(t, u - LAG_D, 1, 1))
                    nc.vector.tensor_tensor(xT_lo[:, :, bass.ds(bd * S, S)], bank_d[:, 0:DC * S].rearrange("p (c s) -> p c s", c=DC),
                                            xT_hi[:, :, bass.ds(bd * S, S)], ALU.subtract).then_inc(m["x1lo_ready"], 1)
                if more:
                    ln1_out(t, u + 1)
                pair_max(14)
                if d:
                    wait(dve, m["gate_done"], count(t, u - LAG_D, 1, 1))
                    wait(dve, m["choice_ready"], count(t, u - LAG_D - 1, 4, 4))
                    nc.vector.tensor_tensor(logits[:], bank_d[0:S, 0:E], gate_bias[:], ALU.add).then_inc(m["logits_ready"], 1)
                if d:
                    wait(dve, m["logits_ready"], count(t, u - LAG_D, 1, 1))
                    apart(dve)
                    nc.vector.max(top8[:], logits[:]).then_inc(m["choice_ready"], 1)
                    wait(dve, m["choice_ready"], count(t, u - LAG_D, 4, 1))
                    apart(dve)
                    nc.vector.max_index(top8_at[:], top8[:], logits[:]).then_inc(m["choice_ready"], 1)
                    wait(dve, m["choice_ready"], count(t, u - LAG_D, 4, 2))
                    nc.vector.scalar_tensor_tensor(gate_counts[:], iota[:], top8_at[:, 0:1], gate_counts[:],
                                                   ALU.is_equal, ALU.add).then_inc(m["choice_ready"], 1)
                    wait(dve, m["choice_ready"], count(t, u - LAG_D, 4, 3))
                    nc.vector.scalar_tensor_tensor(gate_counts[:], iota[:], top8_at[:, 1:2], gate_counts[:],
                                                   ALU.is_equal, ALU.add).then_inc(m["choice_ready"], 1)

            run_steps(dve, step)


def middle_phase(nc, ctx, dram, keep):
    def sb(name, shape, dt):
        return ctx.enter_context(nc.sbuf_tensor(name, shape, dt))

    def sem(name):
        return ctx.enter_context(nc.semaphore(name))

    ROW_SLOTS = 4
    x_res, xT_hi, xT_lo, gate_counts = keep["x_res"], keep["xT_hi"], keep["xT_lo"], keep["gate_counts"]
    ident, iota, psum, cum = keep["ident"], keep["iota"], keep["psum"], keep["cum"]

    we = sb("we", [128, DC, E, D], F32)
    we_hi = sb("we_hi", [128, DC, E, D], F16)
    we_lo = sb("we_lo", [128, DC, E, D], F16)
    expert_b = sb("expert_b", [128, DC, E], F32)
    share = sb("share", [128, E], F32)
    neg_bias = sb("neg_bias", [128, DC, E], F32)
    bias_sum = sb("bias_sum", [128, DC], F32)
    ones = keep["ones"]
    half = sb("half2", [S, 1], F32)
    acc = sb("acc", [128, 2, DC, GT], F32)
    ctxT = sb("ctxT2", [128, 2, DC, KV], F32)
    ctx_rows = sb("ctx_rows", [KC, 2, NKC, D], F32)
    mask = sb("mask", [S, 2, KV], F32)
    mask_add = sb("mask_add", [S, 2, KV], F32)
    ln_stats = sb("ln_stats", [S, 2, 6], F32)
    ln_mv = sb("ln_mv", [S, 2, 2], F32)
    ln_var = sb("ln_var", [S, 2, 1], F32)
    ln_rstd = sb("ln_rstd", [S, 2, 1], F32)
    x2n = sb("x2n", [S, D], F32)
    x2nT = sb("x2nT", [128, DC, S], F32)
    probs = sb("probs", [S, KV], F32)
    row_max = sb("row_max", [S, 1], F32)
    exp_bias = sb("exp_bias", [S, 1], F32)
    prob_sum = sb("prob_sum", [S, 2, 1], F32)
    inv_sum = sb("inv_sum2", [S, 1], F32)
    probsT = sb("probsT2", [KC, NKC, S], F32)
    rows = sb("rows", [S, ROW_SLOTS, ROW], F32)
    place = sb("place", [S, 1], F32)
    slot_base = sb("slot_base", [S, E], F32)
    before = sb("before", [S, S], F32)
    first = sb("first", [S, E], F32)
    chosen = sb("chosen", [S, E], F32)
    unscaled = sb("unscaled", [S, E], F32)
    slot_of = sb("slot_of", [S, E], F32)
    picked = sb("picked", [S, 2, E], F32)
    slots = sb("slots", [S, 2], F32)
    slots_at = sb("slots_at", [S, ROW_SLOTS, 2], U32)
    taken = [0]

    def reuse(*shape):
        size = int(np.prod(shape))
        taken[0] += size
        view = we[:].rearrange("p c e h -> p (c e h)")[0:NT, taken[0] - size:taken[0]]
        if len(shape) == 3:
            return view.rearrange("p (a b c) -> p a b c", b=shape[1], c=shape[2])
        return view if len(shape) == 1 else view.rearrange("p (a b) -> p a b", b=shape[1])

    FULL_MAX = TOKENS // TILE
    over = reuse(E, FULL_MAX)
    rest = reuse(E)
    length = reuse(2, E)
    upto_length = reuse(2 * E, E)
    ends = reuse(2, E)
    starts = reuse(2, E)
    base = reuse(2, E)
    two_halves = reuse(2, E)
    later = reuse(2, E)
    own = reuse(2, E)
    parts = reuse(3, 2 * E)
    tile = reuse(3)
    counts = sb("counts", [128, E], F32)
    x3 = we[:].rearrange("p c e h -> p (c e h)")[0:S, DC * D * E // 2:DC * D * E // 2 + 2 * D].rearrange("p (n d) -> p n d", d=D)
    edges, upto, tile_no, tile_shift, expert_row, pad_place = (
        keep[k] for k in ("edges", "upto", "tile_no", "tile_shift", "expert_row", "pad_place"))
    table, pad_at = keep["table"], keep["pad_at"]
    w_raw = sb("w_raw", [128, 2, W_PIECE], F32)
    w_hi, w_lo = keep["w_hi"], keep["w_lo"]
    route_w = sb("route_w", [128, DC, E], F32)
    route_whi = sb("route_whi", [128, DC, E], F16)
    route_wlo = sb("route_wlo", [128, DC, E], F16)
    route_bias = sb("route_bias", [S, E], F32)
    logits = sb("logits2", [S, E], F32)
    top8 = sb("top82", [S, 8], F32)
    top8_at = sb("top8_at2", [S, 8], U32)
    gap = sb("gap", [S, 1], F32)
    gap_exp = sb("gap_exp", [S, 1], F32)
    gap_sum = sb("gap_sum", [S, 1], F32)
    first_w = sb("first_w", [S, 1], F32)
    second = sb("second", [S, E], F32)

    names = """weights_in we_in0 we_in1 we_in2 we_in3 share_ps share_rdy bias_rdy we_hi_rdy we_lo_rdy route_split consts
        ctxT_in0 ctxT_in1 rows_in0 rows_in1 mask_in0 mask_in1 passed
        ffn_done accT_done x2nT_done s1_done pT_done o_done x3nT_done route_done
        x2nT_rdy exp_rdy pT_rdy x3hi_rdy gexp_rdy
        acc_rdy x2_rdy st2 ag2 x2n_rdy masked_rdy eb_rdy inv_rdy x3_rdy st3 ag3 x3n_rdy x3lo_rdy
        lg_rdy top_rdy at_rdy gap_rdy pair_rdy which_rdy comb_rdy chosen_rdy rank_done pos_rdy pick_rdy slots_rdy
        cum_rdy token_rdy scattered0 scattered1 scattered2 scattered3 x3_out0 x3_out1 pads_out w_in0 w_in1 w_hi_rdy w_lo_rdy rows_set late_in tally_done table
        eps2 rs2 eps3 rs3 mask_rdy""".split()
    m = {n: sem("m_" + n) for n in names}
    ctxT_in, rows_in, mask_in = ([m[f"{k}{i}"] for i in range(2)] for k in ("ctxT_in", "rows_in", "mask_in"))
    we_in = [m[f"we_in{n}"] for n in range(E // 2)]
    scattered = [m[f"scattered{n}"] for n in range(ROW_SLOTS)]
    LAG_ATT, LAG_OUT, LAG_ROUTE, LAG_SEND = 4, 5, 6, 7
    TURN = 2 * GB
    N_W = 5
    SPLIT_FIRST = 3
    TABLE_OPS = 25
    NEG = -1e9 * 16.0

    def cnt(t, u, per, extra):
        return t * (TURN * per) + (u * per + extra)

    def loads(t, u):
        return t * (16 * TURN // 2) + 16 * (u // 2 + 1)

    def sent(t, u):
        return t * (2 * 16 * TURN // ROW_SLOTS) + 2 * 16 * (u // ROW_SLOTS + 1)

    def apart(engine):
        engine.sem_inc(m["passed"], 1)

    def steps(engine, step):
        turns = B // TURN
        for u in range(TURN):
            step(0, u, (True, u >= LAG_ATT, u >= LAG_OUT, u >= LAG_ROUTE, u >= LAG_SEND))
        with engine.Fori(1, turns) as t:
            for u in range(TURN):
                step(t, u, (True,) * 5)
        for u in range(LAG_SEND):
            step(turns, u, (False, u < LAG_ATT, u < LAG_OUT, u < LAG_ROUTE, True))

    with nc.Block() as block:

        @block.sync
        def _(sp):
            sp.dma_start(expert_b[:], dram["expert_bT"].rearrange("(c p) e -> p c e", p=128)).then_inc(we_in[0], 16)
            for n in range(E // 2):
                for c in range(DC):
                    sp.dma_start(we[:, c, 2 * n:2 * n + 2, :], dram["weT"].rearrange("(c p) e h -> p c e h", p=128)[:, c, 2 * n:2 * n + 2, :]).then_inc(we_in[n], 16)
            sp.dma_start(route_w[:], dram["route_wT"].rearrange("(c p) e -> p c e", p=128)).then_inc(m["weights_in"], 16)
            sp.dma_start(route_bias[:], dram["route_b"].rearrange("(o n) -> o n", o=1).broadcast_to([S, E])).then_inc(m["weights_in"], 16)

            sp.dma_start(before[:], dram["before"]).then_inc(m["weights_in"], 16)
            sp.dma_start(slot_base[:], dram["slot_base"]).then_inc(m["weights_in"], 16)
            sp.dma_start(place[:], dram["place"]).then_inc(m["weights_in"], 16)
            for dst, src in keep["late_loads"]:
                sp.dma_start(dst, src).then_inc(m["late_in"], 16)
            for used in keep["attention_semaphores"]:
                sp.sem_clear(used)
            for n in range(2):
                sp.dma_start(dram["dispatch"][DUMMY + n * 128:DUMMY + (n + 1) * 128, :], dram["pads"][n]).then_inc(m["pads_out"], 16)
            for n in range(3):
                sp.dma_start(dram["out"][PAD_OUT + n * 128:PAD_OUT + (n + 1) * 128, :], dram["pads"][n][:, 0:D]).then_inc(m["pads_out"], 16)

            def store(t, u):
                wait(sp, m["x3_rdy"], cnt(t, u, 1, 1))
                apart(sp)
                sp.dma_start(dram["out"][bass.ds((t * TURN + u) * S, S), :], x3[:, u % 2, :]).then_inc(m[f"x3_out{u % 2}"], 16)

            def load(t, u):
                b, p = t * TURN + u, u % 2
                wait(sp, m["w_lo_rdy"], cnt(t, u - 2, 1, 1))
                apart(sp)
                sp.dma_start(w_raw[:, p, :], dram["w12"][:, bass.ds(b * W_PIECE, W_PIECE)]).then_inc(m[f"w_in{p}"], 16)
                wait(sp, m["s1_done"], cnt(t, u - 2, 1, 1))
                apart(sp)
                sp.dma_start(ctxT[:, p, :, :], dram["ctxT"][bass.ds(b, 1), :, :].rearrange("o (c p) s -> p (o c) s", p=128)).then_inc(ctxT_in[p], 16)
                wait(sp, m["mask_rdy"], cnt(t, u - 2, 1, 1))
                apart(sp)
                sp.dma_start(mask[:, p, :], dram["mask"][bass.ds(b, 1), 0, :].broadcast_to([S, KV])).then_inc(mask_in[p], 16)
                wait(sp, m["o_done"], cnt(t, u - 2, 1, 1))
                apart(sp)
                sp.dma_start(ctx_rows[:, p, :, :], dram["ctx"][bass.ds(b, 1), :, :].rearrange("o (c p) d -> p (o c) d", p=KC)).then_inc(rows_in[p], 16)

            turns = B // TURN
            for u in range(TURN):
                load(0, u)
                if u >= 3:
                    store(0, u - 3)
            with sp.Fori(1, turns) as t:
                for u in range(TURN):
                    load(t, u)
                    store(t, u - 3)
            for u in range(3):
                store(turns, u - 3)
            for n in range(2):
                sp.wait_ge(m[f"x3_out{n}"], 16 * B // 2)
            sp.wait_ge(m["pads_out"], 16 * 5)
            sp.wait_ge(m["late_in"], 16 * len(keep["late_loads"]))

        @block.gpsimd
        def _(pool):
            nc.gpsimd.memset(ones[:], 1.0).then_inc(m["consts"], 1)
            nc.gpsimd.memset(half[:], -0.5).then_inc(m["consts"], 1)
            nc.gpsimd.memset(rows[:], 0.0).then_inc(m["rows_set"], 1)
            pool.wait_ge(m["consts"], 2)
            pool.wait_ge(m["weights_in"], 16 * N_W)
            pool.wait_ge(m["rows_set"], 1)
            for n in range(ROW_SLOTS):
                nc.gpsimd.tensor_scalar(rows[:, n, AT_TOKEN:AT_TOKEN + 1], place[:], float((n - ROW_SLOTS) * S), None, ALU.add).then_inc(m["rows_set"], 1)
            pool.wait_ge(m["rows_set"], 1 + ROW_SLOTS)

            def rstd(agg, eps, rs, n, value):
                wait(pool, m[agg], value)
                apart(pool)
                nc.gpsimd.tensor_scalar(ln_var[:, n, :], ln_mv[:, n, 1:2], EPS, None, ALU.add).then_inc(m[eps], 1)
                wait(pool, m[eps], value)
                nc.gpsimd.tensor_tensor(ln_rstd[:, n, :], ln_var[:, n, :], half[:], ALU.pow).then_inc(m[rs], 1)

            def step(t, u, on):
                f, a, o, r, k = on
                if a:
                    rstd("ag2", "eps2", "rs2", 0, cnt(t, u - LAG_ATT, 1, 1))
                if r:
                    ur = u - LAG_ROUTE
                    v = cnt(t, ur, 1, 1)
                    rstd("ag3", "eps3", "rs3", 1, v)
                    if f:
                        wait(pool, m["rs3"], v)
                        wait(pool, scattered[ur % ROW_SLOTS], sent(t, ur - ROW_SLOTS))
                        apart(pool)
                        nc.gpsimd.tensor_scalar(rows[:, ur % ROW_SLOTS, 0:D], x3[:, ur % 2, :], ln_mv[:, 1, 0:1], ln_rstd[:, 1, :], ALU.subtract, ALU.mult).then_inc(m["x3n_rdy"], 1)
                if a:
                    p = (u - LAG_ATT) % 2
                    wait(pool, mask_in[p], loads(t, u - LAG_ATT))
                    wait(pool, m["masked_rdy"], cnt(t, u - LAG_ATT - 2, 1, 1))
                    apart(pool)
                    nc.gpsimd.tensor_scalar(mask_add[:, p, :], mask[:, p, :], NEG, 0.0, ALU.mult, ALU.add).then_inc(m["mask_rdy"], 1)
                if a:
                    ua = u - LAG_ATT
                    at = (t * TURN + ua) * W_PIECE
                    wait(pool, m["w_hi_rdy"], cnt(t, ua, 1, 1))
                    apart(pool)
                    nc.gpsimd.tensor_tensor(w_lo[:, bass.ds(at, W_PIECE)], w_raw[:, ua % 2, :], w_hi[:, bass.ds(at, W_PIECE)],
                                            ALU.subtract).then_inc(m["w_lo_rdy"], 1)
                if r:
                    ur = u - LAG_ROUTE
                    wait(pool, scattered[ur % ROW_SLOTS], sent(t, ur - ROW_SLOTS))
                    apart(pool)
                    nc.gpsimd.tensor_scalar(rows[:, ur % ROW_SLOTS, AT_TOKEN:AT_TOKEN + 1], rows[:, ur % ROW_SLOTS, AT_TOKEN:AT_TOKEN + 1],
                                            float(ROW_SLOTS * S), None, ALU.add).then_inc(m["token_rdy"], 1)
                if k:
                    uk = u - LAG_SEND
                    wait(pool, m["slots_rdy"], cnt(t, uk, 1, 1))
                    wait(pool, m["comb_rdy"], cnt(t, uk, 1, 1))
                    wait(pool, m["token_rdy"], cnt(t, uk, 1, 1))
                    apart(pool)
                    for n in range(2):
                        nc.gpsimd.indirect_dma_start(dram["dispatch"], bass.IndirectOffsetOnAxis(slots_at[:, uk % ROW_SLOTS, n:n + 1], 0),
                                                     rows[:, uk % ROW_SLOTS, :], None).then_inc(scattered[uk % ROW_SLOTS], 16)

            steps(pool, step)
            for n in range(ROW_SLOTS):
                pool.wait_ge(scattered[n], 2 * 16 * B // ROW_SLOTS)

        @block.tensor
        def _(pe):
            pe.wait_ge(m["consts"], 3)
            nc.tensor.matmul(psum[:, 0, 0:E], ones[:], gate_counts[:], start=True, stop=True).then_inc(m["share_ps"], 1)
            pe.wait_ge(m["share_rdy"], 1)

            def mixture(t, u, k):
                e, hc = 2 * (u % GB) + k // 2, k % 2
                g0 = t * (2 * GT) + (u // GB) * GT
                if isinstance(t, int) and t == 0 and u < GB:
                    pe.wait_ge(m["we_lo_rdy"], e + 1)
                wait(pe, m["acc_rdy"], cnt(t, u, 4, k - 1))
                n = 0
                for w, x in ((we_hi, xT_hi), (we_hi, xT_lo), (we_lo, xT_hi)):
                    for kc in range(DC):
                        last = nc.tensor.matmul(psum[:, k % 2, 0:GT], w[:, kc, e, hc * 128:(hc + 1) * 128], x[:, kc, bass.ds(g0, GT)],
                                                start=(n == 0), stop=(n == 5))
                        n += 1
                last.then_inc(m["ffn_done"], 1)

            def step(t, u, on):
                f, a, o, r, k = on
                ua, uo, ur, uk = u - LAG_ATT, u - LAG_OUT, u - LAG_ROUTE, u - LAG_SEND
                def mix(n):
                    if f:
                        mixture(t, u, n)
                if a:
                    wait(pe, m["acc_rdy"], cnt(t, (ua // GB) * GB, 4, 4 * GB))
                    wait(pe, m["x2nT_rdy"], cnt(t, ua - 1, 1, 1))
                    for hc in range(DC):
                        last = nc.tensor.transpose(psum[0:S, 2, hc * 128:(hc + 1) * 128],
                                                   acc[:, (ua // GB) % 2, hc, (ua % GB) * S:(ua % GB + 1) * S], ident[:, :])
                    last.then_inc(m["accT_done"], 1)
                mix(0)
                mix(1)
                if o:
                    wait(pe, m["exp_rdy"], cnt(t, uo, 1, 1))
                    wait(pe, m["pT_rdy"], cnt(t, uo - 1, 1, 1))
                    for c in range(NKC):
                        last = nc.tensor.transpose(psum[0:KC, 5, c * S:(c + 1) * S], probs[:, c * KC:(c + 1) * KC], ident[0:S, 0:S])
                    last.then_inc(m["pT_done"], 1)
                mix(2)
                if o:
                    wait(pe, rows_in[uo % 2], loads(t, uo))
                    wait(pe, m["pT_rdy"], cnt(t, uo, 1, 1))
                    wait(pe, m["x3_rdy"], cnt(t, uo - 1, 1, 1))
                    for c in range(NKC):
                        last = nc.tensor.matmul(psum[0:S, 6, 0:D], probsT[:, c, :], ctx_rows[:, uo % 2, c, :], start=(c == 0), stop=(c == NKC - 1))
                    last.then_inc(m["o_done"], 1)
                if a:
                    wait(pe, m["x2n_rdy"], cnt(t, ua, 1, 1))
                    for kc in range(DC):
                        last = nc.tensor.transpose(psum[:, 2, D + kc * S:D + (kc + 1) * S], x2n[:, kc * 128:(kc + 1) * 128], ident[0:S, 0:S])
                    last.then_inc(m["x2nT_done"], 1)
                mix(3)
                if r:
                    wait(pe, m["x3n_rdy"], cnt(t, ur, 1, 1))
                    wait(pe, m["lg_rdy"], cnt(t, ur - 1, 1, 1))
                    for kc in range(DC):
                        last = nc.tensor.transpose(psum[:, 7, kc * S:(kc + 1) * S], rows[:, ur % ROW_SLOTS, kc * 128:(kc + 1) * 128], ident[0:S, 0:S])
                    last.then_inc(m["x3nT_done"], 1)
                if k:
                    wait(pe, m["chosen_rdy"], cnt(t, uk, 1, 1))
                    wait(pe, m["cum_rdy"], cnt(t, uk - 1, 1, 1))
                    nc.tensor.matmul(psum[0:S, 3, 0:E], before[:], chosen[:], start=True, stop=False)
                    nc.tensor.matmul(psum[0:S, 3, 0:E], ones[:, 0:S], cum[:], start=False, stop=True).then_inc(m["rank_done"], 1)
                if a:
                    wait(pe, ctxT_in[ua % 2], loads(t, ua))
                    wait(pe, m["x2nT_rdy"], cnt(t, ua, 1, 1))
                    wait(pe, m["masked_rdy"], cnt(t, ua - 1, 1, 1))
                    for kc in range(DC):
                        last = nc.tensor.matmul(psum[0:S, 4, 0:KV], x2nT[:, kc, :], ctxT[:, ua % 2, kc, :], start=(kc == 0), stop=(kc == DC - 1))
                    last.then_inc(m["s1_done"], 1)
                if r:
                    if isinstance(t, int) and t * TURN + ur == 0:
                        pe.wait_ge(m["route_split"], 2)
                    wait(pe, m["x3lo_rdy"], cnt(t, ur, 1, 1))
                    b0 = (t * TURN + ur) * S
                    n = 0
                    for left, right in ((xT_hi, route_whi), (xT_hi, route_wlo), (xT_lo, route_whi)):
                        for kc in range(DC):
                            last = nc.tensor.matmul(psum[0:S, 7, DC * S:DC * S + E], left[:, kc, bass.ds(b0, S)], right[:, kc, :], start=(n == 0), stop=(n == 5))
                            n += 1
                    last.then_inc(m["route_done"], 1)

            steps(pe, step)
            pe.wait_ge(m["cum_rdy"], B)
            nc.tensor.matmul(psum[:, 0, 0:E], ones[:], cum[:], start=True, stop=True).then_inc(m["tally_done"], 1)
            pe.wait_ge(m["table"], TABLE_OPS)
            for n in range(3):
                last = nc.tensor.matmul(psum[0:1, 1, n * NT:(n + 1) * NT], tile[:, n:n + 1], ident[0:NT, 0:NT], start=True, stop=True)
            last.then_inc(m["tally_done"], 1)

        @block.scalar
        def _(act):
            act.wait_ge(m["share_ps"], 1)
            nc.scalar.activation(share[:], psum[:, 0, 0:E], ACT.Copy, scale=1.0 / (2 * B * S)).then_inc(m["share_rdy"], 1)
            act.wait_ge(m["share_rdy"], 1)
            for e in range(E):
                act.wait_ge(we_in[e // 2], 16 * (DC + 1 if e < 2 else DC))
                nc.scalar.activation(we_hi[:, :, e, :], we[:, :, e, :], ACT.Copy, scale=share[:, e:e + 1]).then_inc(m["we_hi_rdy"], 1)

            def step(t, u, on):
                f, a, o, r, k = on
                ua, uo, ur, uk = u - LAG_ATT, u - LAG_OUT, u - LAG_ROUTE, u - LAG_SEND
                if o:
                    wait(act, m["eb_rdy"], cnt(t, uo, 1, 1))
                    nc.scalar.activation(probs[:], probs[:], ACT.Exp, bias=exp_bias[:], scale=float(D) ** -0.5,
                                         accum_out=prob_sum[:, uo % 2, :]).then_inc(m["exp_rdy"], 1)
                if o:
                    wait(act, m["pT_done"], cnt(t, uo, 1, 1))
                    wait(act, m["o_done"], cnt(t, uo - 1, 1, 1))
                    nc.scalar.activation(probsT[:].rearrange("p c s -> p (c s)"), psum[0:KC, 5, 0:NKC * S], ACT.Copy).then_inc(m["pT_rdy"], 1)
                if k:
                    wait(act, m["gap_rdy"], cnt(t, uk, 1, 1))
                    nc.scalar.activation(gap_exp[:], gap[:], ACT.Exp).then_inc(m["gexp_rdy"], 1)
                if a:
                    wait(act, m[f"w_in{ua % 2}"], loads(t, ua))
                    apart(act)
                    nc.scalar.activation(w_hi[:, bass.ds((t * TURN + ua) * W_PIECE, W_PIECE)], w_raw[:, ua % 2, :], ACT.Copy).then_inc(m["w_hi_rdy"], 1)
                if a:
                    wait(act, m["x2nT_done"], cnt(t, ua, 1, 1))
                    wait(act, m["s1_done"], cnt(t, ua - 1, 1, 1))
                    nc.scalar.activation(x2nT[:].rearrange("p c s -> p (c s)"), psum[:, 2, D:D + DC * S], ACT.Copy).then_inc(m["x2nT_rdy"], 1)
                if r:
                    b0 = (t * TURN + ur) * S
                    wait(act, m["x3nT_done"], cnt(t, ur, 1, 1))
                    nc.scalar.activation(xT_hi[:, :, bass.ds(b0, S)], psum[:, 7, 0:DC * S].rearrange("p (c s) -> p c s", c=DC), ACT.Copy).then_inc(m["x3hi_rdy"], 1)

            steps(act, step)

        @block.vector
        def _(dve):
            nc.vector.memset(cum[:], 0.0).then_inc(m["consts"], 1)

            def split_expert(e):
                dve.wait_ge(m["we_hi_rdy"], e + 1)
                nc.vector.scalar_tensor_tensor(we_lo[:, :, e, :], we[:, :, e, :], share[:, e:e + 1], we_hi[:, :, e, :],
                                               ALU.mult, ALU.subtract).then_inc(m["we_lo_rdy"], 1)

            for e in range(SPLIT_FIRST):
                split_expert(e)
            dve.wait_ge(we_in[0], 16 * (DC + 1))
            nc.vector.scalar_tensor_tensor(neg_bias[:], expert_b[:], -1.0, share[:].rearrange("p (o e) -> p o e", o=1).broadcast_to([128, DC, E]),
                                           ALU.mult, ALU.mult).then_inc(m["bias_rdy"], 1)
            dve.wait_ge(m["bias_rdy"], 1)
            nc.vector.tensor_reduce(bias_sum[:], neg_bias[:], AX.X, ALU.add, negate=True).then_inc(m["bias_rdy"], 1)
            dve.wait_ge(m["weights_in"], 16 * N_W)
            nc.vector.tensor_copy(route_whi[:], route_w[:]).then_inc(m["route_split"], 1)
            dve.wait_ge(m["route_split"], 1)
            nc.vector.tensor_tensor(route_wlo[:], route_w[:], route_whi[:], ALU.subtract).then_inc(m["route_split"], 1)
            dve.wait_ge(m["bias_rdy"], 2)

            def mix(t, u, k):
                e, hc = 2 * (u % GB) + k // 2, k % 2
                out = acc[:, u // GB, hc, :]
                if isinstance(t, int) and t == 0 and k % 2 == 0 and SPLIT_FIRST + 2 * u + k // 2 < E:
                    split_expert(SPLIT_FIRST + 2 * u + k // 2)
                wait(dve, m["ffn_done"], cnt(t, u, 4, k + 1))
                if e == 0:
                    wait(dve, m["accT_done"], cnt(t, u - GB - 1, 1, 1))
                    nc.vector.tensor_scalar(out, psum[:, k % 2, 0:GT], neg_bias[:, hc, 0:1], bias_sum[:, hc:hc + 1],
                                            ALU.max, ALU.add).then_inc(m["acc_rdy"], 1)
                else:
                    wait(dve, m["acc_rdy"], cnt(t, u, 4, k - 1))
                    nc.vector.scalar_tensor_tensor(out, psum[:, k % 2, 0:GT], neg_bias[:, hc, e:e + 1], out,
                                                   ALU.max, ALU.add).then_inc(m["acc_rdy"], 1)

            def step(t, u, on):
                f, a, o, r, k = on
                ua, uo, ur, uk = u - LAG_ATT, u - LAG_OUT, u - LAG_ROUTE, u - LAG_SEND
                xrow = lambda uu: x_res[:, bass.ds(t * TURN + uu, 1), :].rearrange("p o d -> p (o d)")
                def norm_stats(x, n, st, ag, value):
                    apart(dve)
                    nc.vector.bn_stats(ln_stats[:, n, :], x).then_inc(m[st], 1)
                    wait(dve, m[st], value)
                    apart(dve)
                    nc.vector.bn_aggr(ln_mv[:, n, :], ln_stats[:, n, :]).then_inc(m[ag], 1)
                if o:
                    v = cnt(t, uo, 1, 1)
                    wait(dve, m["s1_done"], v)
                    wait(dve, m["mask_rdy"], v)
                    wait(dve, m["pT_done"], cnt(t, uo - 1, 1, 1))
                    apart(dve)
                    nc.vector.tensor_tensor_reduce(out=probs[:], in0=psum[0:S, 4, 0:KV], in1=mask_add[:, uo % 2, :], scale=1.0, scalar=-3.0e38,
                                                   op0=ALU.add, op1=ALU.max, accum_out=row_max[:]).then_inc(m["masked_rdy"], 1)
                    wait(dve, m["masked_rdy"], v)
                    nc.vector.tensor_scalar(exp_bias[:], row_max[:], -float(D) ** -0.5, None, ALU.mult).then_inc(m["eb_rdy"], 1)
                if a:
                    v = cnt(t, ua, 1, 1)
                    wait(dve, m["accT_done"], v)
                    nc.vector.tensor_tensor(xrow(ua), psum[0:S, 2, 0:D], xrow(ua), ALU.add).then_inc(m["x2_rdy"], 1)
                    wait(dve, m["x2_rdy"], v)
                    norm_stats(xrow(ua), 0, "st2", "ag2", v)
                if f:
                    mix(t, u, 0)
                if r:
                    v = cnt(t, ur, 1, 1)
                    wait(dve, m["x3_rdy"], v)
                    norm_stats(x3[:, ur % 2, :], 1, "st3", "ag3", v)
                if a:
                    v = cnt(t, ua, 1, 1)
                    wait(dve, m["rs2"], v)
                    wait(dve, m["x2nT_done"], cnt(t, ua - 1, 1, 1))
                    nc.vector.tensor_scalar(x2n[:], xrow(ua), ln_mv[:, 0, 0:1], ln_rstd[:, 0, :], ALU.subtract, ALU.mult).then_inc(m["x2n_rdy"], 1)
                if k:
                    v = cnt(t, uk, 1, 1)
                    wait(dve, m["route_done"], v)
                    nc.vector.tensor_tensor(logits[:], psum[0:S, 7, DC * S:DC * S + E], route_bias[:], ALU.add).then_inc(m["lg_rdy"], 1)
                    wait(dve, m["lg_rdy"], v)
                    apart(dve)
                    nc.vector.max(top8[:], logits[:]).then_inc(m["top_rdy"], 1)
                    wait(dve, m["top_rdy"], v)
                    wait(dve, m["gexp_rdy"], cnt(t, uk - 1, 1, 1))
                    nc.vector.tensor_tensor(gap[:], top8[:, 1:2], top8[:, 0:1], ALU.subtract).then_inc(m["gap_rdy"], 1)
                    apart(dve)
                    nc.vector.max_index(top8_at[:], top8[:], logits[:]).then_inc(m["at_rdy"], 1)
                if f:
                    mix(t, u, 1)
                if r and not f:
                    v = cnt(t, ur, 1, 1)
                    wait(dve, m["rs3"], v)
                    wait(dve, m["x3nT_done"], cnt(t, ur - 1, 1, 1))
                    wait(dve, scattered[ur % ROW_SLOTS], sent(t, ur - ROW_SLOTS))
                    nc.vector.tensor_scalar(rows[:, ur % ROW_SLOTS, 0:D], x3[:, ur % 2, :], ln_mv[:, 1, 0:1], ln_rstd[:, 1, :], ALU.subtract, ALU.mult).then_inc(m["x3n_rdy"], 1)
                if k:
                    v = cnt(t, uk, 1, 1)
                    wait(dve, m["at_rdy"], v)
                    nc.vector.tensor_scalar(first[:], iota[:], top8_at[:, 0:1], None, ALU.is_equal).then_inc(m["which_rdy"], 1)
                    nc.vector.tensor_scalar(second[:], iota[:], top8_at[:, 1:2], None, ALU.is_equal).then_inc(m["which_rdy"], 1)
                    wait(dve, m["which_rdy"], cnt(t, uk, 2, 2))
                    nc.vector.tensor_tensor(chosen[:], first[:], second[:], ALU.add).then_inc(m["chosen_rdy"], 1)
                if f:
                    mix(t, u, 2)
                if k:
                    v = cnt(t, uk, 1, 1)
                    wait(dve, m["gexp_rdy"], v)
                    nc.vector.tensor_scalar(gap_sum[:], gap_exp[:], 1.0, None, ALU.add).then_inc(m["pair_rdy"], 1)
                if o:
                    v = cnt(t, uo, 1, 1)
                    wait(dve, m["exp_rdy"], v)
                    nc.vector.reciprocal(inv_sum[:], prob_sum[:, uo % 2, :]).then_inc(m["inv_rdy"], 1)
                if k:
                    nc.vector.scalar_tensor_tensor(unscaled[:], second[:], gap_exp[:], first[:], ALU.mult, ALU.add).then_inc(m["pair_rdy"], 1)
                if k:
                    wait(dve, m["pair_rdy"], cnt(t, uk, 3, 1))
                    nc.vector.reciprocal(first_w[:], gap_sum[:]).then_inc(m["pair_rdy"], 1)
                if o:
                    v = cnt(t, uo, 1, 1)
                    wait(dve, m["inv_rdy"], v)
                    wait(dve, m["o_done"], v)
                    wait(dve, m["x3n_rdy"], cnt(t, uo - 2, 1, 1))
                    wait(dve, m[f"x3_out{uo % 2}"], loads(t, uo - 2))
                    nc.vector.scalar_tensor_tensor(x3[:, uo % 2, :], psum[0:S, 6, 0:D], inv_sum[:], xrow(uo), ALU.mult, ALU.add).then_inc(m["x3_rdy"], 1)
                if f:
                    mix(t, u, 3)
                if r:
                    v = cnt(t, ur, 1, 1)
                    b0 = (t * TURN + ur) * S
                    wait(dve, m["x3hi_rdy"], v)
                    nc.vector.tensor_tensor(xT_lo[:, :, bass.ds(b0, S)], psum[:, 7, 0:DC * S].rearrange("p (c s) -> p c s", c=DC),
                                            xT_hi[:, :, bass.ds(b0, S)], ALU.subtract).then_inc(m["x3lo_rdy"], 1)
                if k:
                    v = cnt(t, uk, 1, 1)
                    wait(dve, m["pair_rdy"], cnt(t, uk, 3, 3))
                    nc.vector.tensor_scalar(rows[:, uk % ROW_SLOTS, AT_W:AT_W + E], unscaled[:], first_w[:], None, ALU.mult).then_inc(m["comb_rdy"], 1)
                    wait(dve, m["rank_done"], v)
                    nc.vector.tensor_tensor(slot_of[:], psum[0:S, 3, 0:E], slot_base[:], ALU.add).then_inc(m["pos_rdy"], 1)
                    nc.vector.tensor_tensor(cum[:], cum[:], chosen[:], ALU.add).then_inc(m["cum_rdy"], 1)
                    wait(dve, m["pos_rdy"], v)
                    nc.vector.tensor_tensor(picked[:, 0, :], slot_of[:], first[:], ALU.mult).then_inc(m["pick_rdy"], 1)
                    nc.vector.tensor_tensor(picked[:, 1, :], slot_of[:], second[:], ALU.mult).then_inc(m["pick_rdy"], 1)
                    wait(dve, m["pick_rdy"], cnt(t, uk, 3, 2))
                    nc.vector.tensor_reduce(slots[:], picked[:], AX.X, ALU.add).then_inc(m["pick_rdy"], 1)
                    wait(dve, m["pick_rdy"], cnt(t, uk, 3, 3))
                    nc.vector.tensor_copy(slots_at[:, uk % ROW_SLOTS, :], slots[:]).then_inc(m["slots_rdy"], 1)

            steps(dve, step)

            table_sem = m["table"]
            run = lambda a: a.rearrange("p n e -> p (n e)")
            nc.vector.tensor_copy(base[:, 0, :], expert_row[:]).then_inc(table_sem, 1)
            nc.vector.memset(two_halves[:, 0, :], 1.0).then_inc(table_sem, 1)
            dve.wait_ge(m["late_in"], 16 * len(keep["late_loads"]))
            dve.wait_ge(m["tally_done"], 1)
            nc.vector.tensor_copy(counts[:], psum[:, 0, 0:E]).then_inc(table_sem, 1)
            dve.wait_ge(table_sem, 3)
            nc.vector.tensor_tensor(pad_at[:], counts[:], pad_place[:], ALU.add).then_inc(table_sem, 1)
            nc.vector.tensor_tensor(over, counts[0:NT, :].rearrange("p (e n) -> p e n", n=1).broadcast_to([NT, E, FULL_MAX]),
                                    edges[:].rearrange("p (o n) -> p o n", o=1).broadcast_to([NT, E, FULL_MAX]), ALU.is_ge).then_inc(table_sem, 1)
            dve.wait_ge(table_sem, 5)
            nc.vector.tensor_reduce(length[:, 0, :], over, AX.X, ALU.add).then_inc(table_sem, 1)
            dve.wait_ge(table_sem, 6)
            nc.vector.scalar_tensor_tensor(rest, length[:, 0, :], -float(TILE), counts[0:NT, :], ALU.mult, ALU.add).then_inc(table_sem, 1)
            nc.vector.scalar_tensor_tensor(base[:, 1, :], length[:, 0, :], float(TILE), expert_row[:], ALU.mult, ALU.add).then_inc(table_sem, 1)
            dve.wait_ge(table_sem, 7)
            nc.vector.tensor_scalar(length[:, 1, :], rest, 0.0, None, ALU.is_gt).then_inc(table_sem, 1)
            nc.vector.tensor_scalar(two_halves[:, 1, :], rest, 128.0, None, ALU.is_gt).then_inc(table_sem, 1)
            dve.wait_ge(table_sem, 9)
            for n in range(2):
                nc.vector.tensor_tensor(upto_length[:, n * E:(n + 1) * E, :], length[:, n, :].rearrange("p (o e) -> p o e", o=1).broadcast_to([NT, E, E]),
                                        upto[:], ALU.mult).then_inc(table_sem, 1)
            dve.wait_ge(table_sem, 12)
            nc.vector.tensor_reduce(run(ends), upto_length, AX.X, ALU.add).then_inc(table_sem, 1)
            dve.wait_ge(table_sem, 13)
            nc.vector.tensor_scalar(ends[:, 1, :], ends[:, 1, :], ends[:, 0, E - 1:E], None, ALU.add).then_inc(table_sem, 1)
            dve.wait_ge(table_sem, 14)
            nc.vector.tensor_tensor(starts, ends, length, ALU.subtract).then_inc(table_sem, 1)
            dve.wait_ge(table_sem, 15)
            nc.vector.tensor_scalar(run(later), run(starts), tile_no[:], None, ALU.is_gt).then_inc(table_sem, 1)
            nc.vector.scalar_tensor_tensor(run(base), run(starts), -float(TILE), run(base), ALU.mult, ALU.add).then_inc(table_sem, 1)
            dve.wait_ge(table_sem, 16)
            nc.vector.scalar_tensor_tensor(run(own), run(ends), tile_no[:], run(later), ALU.is_gt, ALU.subtract).then_inc(table_sem, 1)
            dve.wait_ge(table_sem, 18)
            nc.vector.scalar_tensor_tensor(parts[:, 1, :], run(base), tile_shift[:], run(own), ALU.add, ALU.mult).then_inc(table_sem, 1)
            for n in range(2):
                nc.vector.tensor_tensor(parts[:, 0, n * E:(n + 1) * E], own[:, n, :], iota[0:NT, :], ALU.mult).then_inc(table_sem, 1)
            dve.wait_ge(table_sem, 19)
            nc.vector.tensor_tensor(parts[:, 2, :], parts[:, 1, :], run(two_halves), ALU.mult).then_inc(table_sem, 1)
            dve.wait_ge(table_sem, 22)
            nc.vector.tensor_reduce(tile, parts, AX.X, ALU.add).then_inc(table_sem, 1)
            dve.wait_ge(table_sem, 23)
            for n in range(2):
                nc.vector.tensor_scalar(tile[:, n + 1:n + 2], tile[:, n + 1:n + 2], float(DUMMY + n * 128), None, ALU.add).then_inc(table_sem, 1)
            dve.wait_ge(m["tally_done"], 2)
            nc.vector.tensor_copy(table[:].rearrange("o n u -> o (n u)"), psum[0:1, 1, 0:3 * NT]).then_inc(table_sem, 1)
            dve.wait_ge(table_sem, TABLE_OPS + 1)


def expert_phase(nc, ctx, dram, keep):
    def sb(name, shape, dt):
        return ctx.enter_context(nc.sbuf_tensor(name, shape, dt))

    def sem(name):
        return ctx.enter_context(nc.semaphore(name))

    ident, psum, cum = keep["ident"], keep["psum"], keep["cum"]
    w1_cols = E * DC * HID
    w1_hi, w1_lo = (w[:, 0:w1_cols].rearrange("p (e c h) -> p e c h", e=E, c=DC) for w in (keep["w_hi"], keep["w_lo"]))
    w2_hi, w2_lo = (w[:, w1_cols:W_COLS].rearrange("p (e c d) -> p e c d", e=E, c=HC) for w in (keep["w_hi"], keep["w_lo"]))
    HALF = TILE // 128

    b1, b2, pad_at, pad_rows, table = (keep[k] for k in ("b1", "b2", "pad_at", "pad_rows", "table"))
    rows = sb("rows_e", [128, 2, HALF, ROW], F32)
    meta = sb("meta", [128, 2, HALF, E + 1], F32)
    weight = sb("weight", [128, 2, HALF], F32)
    token_at = sb("token_at", [128, 2, HALF], U32)
    x_hi = sb("x_hi", [128, 2, DC, TILE], F16)
    x_lo = sb("x_lo", [128, 2, DC, TILE], F16)
    h = sb("h", [128, HC, TILE], F32)
    h_hi = sb("h_hi", [128, 2, HC, TILE], F16)
    h_lo = sb("h_lo", [128, 2, HC, TILE], F16)
    y_sum = sb("y_sum", [128, HALF, D], F32)
    y = sb("y", [128, 2, HALF, D], F32)

    names = """pads_sent passed
        rows_in0 rows_in1 xT_done xhi_rdy xlo_rdy up_done h_rdy hhi_rdy hlo_rdy down_done y_sum_rdy y_rdy meta_rdy weight_rdy token_rdy
        added""".split()
    m = {n: sem("x_" + n) for n in names}
    rows_in = [m["rows_in0"], m["rows_in1"]]

    def cnt(t, u, per, extra):
        return t * (2 * per) + (u * per + extra)

    def apart(engine):
        engine.sem_inc(m["passed"], 1)

    def look_up(engine, what, t, u, most):
        return engine.value_load(table[0:1, what, bass.ds(t * 2 + u, 1)], min_val=0, max_val=most)

    def steps(engine, step):
        for t in range(2):
            for u in range(2):
                step(t, u, True, t + u > 0)
        turns = (NT - LAST_TILES) // 2
        with engine.Fori(2, turns) as t:
            for u in range(2):
                step(t, u, True, True)
        for n in range(turns * 2, (turns + 1) * 2):
            step(n // 2, n % 2, True, True)
        with engine.Fori(turns + 1, NT // 2) as t:
            for u in range(2):
                step(t, u, True, True)
        for n in range(NT // 2 * 2, NT + 1):
            step(n // 2, n % 2, n < NT, True)

    with nc.Block() as block:

        @block.sync
        def _(sp):
            def step(t, u, up, down):
                if not up:
                    return
                row = [look_up(sp, 1 + n, t, u, DISPATCH_ROWS - 128) for n in range(HALF)]
                wait(sp, m["xT_done"], cnt(t, u - 2, 1, 1))
                apart(sp)
                wait(sp, m["meta_rdy"], cnt(t, u - 2, 1, 1))
                apart(sp)
                if isinstance(t, int) and 2 * t + u == NT - LAST_TILES:
                    sp.wait_ge(m["pads_sent"], 16 * E)
                for n in range(HALF):
                    sp.dma_start(rows[:, u, n, :], dram["dispatch"][bass.ds(row[n], 128), :]).then_inc(rows_in[u], 16)

            steps(sp, step)

        @block.gpsimd
        def _(pool):
            for e in range(E):
                nc.gpsimd.indirect_dma_start(dram["dispatch"], bass.IndirectOffsetOnAxis(pad_at[:, e:e + 1], 0),
                                             pad_rows[:], None).then_inc(m["pads_sent"], 16)

            def step(t, u, up, down):
                if not down:
                    return
                p = (u - 1) % 2
                wait(pool, m["y_rdy"], cnt(t, u - 1, HALF, HALF))
                wait(pool, m["added"], cnt(t, u - 2, 16 * HALF, 16 * HALF))
                apart(pool)
                for n in range(HALF):
                    nc.gpsimd.indirect_dma_start(dram["out"], bass.IndirectOffsetOnAxis(token_at[:, p, n:n + 1], 0), y[:, p, n, :], None,
                                                 compute_op=ALU.add).then_inc(m["added"], 16)

            steps(pool, step)
            pool.wait_ge(m["added"], 16 * HALF * NT)

        @block.tensor
        def _(pe):
            def turn_rows(t, u):
                p = u % 2
                wait(pe, rows_in[p], t * (16 * HALF) + 16 * HALF * (u // 2 + 1))
                wait(pe, m["xlo_rdy"], cnt(t, u - 1, 1, 1))
                for kc in range(DC):
                    for n in range(HALF):
                        last = nc.tensor.transpose(psum[:, 0, kc * TILE + n * 128:kc * TILE + (n + 1) * 128],
                                                   rows[:, p, n, kc * 128:(kc + 1) * 128], ident[:, :])
                last.then_inc(m["xT_done"], 1)

            turn_rows(0, 0)

            def step(t, u, up, down):
                p, q = u % 2, (u - 1) % 2
                more = up and not (isinstance(t, int) and 2 * t + u == NT - 1)
                if up:
                    e = look_up(pe, 0, t, u, E - 1)
                    wait(pe, m["xlo_rdy"], cnt(t, u, 1, 1))
                    for c in range(HC):
                        if c % 2 == 0:
                            wait(pe, m["h_rdy"], cnt(t, u - 1, HC, c + 2))
                            apart(pe)
                        n = 0
                        for w, x in ((w1_hi, x_hi), (w1_hi, x_lo), (w1_lo, x_hi)):
                            for kc in range(DC):
                                last = nc.tensor.matmul(psum[:, 1 + c // 2, (c % 2) * TILE:(c % 2 + 1) * TILE],
                                                        w[:, bass.ds(e, 1), kc, c * 128:(c + 1) * 128].rearrange("p o h -> p (o h)"),
                                                        x[:, p, kc, :], start=(n == 0), stop=(n == 5))
                                n += 1
                        if c % 2 == 1:
                            last.then_inc(m["up_done"], 1)
                if more:
                    turn_rows(t, u + 1)
                if down:
                    e = look_up(pe, 0, t, u - 1, E - 1)
                    wait(pe, m["hlo_rdy"], cnt(t, u - 1, 2, 2))
                    for s in range(HALF):
                        wait(pe, m["y_sum_rdy"], cnt(t, u - 2, HALF, s + 1))
                        n = 0
                        for hh, w in ((h_hi, w2_hi), (h_hi, w2_lo), (h_lo, w2_hi)):
                            for kc in range(HC):
                                last = nc.tensor.matmul(psum[:, 3 + s, 0:D], hh[:, q, kc, s * 128:(s + 1) * 128],
                                                        w[:, bass.ds(e, 1), kc, :].rearrange("p o d -> p (o d)"), start=(n == 0), stop=(n == 11))
                                n += 1
                        last.then_inc(m["down_done"], 1)

            steps(pe, step)

        @block.scalar
        def _(act):
            def high_x(t, u):
                p = u % 2
                wait(act, m["xT_done"], cnt(t, u, 1, 1))
                wait(act, m["up_done"], cnt(t, u - 2, 2, 2))
                nc.scalar.activation(x_hi[:, p, :, :].rearrange("p c s -> p (c s)"), psum[:, 0, 0:DC * TILE], ACT.Copy).then_inc(m["xhi_rdy"], 1)

            high_x(0, 0)

            def step(t, u, up, down):
                if not up:
                    return
                p = u % 2
                more = not (isinstance(t, int) and 2 * t + u == NT - 1)
                e = look_up(act, 0, t, u, E - 1)
                for c in range(HC):
                    if c % 2 == 0:
                        wait(act, m["up_done"], cnt(t, u, 2, c // 2 + 1))
                        wait(act, m["hlo_rdy"], cnt(t, u - 1, 2, c // 2 + 1))
                        apart(act)
                    nc.scalar.activation(h[:, c, :], psum[:, 1 + c // 2, (c % 2) * TILE:(c % 2 + 1) * TILE], ACT.Relu,
                                         bias=b1[:, c, bass.ds(e, 1)]).then_inc(m["h_rdy"], 1)
                if more:
                    high_x(t, u + 1)
                wait(act, m["down_done"], cnt(t, u - 2, HALF, HALF))
                for k in range(2):
                    wait(act, m["h_rdy"], cnt(t, u, HC, 2 * k + 2))
                    nc.scalar.activation(h_hi[:, p, 2 * k:2 * k + 2, :], h[:, 2 * k:2 * k + 2, :], ACT.Copy).then_inc(m["hhi_rdy"], 1)

            steps(act, step)

        @block.vector
        def _(dve):
            def low_x(t, u):
                p = u % 2
                wait(dve, m["xhi_rdy"], cnt(t, u, 1, 1))
                nc.vector.tensor_tensor(x_lo[:, p, :, :].rearrange("p c s -> p (c s)"), psum[:, 0, 0:DC * TILE],
                                        x_hi[:, p, :, :].rearrange("p c s -> p (c s)"), ALU.subtract).then_inc(m["xlo_rdy"], 1)

            low_x(0, 0)

            def step(t, u, up, down):
                p, q = u % 2, (u - 1) % 2
                more = up and not (isinstance(t, int) and 2 * t + u == NT - 1)
                if up:
                    wait(dve, rows_in[p], t * (16 * HALF) + 16 * HALF)
                    nc.vector.tensor_copy(meta[:, p, :, :], rows[:, p, :, AT_W:AT_TOKEN + 1]).then_inc(m["meta_rdy"], 1)
                if more:
                    low_x(t, u + 1)
                if up:
                    for k in range(2):
                        wait(dve, m["hhi_rdy"], cnt(t, u, 2, k + 1))
                        nc.vector.tensor_tensor(h_lo[:, p, 2 * k:2 * k + 2, :], h[:, 2 * k:2 * k + 2, :], h_hi[:, p, 2 * k:2 * k + 2, :],
                                                ALU.subtract).then_inc(m["hlo_rdy"], 1)
                if down:
                    e = look_up(dve, 0, t, u - 1, E - 1)
                    for n in range(HALF):
                        wait(dve, m["down_done"], cnt(t, u - 1, HALF, n + 1))
                        nc.vector.tensor_tensor(y_sum[:, n, :], psum[:, 3 + n, 0:D], b2[:, bass.ds(e, 1), :].rearrange("p o d -> p (o d)"),
                                                ALU.add).then_inc(m["y_sum_rdy"], 1)
                        wait(dve, m["y_sum_rdy"], cnt(t, u - 1, HALF, n + 1))
                        wait(dve, m["weight_rdy"], cnt(t, u - 1, 1, 1))
                        wait(dve, m["added"], cnt(t, u - 3, 16 * HALF, 16 * HALF))
                        nc.vector.tensor_scalar(y[:, q, n, :], y_sum[:, n, :], weight[:, q, n:n + 1], None, ALU.mult).then_inc(m["y_rdy"], 1)
                if up:
                    e = look_up(dve, 0, t, u, E - 1)
                    wait(dve, m["meta_rdy"], cnt(t, u, 1, 1))
                    nc.vector.tensor_copy(weight[:, p, :].rearrange("p (n o) -> p n o", o=1), meta[:, p, :, bass.ds(e, 1)]).then_inc(m["weight_rdy"], 1)
                    wait(dve, m["added"], cnt(t, u - 2, 16 * HALF, 16 * HALF))
                    nc.vector.tensor_copy(token_at[:, p, :].rearrange("p (n o) -> p n o", o=1), meta[:, p, :, E:E + 1]).then_inc(m["token_rdy"], 1)

            steps(dve, step)


def build(nc, dram):
    with ExitStack() as ctx:
        def sb(name, shape, dt):
            return ctx.enter_context(nc.sbuf_tensor(name, shape, dt))

        keep = {
            "x_res": sb("x_res", [S, B, D], F32),
            "xT_hi": sb("xT_hi", [128, DC, B * S], F16),
            "xT_lo": sb("xT_lo", [128, DC, B * S], F16),
            "gate_counts": sb("gate_counts", [S, E], F32),
            "cum": sb("cum", [S, E], F32),
            "ident": sb("ident", [128, 128], F32),
            "iota": sb("iota", [S, E], F32),
            "psum": ctx.enter_context(nc.psum_tensor("psum", [128, 8, 512], F32)),
        }
        with ExitStack() as scope:
            attention_phase(nc, scope, dram, keep)
        keep["w_hi"] = sb("w_hi", [128, W_COLS], F16)
        keep["w_lo"] = sb("w_lo", [128, W_COLS], F16)
        last = {"b1": [128, HC, E], "b2": [128, E, D], "pad_place": [128, E], "pad_rows": [128, ROW],
                "edges": [NT, TOKENS // TILE], "upto": [NT, E, E], "tile_no": [NT, 1], "tile_shift": [NT, 1], "expert_row": [NT, E]}
        for name, shape in last.items():
            keep[name] = sb(name, shape, F32)
        keep["late_loads"] = [
            (keep["b1"][:], dram["b1T"].rearrange("(c p) e -> p c e", p=128)),
            (keep["b2"][:], dram["b2"].rearrange("(o e) d -> o e d", o=1).broadcast_to([128, E, D])),
            (keep["pad_place"][:], dram["pad_place"]),
            (keep["pad_rows"][:], dram["pads"][2]),
            *((keep[name][:], dram[name]) for name in ("edges", "upto", "tile_no", "tile_shift")),
            (keep["expert_row"][:], dram["slot_base"][0:NT, :]),
        ]
        keep["table"] = sb("table", [1, 3, NT], U32)
        keep["pad_at"] = sb("pad_at", [128, E], U32)
        keep["ones"] = sb("ones", [S, 128], F32)
        for phase in (middle_phase, expert_phase):
            with ExitStack() as scope:
                phase(nc, scope, dram, keep)


def kernel(**inputs):
    import concourse.bacc as bacc
    from concourse.bass_utils import run_bass_kernel_spmd

    a = {name: np.asarray(value) for name, value in inputs.items()}
    w_kv = a["L0_xattn_w_kv"]
    w1 = a["L1_ffn_W1"].reshape(E, HID, DC, 128).transpose(3, 0, 2, 1)
    w2 = a["L1_ffn_W2"].reshape(E, D, HC, 128).transpose(3, 0, 2, 1)
    pads = np.zeros((3, 128, ROW), np.float32)
    pads[:, :, AT_TOKEN] = PAD_OUT + np.arange(3 * 128).reshape(3, 128)
    host = {
        "x": a["x"],
        "ctx": a["ctx_1024"],
        "ctxT": a["ctx_1024"].transpose(0, 2, 1),
        "mask": a["mask_Bx1xS2_fk0"],
        "wqT": a["L0_xattn_w_q"].T,
        "wkT": w_kv[:D].T,
        "wvT": w_kv[D:].T,
        "woT": a["L0_xattn_w_out"].T,
        "bo": a["L0_xattn_b_out"],
        "gate_wT": a["L0_ffn_gate_w"].T,
        "gate_b": a["L0_ffn_gate_b"],
        "weT": a["L0_ffn_expert_w"].transpose(2, 0, 1),
        "expert_bT": a["L0_ffn_expert_b"].T,
        "w12": np.concatenate([w1.reshape(128, -1), w2.reshape(128, -1)], axis=1),
        "b1T": a["L1_ffn_b1"].T,
        "b2": a["L1_ffn_b2"],
        "route_wT": a["L1_ffn_Wg"].T,
        "route_b": a["L1_ffn_bg"],
        "ident": np.eye(128, dtype=np.float32),
        "iota": np.broadcast_to(np.arange(E, dtype=np.float32), (S, E)),
        "parity": ((np.arange(128)[:, None] // HD) % 2 == np.arange(2)).astype(np.float32),
        "before": np.triu(np.ones((S, S), np.float32), 1),
        "slot_base": np.broadcast_to(np.arange(E, dtype=np.float32) * CAP, (S, E)),
        "place": np.arange(S, dtype=np.float32)[:, None],
        "pads": pads,
        "pad_place": (np.arange(128)[:, None] + np.arange(E) * CAP).astype(np.float32),
        "edges": np.broadcast_to(np.arange(1, TOKENS // TILE + 1, dtype=np.float32) * TILE, (NT, TOKENS // TILE)),
        "upto": np.broadcast_to(np.tril(np.ones((E, E), np.float32)), (NT, E, E)),
        "tile_no": np.arange(NT, dtype=np.float32)[:, None],
        "tile_shift": np.arange(NT, dtype=np.float32)[:, None] * TILE - DUMMY,
    }
    nc = bacc.Bacc("TRN2", target_bir_lowering=False, num_devices=1)
    arrays, dram = {}, {}
    for name, value in host.items():
        arrays[f"in_{name}_dram"] = np.ascontiguousarray(value)
        dram[name] = nc.dram_tensor(f"in_{name}_dram", value.shape, mybir.dt.from_np(value.dtype), kind="ExternalInput").ap()
    dram["out"] = nc.dram_tensor("out_0_dram", (OUT_ROWS, D), F32, kind="ExternalOutput").ap()
    dram["dispatch"] = nc.dram_tensor("dispatch_dram", (DISPATCH_ROWS, ROW), F32, kind="Internal").ap()
    build(nc, dram)
    result = run_bass_kernel_spmd(nc, [arrays], core_ids=[0])
    return result.results[0]["out_0_dram"][:TOKENS].reshape(B, S, D)
```
